# Optimizing a Trainium2 kernel written in Bass

```python
import numpy as np
import jax
import jax.numpy as jnp

def _softmax(x, axis=-1):
    return jax.nn.softmax(x, axis=axis)

def _gelu(x):
    return jax.nn.gelu(x, approximate=True)

def _silu(x):
    return jax.nn.silu(x)

def _sigmoid(x):
    return jax.nn.sigmoid(x)

def _layernorm(x, axis=-1, eps=1e-05):
    m = jnp.mean(x, axis=axis, keepdims=True)
    v = jnp.var(x, axis=axis, keepdims=True)
    return (x - m) / jnp.sqrt(v + eps)

def _scatter_add(tgt, idx, src, axis=0):
    return tgt.at[idx].add(src)

def _segment_sum(src, seg, n):
    return jax.ops.segment_sum(src, seg, n)
kernel_name = 'mk_conv_seq_d2_conv_nchw64_r4_cb755f'

def setup_inputs(seed: int=0):
    np.random.seed(seed)
    _w = jnp.asarray

    def _rec_inputs():
        import jax
        import jax.numpy as jnp
        _gk = jax.random.key(seed)
        x = -0.0002091 + 1 * jax.random.normal(jax.random.fold_in(_gk, 1), (32, 16, 56, 56), jnp.float32)
        return x
    x = _rec_inputs()

    def _L0_conv_setup():
        import jax, jax.numpy as jnp
        import numpy as np
        T = 10
        EPS = 1e-05
        key = jax.random.key(seed)
        k1, k2 = jax.random.split(key)
        B, C, H, W = (32, 16, 56, 56)
        X = jax.random.normal(k1, (B, C, H, W), dtype=jnp.float32)
        beta = jnp.zeros((C,), dtype=jnp.float32)
        return {'X': X, 'beta': beta}
    _L0_conv_all = _L0_conv_setup()
    _L0_conv_in = {k: v for k, v in _L0_conv_all.items() if k in ('beta',)}
    del _L0_conv_all

    def _L1_conv_setup():
        import jax, jax.numpy as jnp
        import numpy as np
        KK = 9
        BN_EPS = 1e-05

        def _dcn_bn_act_res(x, w_off, b_off, w, b, gamma, beta):
            B, C, H, W = x.shape
            O = w.shape[0]
            om = jax.lax.conv_general_dilated(x, w_off, window_strides=(1, 1), padding=[(1, 1), (1, 1)], dimension_numbers=('NCHW', 'OIHW', 'NCHW')) + b_off[None, :, None, None]
            off_y = om[:, :KK]
            off_x = om[:, KK:2 * KK]
            mask = jax.nn.sigmoid(om[:, 2 * KK:])
            ky, kx = jnp.meshgrid(jnp.arange(3), jnp.arange(3), indexing='ij')
            ky = ky.reshape(KK).astype(jnp.float32) - 1.0
            kx = kx.reshape(KK).astype(jnp.float32) - 1.0
            hs = jnp.arange(H, dtype=jnp.float32)
            ws = jnp.arange(W, dtype=jnp.float32)
            py = off_y + hs[None, None, :, None] + ky[None, :, None, None]
            px = off_x + ws[None, None, None, :] + kx[None, :, None, None]
            y0 = jnp.floor(py)
            x0 = jnp.floor(px)
            wy = py - y0
            wx = px - x0
            y0i = y0.astype(jnp.int32)
            x0i = x0.astype(jnp.int32)

            def gather(img, yi, xi):
                valid = (yi >= 0) & (yi < H) & (xi >= 0) & (xi < W)
                yc = jnp.clip(yi, 0, H - 1)
                xc = jnp.clip(xi, 0, W - 1)
                return img[:, yc, xc] * valid[None].astype(img.dtype)

            def sample_one(img, yi, xi, wy_, wx_):
                v00 = gather(img, yi, xi)
                v01 = gather(img, yi, xi + 1)
                v10 = gather(img, yi + 1, xi)
                v11 = gather(img, yi + 1, xi + 1)
                w00 = ((1 - wy_) * (1 - wx_))[None]
                w01 = ((1 - wy_) * wx_)[None]
                w10 = (wy_ * (1 - wx_))[None]
                w11 = (wy_ * wx_)[None]
                return v00 * w00 + v01 * w01 + v10 * w10 + v11 * w11
            sampled = jax.vmap(sample_one)(x, y0i, x0i, wy, wx)
            sampled = sampled * mask[:, None]
            out = jnp.einsum('bckhw,ock->bohw', sampled, w.reshape(O, C, KK))
            out = out + b[None, :, None, None]
            mu = out.mean(axis=(0, 2, 3), keepdims=True)
            var = out.var(axis=(0, 2, 3), keepdims=True)
            out = (out - mu) * jax.lax.rsqrt(var + BN_EPS)
            out = out * gamma[None, :, None, None] + beta[None, :, None, None]
            return jax.nn.relu(out) + x
        key = jax.random.key(seed)
        ks = jax.random.split(key, 8)
        B, C, H, W = (2, 16, 64, 64)
        O = 16
        x = jax.random.normal(ks[0], (B, C, H, W), dtype=jnp.float32)
        w_off = jax.random.normal(ks[1], (3 * KK, C, 3, 3), dtype=jnp.float32) * 0.05
        b_off = jnp.zeros((3 * KK,), dtype=jnp.float32)
        w = jax.random.normal(ks[2], (O, C, 3, 3), dtype=jnp.float32) * (1.0 / np.sqrt(C * KK))
        b = jnp.zeros((O,), dtype=jnp.float32)
        gamma = jnp.ones((O,), dtype=jnp.float32)
        beta = jnp.zeros((O,), dtype=jnp.float32)
        return {'x': x, 'w_off': w_off, 'b_off': b_off, 'w': w, 'b': b, 'gamma': gamma, 'beta': beta}
    _L1_conv_all = _L1_conv_setup()
    _L1_conv_in = {k: v for k, v in _L1_conv_all.items() if k in ('w_off', 'b_off', 'w', 'b', 'gamma', 'beta')}
    del _L1_conv_all
    return {'x': x, 'L0_conv_beta': _L0_conv_in['beta'], 'L1_conv_w_off': _L1_conv_in['w_off'], 'L1_conv_b_off': _L1_conv_in['b_off'], 'L1_conv_w': _L1_conv_in['w'], 'L1_conv_b': _L1_conv_in['b'], 'L1_conv_gamma': _L1_conv_in['gamma'], 'L1_conv_beta': _L1_conv_in['beta']}

def reference(x, L0_conv_beta, L1_conv_w_off, L1_conv_b_off, L1_conv_w, L1_conv_b, L1_conv_gamma, L1_conv_beta):
    import jax
    import jax.numpy as jnp

    def _L0_conv_ref(X, beta):
        import jax, jax.numpy as jnp
        import numpy as np
        T = 10
        EPS = 1e-05
        B, C, H, W = X.shape
        d = C
        m = B * H * W
        x = jnp.transpose(X, (1, 0, 2, 3)).reshape(d, m)
        mean = jnp.mean(x, axis=1, keepdims=True)
        xc = x - mean
        I = jnp.eye(d, dtype=X.dtype)
        Sigma = EPS * I + xc @ xc.T / m
        fix = 0.9 + 0.1 * I
        Sigma = Sigma * fix
        rTr = 1.0 / jnp.trace(Sigma)
        Sigma_N = Sigma * rTr
        P = I
        for _ in range(T):
            P = 1.5 * P - 0.5 * (P @ P @ P @ Sigma_N)
        wm = P * jnp.sqrt(rTr)
        xn = wm @ xc
        X_hat = jnp.transpose(xn.reshape(C, B, H, W), (1, 0, 2, 3))
        X_hat = X_hat + beta.reshape(1, C, 1, 1)
        return X_hat

    def _L1_conv_ref(x, w_off, b_off, w, b, gamma, beta):
        import jax, jax.numpy as jnp
        import numpy as np
        KK = 9
        BN_EPS = 1e-05

        def _dcn_bn_act_res(x, w_off, b_off, w, b, gamma, beta):
            B, C, H, W = x.shape
            O = w.shape[0]
            om = jax.lax.conv_general_dilated(x, w_off, window_strides=(1, 1), padding=[(1, 1), (1, 1)], dimension_numbers=('NCHW', 'OIHW', 'NCHW')) + b_off[None, :, None, None]
            off_y = om[:, :KK]
            off_x = om[:, KK:2 * KK]
            mask = jax.nn.sigmoid(om[:, 2 * KK:])
            ky, kx = jnp.meshgrid(jnp.arange(3), jnp.arange(3), indexing='ij')
            ky = ky.reshape(KK).astype(jnp.float32) - 1.0
            kx = kx.reshape(KK).astype(jnp.float32) - 1.0
            hs = jnp.arange(H, dtype=jnp.float32)
            ws = jnp.arange(W, dtype=jnp.float32)
            py = off_y + hs[None, None, :, None] + ky[None, :, None, None]
            px = off_x + ws[None, None, None, :] + kx[None, :, None, None]
            y0 = jnp.floor(py)
            x0 = jnp.floor(px)
            wy = py - y0
            wx = px - x0
            y0i = y0.astype(jnp.int32)
            x0i = x0.astype(jnp.int32)

            def gather(img, yi, xi):
                valid = (yi >= 0) & (yi < H) & (xi >= 0) & (xi < W)
                yc = jnp.clip(yi, 0, H - 1)
                xc = jnp.clip(xi, 0, W - 1)
                return img[:, yc, xc] * valid[None].astype(img.dtype)

            def sample_one(img, yi, xi, wy_, wx_):
                v00 = gather(img, yi, xi)
                v01 = gather(img, yi, xi + 1)
                v10 = gather(img, yi + 1, xi)
                v11 = gather(img, yi + 1, xi + 1)
                w00 = ((1 - wy_) * (1 - wx_))[None]
                w01 = ((1 - wy_) * wx_)[None]
                w10 = (wy_ * (1 - wx_))[None]
                w11 = (wy_ * wx_)[None]
                return v00 * w00 + v01 * w01 + v10 * w10 + v11 * w11
            sampled = jax.vmap(sample_one)(x, y0i, x0i, wy, wx)
            sampled = sampled * mask[:, None]
            out = jnp.einsum('bckhw,ock->bohw', sampled, w.reshape(O, C, KK))
            out = out + b[None, :, None, None]
            mu = out.mean(axis=(0, 2, 3), keepdims=True)
            var = out.var(axis=(0, 2, 3), keepdims=True)
            out = (out - mu) * jax.lax.rsqrt(var + BN_EPS)
            out = out * gamma[None, :, None, None] + beta[None, :, None, None]
            return jax.nn.relu(out) + x
        return _dcn_bn_act_res(x, w_off, b_off, w, b, gamma, beta)

    def _gn(v, G=32, eps=1e-05):
        B_, C_, H_, W_ = v.shape
        g = v.reshape(B_, G, C_ // G, H_, W_)
        m = jnp.mean(g, axis=(2, 3, 4), keepdims=True)
        s = jnp.var(g, axis=(2, 3, 4), keepdims=True)
        return ((g - m) / jnp.sqrt(s + eps)).reshape(v.shape)

    def _ln_c(v, eps=1e-06):
        m = jnp.mean(v, axis=1, keepdims=True)
        s = jnp.var(v, axis=1, keepdims=True)
        return (v - m) / jnp.sqrt(s + eps)

    def _ln_t(v, eps=1e-05):
        m = jnp.mean(v, axis=-1, keepdims=True)
        s = jnp.var(v, axis=-1, keepdims=True)
        return (v - m) / jnp.sqrt(s + eps)

    def _to_tokens(v):
        B_, C_, H_, W_ = v.shape
        return v.reshape(B_, C_, H_ * W_).transpose(0, 2, 1)

    def _from_tokens(t, like):
        B_, C_, H_, W_ = like.shape
        return t.transpose(0, 2, 1).reshape(B_, C_, H_, W_)
    x = _L0_conv_ref(x, L0_conv_beta)
    x = _L1_conv_ref(x, L1_conv_w_off, L1_conv_b_off, L1_conv_w, L1_conv_b, L1_conv_gamma, L1_conv_beta)
    return x

_drawn_inputs = setup_inputs


def setup_inputs(seed=0):
    import zlib

    import numpy as np

    out = dict(_drawn_inputs(seed))
    spreads = {'L0_conv_beta': (0.0, 0.1),
     'L1_conv_b_off': (0.0, 0.1),
     'L1_conv_b': (0.0, 0.1),
     'L1_conv_gamma': (1.0, 0.2),
     'L1_conv_beta': (0.0, 0.1)}
    factors = {}
    for name, (base, spread) in spreads.items():
        noise = np.random.default_rng([zlib.crc32(name.encode()), seed]).standard_normal(out[name].shape)
        drawn = base * np.exp(spread * noise) if base else spread * noise
        out[name] = jnp.asarray(drawn.astype(out[name].dtype))
    for name, factor in factors.items():
        out[name] = (out[name] * factor).astype(out[name].dtype)
    return out
```

```python
import concourse.bass as bass
from concourse import mybir
from contextlib import ExitStack

B, C, H, W = 32, 16, 56, 56
O = 16
KK = 9
HW = H * W
M_ALL = B * HW
GROUPS = 4
GB = B // GROUPS
PADW = W + 2
PADHW = (H + 2) * PADW
PAIRS = B // 2
UNIT_ROWS = 4
UNITS = H // UNIT_ROWS
N_UNITS = PAIRS * UNITS
UPX = UNIT_ROWS * W
WIN = 8
N_WIN = 15
BASE_WIN = 7
STAGE_ROWS = UNIT_ROWS + 2 + WIN - 1
TOP = 64
NEAR = 2 * WIN
XT_ROWS = TOP + H + TOP
XT_ROW = XT_ROWS * C
PLANE = B * KK * HW
DENSE = PLANE // 128
DCH = 392
D_RING = 3
D_IT = DENSE // DCH // D_RING
NT = 10
KINDS = 6
TAPS_PX = KK * W


KIND = {}


KIND = {}


KIND = {}


KIND = {}


KIND = {}


KIND = {}


KIND = {}


KIND = {}


KIND = {}


KIND = {}


def program(nc, dr):
    fp32, f32r, i32 = mybir.dt.float32, mybir.dt.float32r, mybir.dt.int32
    ALU, ACT, AX = mybir.AluOpType, mybir.ActivationFunctionType, mybir.AxisListType

    def dram(name, offset, dims):
        return bass.AP(tensor=dr[name].tensor, offset=offset, ap=dims)

    def sub(tile, part, parts, offset, dims):
        pitch = tile[:].ap[0][0]
        return bass.AP(tensor=tile[:].tensor, offset=part * pitch + offset, ap=[[pitch, parts]] + dims)

    def peel(eng, count, body):
        body(0, False)
        with eng.Fori(1, count - 1) as it:
            body(it, False)
        body(count - 1, True)

    def wait(eng, sem, value):
        if not (isinstance(value, int) and value <= 0):
            eng.wait_ge(sem, value)

    outer = ExitStack()
    with outer:
        def tools(stack):
            def sb(name, cols, dt=fp32, parts=128):
                return stack.enter_context(nc.sbuf_tensor(name, [parts, cols], dt))

            def ps(name, banks=1):
                return stack.enter_context(nc.psum_tensor(name, [128, 512 * banks], fp32))

            def sem(name):
                return stack.enter_context(nc.semaphore(name))
            return sb, ps, sem

        sb, ps, sem = tools(outer)
        X = sb("X", GROUPS * HW)
        XH = sb("XH", GROUPS * PADHW)
        ident = sb("ident", 128)
        same_image = sb("same_image", 128)
        same_channel = sb("same_channel", 128)
        vecs = sb("vecs", 4)
        wm = sb("wm", 128)
        zeros = sb("zeros", XT_ROWS * C)

        with ExitStack() as st:
            sb, ps, sem = tools(st)
            CH = 448
            IT = GROUPS * HW // CH // 2
            eps_eye = sb("eps_eye", 128)
            shrink = sb("shrink", 128)
            xs4 = sb("xs4", GROUPS)
            small = sb("small", 8)
            flat = [sb(f"flat{i}", CH) for i in range(2)]
            pix = [sb(f"pix{i}", 512, parts=112) for i in range(2)]
            S1, S2, SN, Pm, P15, PP, PS = [sb(n, 128) for n in ("S1", "S2", "SN", "Pm", "P15", "PP", "PS")]
            sig = sb("sig", C)
            ps_pix = [ps(f"ps_pix{i}") for i in range(2)]
            ps_gram = ps("ps_gram")
            ps_a, ps_b, ps_c = ps("ps_a"), ps("ps_b"), ps("ps_c")
            consts_loaded = sem("consts_loaded")
            x_loaded = [sem(f"x_loaded{g}") for g in range(GROUPS)]
            dve_step, pe_step, act_step = sem("dve_step"), sem("pe_step"), sem("act_step")
            centred, staged, transposed, evacuated, grammed = [
                sem(n) for n in ("centred", "staged", "transposed", "evacuated", "grammed")]
            new_p, products, pp_ready, act_ready = [sem(n) for n in ("new_p", "products", "pp_ready", "act_ready")]
            zeroed = sem("zeroed")
            LOADS = ((ident, "ident"), (same_image, "same_image"), (same_channel, "same_channel"), (vecs, "vecs"),
                     (eps_eye, "eps_eye"), (shrink, "shrink"))
            block = st.enter_context(nc.Block())

            @block.sync
            def _(sp):
                for g in range(GROUPS):
                    sp.dma_start(X[:, g * HW:(g + 1) * HW],
                                 dram("x", g * 128 * HW, [[HW, 128], [1, HW]])).then_inc(x_loaded[g], 16)

            @block.gpsimd
            def _(pool):
                pool.memset(XH[:, :], 0.0).then_inc(zeroed, 1)
                pool.memset(zeros[:, :], 0.0).then_inc(zeroed, 1)
                pool.wait_ge(zeroed, 2)

            @block.scalar
            def _(act):
                for tile, name in LOADS:
                    n = tile[:].shape[1]
                    act.dma_start(tile[:, :], dram(name, 0, [[n, 128], [1, n]])).then_inc(consts_loaded, 16)
                act.wait_ge(centred, GROUPS)

                def stage(it, last):
                    for b in range(2):
                        c = 2 * it + b
                        wait(act, transposed, c - 1)
                        nc.scalar.copy(flat[b][:, :], sub(X, 0, 128, c * CH, [[1, CH]])).then_inc(staged, 1)
                peel(act, IT, stage)
                act.wait_ge(dve_step, 11)
                nc.scalar.activation(small[:, 4:5], small[:, 3:4], ACT.Sqrt).then_inc(act_step, 1)

                def newton(i, last):
                    act.wait_ge(new_p, i + 1)
                    nc.scalar.mul(P15[:, :], Pm[:, :], 1.5).then_inc(act_ready, 1)
                    act.wait_ge(products, 3 * i + 2)
                    nc.scalar.copy(PS[:, :], ps_b[:, 0:128]).then_inc(act_ready, 1)
                peel(act, NT, newton)

            @block.vector
            def _(dve):
                done = [0]

                def step(ins):
                    done[0] += 1
                    ins.then_inc(dve_step, 1)
                    dve.wait_ge(dve_step, done[0])

                for g in range(GROUPS):
                    dve.wait_ge(x_loaded[g], 16)
                    last = nc.vector.reduce_sum(xs4[:, g:g + 1], X[:, g * HW:(g + 1) * HW], axis=AX.X)
                step(last)
                step(nc.vector.reduce_sum(small[:, 0:1], xs4[:, :], axis=AX.X))
                dve.wait_ge(pe_step, 1)
                step(nc.vector.tensor_scalar(small[:, 1:2], ps_a[:, 0:1], 1.0 / M_ALL, None, ALU.mult))
                for g in range(GROUPS):
                    v = X[:, g * HW:(g + 1) * HW]
                    nc.vector.tensor_scalar(v, v, small[:, 1:2], None, ALU.subtract).then_inc(centred, 1)

                def evac(it, last):
                    for b in range(2):
                        c = 2 * it + b
                        dve.wait_ge(transposed, c + 1)
                        wait(dve, grammed, c - 1)
                        nc.vector.tensor_copy(pix[b][:, :], ps_pix[b][0:112, :]).then_inc(evacuated, 1)
                peel(dve, IT, evac)
                dve.wait_ge(grammed, 2 * IT)
                step(nc.vector.tensor_tensor(S1[:, :], ps_gram[:, 0:128], same_image[:, :], ALU.mult))
                dve.wait_ge(pe_step, 2)
                step(nc.vector.reduce_sum(sig[:, :], sub(ps_b, 0, 128, 0, [[1, C], [C, GB]]), axis=AX.X))
                step(nc.vector.tensor_tensor(S2[:, :].rearrange("p (b c) -> p b c", c=C),
                                             sub(sig, 0, 128, 0, [[0, GB], [1, C]]),
                                             same_image[:, :].rearrange("p (b c) -> p b c", c=C), ALU.mult))
                step(nc.vector.scalar_tensor_tensor(S1[:, :], S2[:, :], 1.0 / M_ALL, eps_eye[:, :],
                                                    ALU.mult, ALU.add))
                step(nc.vector.tensor_tensor(S2[:, :], S1[:, :], shrink[:, :], ALU.mult))
                step(nc.vector.tensor_tensor(S1[:, :], S2[:, :], ident[:, :], ALU.mult))
                step(nc.vector.reduce_sum(small[:, 2:3], S1[:, :], axis=AX.X))
                dve.wait_ge(pe_step, 3)
                step(nc.vector.reciprocal(small[:, 3:4], ps_c[:, 0:1]))
                step(nc.vector.tensor_scalar(SN[:, :], S2[:, :], small[:, 3:4], None, ALU.mult))
                dve.wait_ge(act_step, 1)
                step(nc.vector.reciprocal(small[:, 5:6], small[:, 4:5]))
                step(nc.vector.scalar_tensor_tensor(small[:, 6:7], small[:, 5:6], small[:, 3:4], small[:, 4:5],
                                                    ALU.mult, ALU.add))
                step(nc.vector.tensor_scalar(small[:, 7:8], small[:, 6:7], 0.5, None, ALU.mult))
                nc.vector.tensor_copy(Pm[:, :], ident[:, :]).then_inc(new_p, 1)

                def newton(i, last):
                    dve.wait_ge(products, 3 * i + 1)
                    nc.vector.tensor_copy(PP[:, :], ps_a[:, 0:128]).then_inc(pp_ready, 1)
                    dve.wait_ge(products, 3 * i + 3)
                    dve.wait_ge(act_ready, 2 * i + 1)
                    nc.vector.scalar_tensor_tensor(Pm[:, :], ps_c[:, 0:128], -0.5, P15[:, :],
                                                   ALU.mult, ALU.add).then_inc(new_p, 1)
                peel(dve, NT, newton)
                dve.wait_ge(new_p, NT + 1)
                step(nc.vector.tensor_scalar(wm[:, :], Pm[:, :], small[:, 7:8], None, ALU.mult))

            @block.tensor
            def _(pe):
                pe.wait_ge(consts_loaded, 16 * len(LOADS))
                pe.wait_ge(dve_step, 2)
                nc.tensor.matmul(ps_a[:, 0:1], same_channel[:, :], small[:, 0:1],
                                 start=True, stop=True).then_inc(pe_step, 1)

                def gram(it, last, first):
                    for b in range(2):
                        c = 2 * it + b
                        pe.wait_ge(staged, c + 1)
                        wait(pe, evacuated, c - 1)
                        for i in range(4):
                            t = nc.tensor.transpose(ps_pix[b][0:112, i * 128:(i + 1) * 128],
                                                    flat[b][:, i * 112:(i + 1) * 112], ident[:, :])
                        t.then_inc(transposed, 1)
                        pe.wait_ge(evacuated, c + 1)
                        for i in range(4):
                            m = nc.tensor.matmul(ps_gram[:, 0:128], pix[b][:, i * 128:(i + 1) * 128],
                                                 pix[b][:, i * 128:(i + 1) * 128],
                                                 start=(first and b == 0 and i == 0), stop=(last and b == 1 and i == 3))
                        m.then_inc(grammed, 1)
                peel(pe, IT, lambda it, last: gram(it, last, isinstance(it, int) and it == 0))
                pe.wait_ge(dve_step, 4)
                nc.tensor.matmul(ps_b[:, 0:128], same_channel[:, :], S1[:, :], start=True, stop=True).then_inc(pe_step, 1)
                pe.wait_ge(dve_step, 10)
                nc.tensor.matmul(ps_c[:, 0:1], same_image[:, :], small[:, 2:3], start=True, stop=True).then_inc(pe_step, 1)
                pe.wait_ge(dve_step, 12)

                def newton(i, last):
                    pe.wait_ge(new_p, i + 1)
                    nc.tensor.matmul(ps_a[:, 0:128], Pm[:, :], Pm[:, :], start=True, stop=True).then_inc(products, 1)
                    nc.tensor.matmul(ps_b[:, 0:128], Pm[:, :], SN[:, :], start=True, stop=True).then_inc(products, 1)
                    pe.wait_ge(pp_ready, i + 1)
                    pe.wait_ge(act_ready, 2 * i + 2)
                    nc.tensor.matmul(ps_c[:, 0:128], PP[:, :], PS[:, :], start=True, stop=True).then_inc(products, 1)
                peel(pe, NT, newton)

        with ExitStack() as st:
            sb, ps, sem = tools(st)
            ROWS = 8
            CH = ROWS * W
            IT = H // ROWS
            xst = [sb(f"xst{i}", CH + W) for i in range(2)]
            xts = [sb(f"xts{i}", GB * ROWS * C, parts=W) for i in range(2)]
            ps_w = [ps(f"ps_w{i}") for i in range(2)]
            ps_x = [ps(f"ps_x{i}", 2) for i in range(2)]
            padded = sem("padded")
            whitened, with_beta, kept, turned, sorted_, stored_pads, stored_xh = [
                sem(n) for n in ("whitened", "with_beta", "kept", "turned", "sorted", "stored_pads", "stored_xh")]
            stored_xt = [sem(f"stored_xt{i}") for i in range(2)]
            block = st.enter_context(nc.Block())

            @block.tensor
            def _(pe):
                pe.wait_ge(padded, 2)

                def lead(c, g, yb):
                    wait(pe, with_beta, c - 1)
                    nc.tensor.matmul(ps_w[g % 2][:, 0:CH], wm[:, :], sub(X, 0, 128, g * HW + yb * CH, [[1, CH]]),
                                     start=True, stop=True).then_inc(whitened, 1)

                def body(yb, last):
                    for g in range(GROUPS):
                        c = yb * GROUPS + g
                        lead(c, g, yb)
                        pe.wait_ge(with_beta, c + 1)
                        wait(pe, sorted_, c - 1)
                        for r in range(ROWS):
                            t = nc.tensor.transpose(ps_x[g % 2][0:2 * W, r * 128:(r + 1) * 128],
                                                    xst[g % 2][:, r * W:(r + 2) * W], ident[:, :])
                        t.then_inc(turned, 1)
                peel(pe, IT, body)

            @block.scalar
            def _(act):
                def body(yb, last):
                    for g in range(GROUPS):
                        c = yb * GROUPS + g
                        act.wait_ge(whitened, c + 1)
                        wait(act, turned, c - 1)
                        wait(act, kept, c - 1)
                        nc.scalar.activation(xst[g % 2][:, 0:CH], ps_w[g % 2][:, 0:CH], ACT.Identity,
                                             bias=vecs[:, 0:1]).then_inc(with_beta, 1)
                peel(act, IT, body)

            @block.gpsimd
            def _(pool):
                for i in range(2):
                    pool.memset(xst[i][:, CH:CH + W], 0.0).then_inc(padded, 1)

                def body(yb, last):
                    for g in range(GROUPS):
                        pool.wait_ge(with_beta, yb * GROUPS + g + 1)
                        pool.tensor_copy(sub(XH, 0, 128, g * PADHW + (yb * ROWS + 1) * PADW + 1, [[PADW, ROWS], [1, W]]),
                                         xst[g % 2][:, 0:CH].rearrange("p (r w) -> p r w", w=W)).then_inc(kept, 1)
                peel(pool, IT, body)

            @block.vector
            def _(dve):
                def body(yb, last):
                    for g in range(GROUPS):
                        c = yb * GROUPS + g
                        dve.wait_ge(turned, c + 1)
                        wait(dve, stored_xt[g % 2], 16 * (yb * 2 + g // 2))
                        for h in range(2):
                            e = nc.vector.tensor_copy(
                                sub(xts[g % 2], 0, W, h * 4 * C, [[ROWS * C, GB], [C, 4], [1, C]]),
                                sub(ps_x[g % 2], 0, W, h * 512, [[C, GB], [128, 4], [1, C]]))
                        e.then_inc(sorted_, 1)
                peel(dve, IT, body)

            @block.sync
            def _(sp):
                for first in (TOP - NEAR, TOP + H):
                    sp.dma_start(dram("xt", first * C, [[XT_ROW, W], [W * XT_ROW, B], [1, NEAR * C]]),
                                 sub(zeros, 0, W, 0, [[0, B], [1, NEAR * C]])).then_inc(stored_pads, 16)

                for row in (0, H + 1):
                    sp.dma_start(dram("xh", row * PADW, [[PADHW, 128], [128 * PADHW, GROUPS], [1, PADW]]),
                                 sub(XH, 0, 128, row * PADW, [[PADHW, GROUPS], [1, PADW]])).then_inc(stored_xh, 16)

                def body(yb, last):
                    for g in range(GROUPS):
                        sp.wait_ge(sorted_, yb * GROUPS + g + 1)
                        sp.dma_start(dram("xt", g * GB * W * XT_ROW + (TOP + yb * ROWS) * C,
                                          [[XT_ROW, W], [W * XT_ROW, GB], [1, ROWS * C]]),
                                     sub(xts[g % 2], 0, W, 0, [[ROWS * C, GB], [1, ROWS * C]])).then_inc(stored_xt[g % 2], 16)
                        sp.wait_ge(kept, yb * GROUPS + g + 1)
                        sp.dma_start(dram("xh", g * 128 * PADHW + (yb * ROWS + 1) * PADW, [[PADHW, 128], [1, ROWS * PADW]]),
                                     sub(XH, 0, 128, g * PADHW + (yb * ROWS + 1) * PADW, [[1, ROWS * PADW]])
                                     ).then_inc(stored_xh, 16)
                peel(sp, IT, body)
                sp.wait_ge(stored_xh, 16 * (IT * GROUPS + 2))
                sp.wait_ge(stored_pads, 32)
                for i in range(2):
                    sp.wait_ge(stored_xt[i], 16 * IT * 2)

        with ExitStack() as st:
            sb, ps, sem = tools(st)
            ROWS = 8
            CH = ROWS * W
            NCH = H // ROWS
            SHIFTS = 3 * 2 * C
            woff = sb("woff", 3 * 96, parts=SHIFTS)
            boff = sb("boff", 1, parts=96)
            x3 = [sb(f"x3{i}", H * PADW, parts=SHIFTS) for i in range(2)]
            om = [sb(f"om{i}", HW, parts=96) for i in range(2)]
            ps_o = [ps(f"ps_o{i}") for i in range(2)]
            w_loaded, convolved, biased = sem("w_loaded"), sem("convolved"), sem("biased")
            x3_loaded = [sem(f"x3_loaded{i}") for i in range(2)]
            om_stored = [sem(f"om_stored{i}") for i in range(2)]
            block = st.enter_context(nc.Block())

            @block.sync
            def _(sp):
                sp.dma_start(woff[:, :], dram("woff", 0, [[3 * 96, SHIFTS], [1, 3 * 96]])).then_inc(w_loaded, 16)
                sp.dma_start(boff[:, :], dram("boff", 0, [[1, 96], [1, 1]])).then_inc(w_loaded, 16)

                def body(it, last):
                    for b in range(2):
                        pair = 2 * it + b
                        wait(sp, convolved, (pair - 1) * NCH)
                        for dy in range(3):
                            sp.dma_start(sub(x3[b], dy * 2 * C, 2 * C, 0, [[1, H * PADW]]),
                                         dram("xh", pair * 2 * C * PADHW + dy * PADW,
                                              [[PADHW, 2 * C], [1, H * PADW]])).then_inc(x3_loaded[b], 16)
                peel(sp, PAIRS // 2, body)

            @block.tensor
            def _(pe):
                pe.wait_ge(w_loaded, 32)

                def body(it, last):
                    for b in range(2):
                        pair = 2 * it + b
                        pe.wait_ge(x3_loaded[b], 48 * (it + 1))
                        for ch in range(NCH):
                            n = pair * NCH + ch
                            bank = (b * NCH + ch) % 2
                            wait(pe, biased, n - 1)
                            for kx in range(3):
                                m = nc.tensor.matmul(ps_o[bank][0:96, 0:CH], woff[:, kx * 96:(kx + 1) * 96],
                                                     sub(x3[b], 0, SHIFTS, ch * ROWS * PADW + kx, [[PADW, ROWS], [1, W]]),
                                                     start=(kx == 0), stop=(kx == 2))
                            m.then_inc(convolved, 1)
                peel(pe, PAIRS // 2, body)

            @block.scalar
            def _(act):
                act.wait_ge(w_loaded, 32)

                def body(it, last):
                    for b in range(2):
                        pair = 2 * it + b
                        wait(act, om_stored[b], 48 * it)
                        for ch in range(NCH):
                            n = pair * NCH + ch
                            act.wait_ge(convolved, n + 1)
                            nc.scalar.activation(om[b][:, ch * CH:(ch + 1) * CH], ps_o[(b * NCH + ch) % 2][0:96, 0:CH],
                                                 ACT.Identity, bias=boff[:, 0:1]).then_inc(biased, 1)
                        act.wait_ge(biased, (pair + 1) * NCH)
                        for kind in range(3):
                            act.dma_start(dram("om", kind * PLANE + pair * 2 * KK * HW, [[HW, 2 * KK], [1, HW]]),
                                          sub(om[b], 32 * kind, 2 * KK, 0, [[1, HW]])).then_inc(om_stored[b], 16)
                peel(act, PAIRS // 2, body)
                for b in range(2):
                    act.wait_ge(om_stored[b], 48 * PAIRS // 2)

        with ExitStack() as st:
            sb, ps, sem = tools(st)
            RPC = DCH // W
            val = [sb(f"val{i}", 3 * DCH) for i in range(D_RING)]
            px = [sb(f"px{i}", DCH) for i in range(D_RING)]
            logit = [sb(f"logit{i}", DCH) for i in range(D_RING)]
            grid = [sb(f"grid{i}", DCH) for i in range(D_RING)]
            parts = [sb(f"parts{i}", KINDS * DCH, f32r) for i in range(D_RING)]
            row_max, row_min = sb("row_max", DENSE // W), sb("row_min", DENSE // W)
            loaded = [sem(f"loaded{i}") for i in range(D_RING)]
            stored = [sem(f"stored{i}") for i in range(D_RING)]
            masked, summed, ranged, scaled, high, low, ranges_stored = [sem(n) for n in (
                "masked", "summed", "ranged", "scaled", "high", "low", "ranges_stored")]
            block = st.enter_context(nc.Block())

            def part(b, k):
                return sub(parts[b], 0, 128, k * DCH, [[2 * DCH, 3], [1, DCH]])

            def three(tile):
                return sub(tile, 0, 128, 0, [[DCH, 3], [1, DCH]])

            def overlapped(eng, lead, tail):
                lead(0, 0)

                def body(it, last):
                    for b in range(D_RING):
                        wrap = b == D_RING - 1
                        if not (last and wrap):
                            lead(it + (1 if wrap else 0), 0 if wrap else b + 1)
                        tail(it, b)
                peel(eng, D_IT, body)

            @block.sync
            def _(sp):
                def lead(it, b):
                    n = D_RING * it + b
                    wait(sp, low, n - D_RING + 1)
                    for tile, off, kind in ((logit[b], 0, 2), (px[b], 0, 1), (val[b], 2 * DCH, 0)):
                        sp.dma_start(sub(tile, 0, 128, off, [[1, DCH]]),
                                     dram("om", kind * PLANE + n * DCH, [[DENSE, 128], [1, DCH]])).then_inc(loaded[b], 16)
                    sp.dma_start(grid[b][:, :], dram("grid", n * DCH, [[DENSE, 128], [1, DCH]])).then_inc(loaded[b], 16)

                def body(it, last):
                    for b in range(D_RING):
                        lead(it, b)
                peel(sp, D_IT, body)
                sp.wait_ge(ranged, D_RING * D_IT)
                for tile, name in ((row_max, "row_max"), (row_min, "row_min")):
                    sp.dma_start(dram(name, 0, [[DENSE // W, 128], [1, DENSE // W]]), tile[:, :]).then_inc(ranges_stored, 16)
                for b in range(D_RING):
                    sp.wait_ge(stored[b], 16 * D_IT)
                sp.wait_ge(ranges_stored, 32)

            @block.scalar
            def _(act):
                def lead(it, b):
                    n = D_RING * it + b
                    act.wait_ge(loaded[b], 64 * (it + 1))
                    nc.scalar.activation(sub(val[b], 0, 128, DCH, [[1, DCH]]), logit[b][:, :], ACT.Sigmoid).then_inc(masked, 1)

                def store(it, b):
                    n = D_RING * it + b
                    act.wait_ge(low, n + 1)
                    act.dma_start(dram("parts", n * DCH, [[DENSE, 128], [PLANE, KINDS], [1, DCH]]),
                                  sub(parts[b], 0, 128, 0, [[DCH, KINDS], [1, DCH]]).bitcast(fp32)).then_inc(stored[b], 16)

                def tail(it, b):
                    n = D_RING * it + b
                    act.wait_ge(scaled, n + 1)
                    wait(act, stored[b], 16 * it)
                    nc.scalar.copy(part(b, 0), three(val[b])).then_inc(high, 1)
                    if b or not (isinstance(it, int) and it == 0):
                        store(it if b else it - 1, (b - 1) % D_RING)
                overlapped(act, lead, tail)
                store(D_IT - 1, D_RING - 1)

            @block.gpsimd
            def _(pool):
                def body(it, last):
                    for b in range(D_RING):
                        n = D_RING * it + b
                        pool.wait_ge(high, n + 1)
                        pool.tensor_tensor(part(b, 1), three(val[b]), part(b, 0).bitcast(fp32), ALU.subtract).then_inc(low, 1)
                peel(pool, D_IT, body)

            @block.vector
            def _(dve):
                def body(it, last):
                    for b in range(D_RING):
                        n = D_RING * it + b
                        dve.wait_ge(loaded[b], 64 * (it + 1))
                        nc.vector.tensor_tensor(px[b][:, :], px[b][:, :], grid[b][:, :], ALU.add).then_inc(summed, 1)
                        oy = sub(val[b], 0, 128, 2 * DCH, [[W, RPC], [1, W]])
                        nc.vector.tensor_reduce(sub(row_max, 0, 128, n * RPC, [[1, RPC]]), oy, axis=AX.X, op=ALU.max)
                        nc.vector.tensor_reduce(sub(row_min, 0, 128, n * RPC, [[1, RPC]]), oy, axis=AX.X,
                                                op=ALU.min).then_inc(ranged, 1)
                        dve.wait_ge(summed, n + 1)
                        dve.wait_ge(masked, n + 1)
                        nc.vector.tensor_tensor(sub(val[b], 0, 128, 0, [[1, DCH]]), sub(val[b], 0, 128, DCH, [[1, DCH]]),
                                                px[b][:, :], ALU.mult).then_inc(scaled, 1)
                peel(dve, D_IT, body)

        with ExitStack() as st:
            sb, ps, sem = tools(st)
            ROW = TAPS_PX
            sel32 = sb("sel32", 4 * 128)
            sel = sb("sel", 4 * 128, f32r)
            sel_plus, sel_minus, sel_y = sel[:, 0:128], sel[:, 128:256], [sel[:, 256:384], sel[:, 384:512]]
            win_bias = sb("win_bias", N_WIN)
            conv_w = sb("conv_w", KK * 32)
            conv_b = sb("conv_b", 1)
            stage = [[sb(f"stage{b}{i}", STAGE_ROWS * C) for i in range(2)] for b in range(2)]
            rows = [sb(f"rows{b}", KK * UPX, f32r) for b in range(2)]
            plus = [sb(f"plus{b}", ROW) for b in range(2)]
            tent_x = [sb(f"tent_x{b}", ROW) for b in range(2)]
            dist_y = [sb(f"dist_y{b}", 2 * ROW) for b in range(2)]
            G = [sb(f"G{b}", 2 * UNIT_ROWS * ROW) for b in range(2)]
            res = [sb(f"res{b}", UPX // 2) for b in range(2)]
            ps_p, ps_m = ps("ps_p"), ps("ps_m")
            ps_y, ps_v = ps("ps_y", 2), ps("ps_v", 2)
            ps_r = [ps(f"ps_r{b}") for b in range(2)]
            consts_loaded, cleared, cast = sem("dcn_consts_loaded"), sem("cleared"), sem("cast")
            stage_loaded = [sem(f"stage_loaded{b}") for b in range(2)]
            rows_loaded = [sem(f"rows_loaded{b}") for b in range(2)]
            x_spread, y_spread, plus_ready, tent_ready, dist_ready, dist_capped, sampled, weighted, reduced, res_ready = [
                sem(n) for n in ("x_spread", "y_spread", "plus_ready", "tent_ready", "dist_ready", "dist_capped",
                                 "sampled", "weighted", "reduced", "res_ready")]
            res_stored = [sem(f"res_stored{b}") for b in range(2)]
            LOADS = ((sel32, "sel"), (win_bias, "win_bias"), (conv_w, "conv_w"), (conv_b, "conv_b"))
            IT = N_UNITS // 2
            block = st.enter_context(nc.Block())

            def place(eng, it, b):
                pair, u = it // (UNITS // 2), (it % (UNITS // 2)) * 2 + b
                return (pair, u) if isinstance(it, int) else (eng.snap(pair), eng.snap(u))

            def load_unit(eng, b, pair, u, win):
                for i in range(2):
                    eng.dma_start(sub(stage[b][i], 64 * i, W, 0, [[1, STAGE_ROWS * C]]),
                                  dram("xt", (pair * 2 + i) * W * XT_ROW + (TOP - 1 + u * UNIT_ROWS + WIN * win - 60) * C,
                                       [[XT_ROW, W], [1, STAGE_ROWS * C]])).then_inc(stage_loaded[b], 16)

            def load_rows(eng, b, pair, u):
                for i in range(2):
                    eng.dma_start(sub(rows[b], KINDS * i, KINDS, 0, [[UPX, KK], [1, UPX]]).bitcast(fp32),
                                  dram("parts", (pair * 2 + i) * KK * HW + u * UPX,
                                       [[PLANE, KINDS], [HW, KK], [1, UPX]])).then_inc(rows_loaded[b], 16)

            def conv_rows(b, pair, u):
                for j in range(4):
                    i, h = j // 2, j % 2
                    yield (dram("conv", (pair * 2 + i) * O * HW + u * UPX + h * (UPX // 2), [[HW, O], [1, UPX // 2]]),
                           sub(res[b], 32 * j, O, 0, [[1, UPX // 2]]))

            def taps(b, q):
                return sub(rows[b], 0, 128, q * W, [[UPX, KK], [1, W]])

            @block.sync
            def _(sp):
                sp.wait_ge(cleared, 6)

                def store(it, b):
                    where = place(sp, it, b)
                    sp.wait_ge(res_ready, 2 * it + b + 1)
                    for dst, src in conv_rows(b, *where):
                        sp.dma_start(dst, src).then_inc(res_stored[b], 16)

                def body(it, last):
                    for b in range(2):
                        n = 2 * it + b
                        pair, u = place(sp, it, b)
                        wait(sp, sampled, 2 * UNIT_ROWS * (n - 1))
                        load_unit(sp, b, pair, u, BASE_WIN)
                        wait(sp, y_spread, UNIT_ROWS * (n - 1))
                        load_rows(sp, b, pair, u)
                        if not (isinstance(it, int) and it == 0):
                            store(it - 1, b)
                peel(sp, IT, body)
                for b in range(2):
                    store(IT - 1, b)
                for b in range(2):
                    sp.wait_ge(res_stored[b], 64 * IT)

            @block.gpsimd
            def _(pool):
                for b in range(2):
                    for i in range(2):
                        pool.memset(stage[b][i][:, :], 0.0).then_inc(cleared, 1)
                    pool.memset(rows[b][:, :].bitcast(fp32), 0.0).then_inc(cleared, 1)

            def stream(eng, lead, work, after=None):
                lead(0, 0, 0)

                def body(it, last):
                    for b in range(2):
                        for q in range(UNIT_ROWS):
                            wrap = q == UNIT_ROWS - 1
                            if not (last and b == 1 and wrap):
                                lead(it + (1 if wrap and b else 0), (1 - b) if wrap else b, (q + 1) % UNIT_ROWS)
                            work(it, b, q)
                            if after and q == 1 and not (isinstance(it, int) and it == 0 and b == 0):
                                after(it - 1 + b, 1 - b)
                peel(eng, IT, body)
                if after:
                    after(IT - 1, 1)

            @block.tensor
            def _(pe):
                pe.wait_ge(cast, 1)
                pe.wait_ge(consts_loaded, 16 * len(LOADS))

                def lead(it, b, q):
                    r = (2 * it + b) * UNIT_ROWS + q
                    if q == 0:
                        pe.wait_ge(rows_loaded[b], 32 * (it + 1))
                    wait(pe, plus_ready, r)
                    nc.tensor.matmul(ps_p[:, 0:ROW], sel_plus, taps(b, q), start=True, stop=True)
                    wait(pe, tent_ready, r)
                    nc.tensor.matmul(ps_m[:, 0:ROW], sel_minus, taps(b, q), start=True, stop=True).then_inc(x_spread, 1)
                    wait(pe, dist_ready, r)
                    for i in range(2):
                        m = nc.tensor.matmul(ps_y[:, i * 512:i * 512 + ROW], sel_y[i], taps(b, q), start=True, stop=True)
                    m.then_inc(y_spread, 1)

                def work(it, b, q):
                    r = (2 * it + b) * UNIT_ROWS + q
                    if q == 0:
                        pe.wait_ge(stage_loaded[b], 32 * (it + 1))
                    pe.wait_ge(tent_ready, r + 1)
                    for i in range(2):
                        wait(pe, weighted, 2 * r - 1 + i)
                        for ky in range(3):
                            m = nc.tensor.matmul(ps_v[:, i * 512 + ky * 3 * W:i * 512 + (ky + 1) * 3 * W],
                                                 stage[b][i][:, (q + ky) * C:(q + ky + WIN) * C],
                                                 tent_x[q % 2][:, ky * 3 * W:(ky + 1) * 3 * W],
                                                 start=True, stop=True)
                        m.then_inc(sampled, 1)

                def after(it, b):
                    n = 2 * it + b
                    pe.wait_ge(weighted, 2 * UNIT_ROWS * (n + 1))
                    wait(pe, res_ready, n - 1)
                    for k in range(KK):
                        for j in range(4):
                            i, h = j // 2, j % 2
                            m = nc.tensor.matmul(ps_r[b][32 * j:32 * j + 32, 0:UPX // 2], conv_w[:, k * 32:(k + 1) * 32],
                                                 sub(G[b], 0, 128, (i * UNIT_ROWS + 2 * h) * ROW + k * W, [[ROW, 2], [1, W]]),
                                                 start=(k == 0), stop=(k == KK - 1))
                    m.then_inc(reduced, 1)
                stream(pe, lead, work, after)

            @block.scalar
            def _(act):
                for tile, name in LOADS:
                    n = tile[:].shape[1]
                    act.dma_start(tile[:, :], dram(name, 0, [[n, 128], [1, n]])).then_inc(consts_loaded, 16)
                act.wait_ge(consts_loaded, 16 * len(LOADS))
                nc.scalar.copy(sel[:, :], sel32[:, :]).then_inc(cast, 1)

                def lead(it, b, q):
                    r = (2 * it + b) * UNIT_ROWS + q
                    act.wait_ge(x_spread, r + 1)
                    wait(act, tent_ready, r - 1)
                    nc.scalar.activation(plus[q % 2][:, :], ps_p[:, 0:ROW], ACT.Relu).then_inc(plus_ready, 1)
                    act.wait_ge(y_spread, r + 1)
                    wait(act, weighted, 2 * (r - 1))
                    nc.scalar.activation(sub(dist_y[q % 2], 0, 128, 0, [[ROW, 2], [1, ROW]]),
                                         sub(ps_y, 0, 128, 0, [[512, 2], [1, ROW]]), ACT.Abs,
                                         bias=win_bias[:, BASE_WIN:BASE_WIN + 1]).then_inc(dist_ready, 1)

                def after(it, b):
                    n = 2 * it + b
                    act.wait_ge(reduced, n + 1)
                    wait(act, res_stored[b], 64 * it)
                    nc.scalar.activation(res[b][:, :], ps_r[b][:, 0:UPX // 2], ACT.Identity, scale=-1.0,
                                         bias=conv_b[:, 0:1]).then_inc(res_ready, 1)
                stream(act, lead, lambda it, b, q: None, after)

            @block.vector
            def _(dve):
                def lead(it, b, q):
                    r = (2 * it + b) * UNIT_ROWS + q
                    dve.wait_ge(x_spread, r + 1)
                    dve.wait_ge(plus_ready, r + 1)
                    wait(dve, sampled, 2 * (r - 1))
                    nc.vector.scalar_tensor_tensor(tent_x[q % 2][:, :], ps_m[:, 0:ROW], 0.0, plus[q % 2][:, :],
                                                   ALU.max, ALU.min).then_inc(tent_ready, 1)

                def work(it, b, q):
                    r = (2 * it + b) * UNIT_ROWS + q
                    if q == 0:
                        wait(dve, reduced, 2 * it + b - 1)
                    dve.wait_ge(dist_ready, r + 1)
                    nc.vector.tensor_scalar(dist_y[q % 2][:, :], dist_y[q % 2][:, :], 1.0, 1.0,
                                            ALU.min, ALU.subtract).then_inc(dist_capped, 1)
                    dve.wait_ge(dist_capped, r + 1)
                    for i in range(2):
                        dve.wait_ge(sampled, 2 * r + 1 + i)
                        nc.vector.tensor_tensor(
                            sub(G[b], 0, 128, (i * UNIT_ROWS + q) * ROW, [[1, ROW]]),
                            sub(dist_y[q % 2], 0, 128, i * ROW, [[1, ROW]]),
                            sub(ps_v, 0, 128, i * 512, [[1, ROW]]), ALU.mult).then_inc(weighted, 1)
                stream(dve, lead, work)

        with ExitStack() as st:
            sb, ps, sem = tools(st)
            ROW = TAPS_PX
            TABLE = N_UNITS * N_WIN
            PU = UNITS * N_WIN
            ranges = sb("ranges", 2 * 2 * KK * H, parts=PAIRS)
            unit_range = sb("unit_range", 2 * UNITS, parts=PAIRS)
            bounds = sb("bounds", 2 * N_WIN, parts=PAIRS)
            need = sb("need", 2 * PU, parts=PAIRS)
            needed, ordinal, numbered = (X[0:1, k * TABLE:(k + 1) * TABLE] for k in range(3))
            by_unit = sb("by_unit", N_UNITS, parts=1)
            by_pair = sb("by_pair", PAIRS, parts=1)
            turn_of = sb("turn_of", TABLE, i32, parts=1)
            any_unit = sb("any_unit", N_UNITS, i32, parts=1)
            any_pair = sb("any_pair", PAIRS, i32, parts=1)
            far_count = sb("far_count", 3, parts=1)
            any_far = sb("any_far", 1, i32, parts=1)
            xsel32 = sb("xsel32", 4 * 128)
            xsel = sb("xsel", 4 * 128, f32r)
            xwin_bias = sb("xwin_bias", N_WIN)
            xconv_w = sb("xconv_w", KK * 32)
            xstage = [sb(f"xstage{i}", STAGE_ROWS * C) for i in range(2)]
            xrows = sb("xrows", KK * UPX, f32r)
            xplus, xtent = sb("xplus", ROW), sb("xtent", ROW)
            xdist = sb("xdist", 2 * ROW)
            xG = sb("xG", 2 * UNIT_ROWS * ROW)
            before, added_to = sb("before", UPX // 2), sb("added_to", UPX // 2)
            xps_p, xps_m, xps_r = ps("xps_p"), ps("xps_m"), ps("xps_r")
            xps_y, xps_v = ps("xps_y", 2), ps("xps_v", 2)
            names = ("x_consts", "x_cleared", "x_cast", "x_ranges", "x_step", "x_need_stored", "x_need_loaded", "x_tables",
                     "x_pads", "x_loaded", "x_before", "x_reduced", "x_added", "x_stored", "x_turn")
            S = {n: sem(n) for n in names}
            Q = {n: [sem(f"{n}_row{q}") for q in range(UNIT_ROWS)] for n in (
                "x_spreads", "x_plus_ready", "x_tent_ready", "x_dist_ready", "x_capped", "x_sampled", "x_weighted")}
            block = st.enter_context(nc.Block())

            def windows(eng, work):
                eng.wait_ge(S["x_tables"], 4)
                with eng.Fori(0, PAIRS) as pair:
                    some = eng.value_load(any_pair[0:1, bass.ds(pair, 1)], min_val=0, max_val=1)
                    with eng.If(some > 0):
                        with eng.Fori(0, UNITS) as u:
                            some_u = eng.value_load(any_unit[0:1, bass.ds(pair * UNITS + u, 1)], min_val=0, max_val=1)
                            with eng.If(some_u > 0):
                                with eng.Fori(0, N_WIN) as win:
                                    turn = eng.value_load(turn_of[0:1, bass.ds((pair * UNITS + u) * N_WIN + win, 1)],
                                                          min_val=0, max_val=TABLE)
                                    with eng.If(turn > 0):
                                        work(turn, pair, u, win)
                                    eng.nop()
                            eng.nop()
                    eng.nop()

            def xconv_rows(tile, pair, u):
                for j in range(4):
                    i, h = j // 2, j % 2
                    yield (dram("conv", (pair * 2 + i) * O * HW + u * UPX + h * (UPX // 2), [[HW, O], [1, UPX // 2]]),
                           sub(tile, 32 * j, O, 0, [[1, UPX // 2]]))

            @block.sync
            def _(sp):
                for k, name in enumerate(("row_max", "row_min")):
                    n = 2 * KK * H
                    sp.dma_start(sub(ranges, 0, PAIRS, k * n, [[1, n]]), dram(name, 0, [[n, PAIRS], [1, n]])).then_inc(S["x_ranges"], 16)
                sp.dma_start(bounds[:, :], dram("bounds", 0, [[2 * N_WIN, PAIRS], [1, 2 * N_WIN]])).then_inc(S["x_ranges"], 16)
                sp.wait_ge(S["x_step"], 6)
                sp.dma_start(dram("needed", 0, [[PU, PAIRS], [1, PU]]), need[:, 0:PU]).then_inc(S["x_need_stored"], 16)
                sp.wait_ge(S["x_need_stored"], 16)
                sp.dma_start(needed, dram("needed", 0, [[TABLE, 1], [1, TABLE]])).then_inc(S["x_need_loaded"], 16)
                sp.wait_ge(S["x_cleared"], 5)
                sp.wait_ge(S["x_tables"], 4)
                far = sp.value_load(any_far[0:1, 0:1], min_val=0, max_val=1)
                with sp.If(far > 0):
                    for a, z in ((0, TOP - NEAR), (TOP + H + NEAR, XT_ROWS)):
                        sp.dma_start(dram("xt", a * C, [[XT_ROW, W], [W * XT_ROW, B], [1, (z - a) * C]]),
                                     sub(zeros, 0, W, 0, [[0, B], [1, (z - a) * C]])).then_inc(S["x_pads"], 16)
                    sp.wait_ge(S["x_pads"], 32)
                sp.nop()

                def work(turn, pair, u, win):
                    for i in range(2):
                        sp.dma_start(sub(xstage[i], 64 * i, W, 0, [[1, STAGE_ROWS * C]]),
                                     dram("xt", (pair * 2 + i) * W * XT_ROW + (TOP - 1 - 60 + u * UNIT_ROWS + win * WIN) * C,
                                          [[XT_ROW, W], [1, STAGE_ROWS * C]])).then_inc(S["x_loaded"], 16)
                        sp.dma_start(sub(xrows, KINDS * i, KINDS, 0, [[UPX, KK], [1, UPX]]).bitcast(fp32),
                                     dram("parts", (pair * 2 + i) * KK * HW + u * UPX,
                                          [[PLANE, KINDS], [HW, KK], [1, UPX]])).then_inc(S["x_loaded"], 16)
                    for there, here in xconv_rows(before, pair, u):
                        sp.dma_start(here, there).then_inc(S["x_before"], 16)
                    sp.wait_ge(S["x_added"], turn)
                    sp.sem_inc(S["x_turn"], 1)
                    for there, here in xconv_rows(added_to, pair, u):
                        sp.dma_start(there, here).then_inc(S["x_stored"], 16)
                    sp.wait_ge(S["x_stored"], 64 * turn)
                    sp.sem_inc(S["x_turn"], 1)
                windows(sp, work)

            @block.gpsimd
            def _(pool):
                for tile in (xstage[0][:, :], xstage[1][:, :], xrows[:, :].bitcast(fp32), before[:, :], added_to[:, :]):
                    pool.memset(tile, 0.0).then_inc(S["x_cleared"], 1)

            @block.vector
            def _(dve):
                done = [0]

                def step(ins):
                    done[0] += 1
                    ins.then_inc(S["x_step"], 1)
                    dve.wait_ge(S["x_step"], done[0])

                dve.wait_ge(S["x_ranges"], 48)
                n = 2 * KK * H
                step(nc.vector.tensor_reduce(unit_range[:, 0:UNITS],
                                             sub(ranges, 0, PAIRS, 0, [[UNIT_ROWS, UNITS], [H, 2 * KK], [1, UNIT_ROWS]]),
                                             axis=AX.XY, op=ALU.max))
                step(nc.vector.tensor_reduce(unit_range[:, UNITS:],
                                             sub(ranges, 0, PAIRS, n, [[UNIT_ROWS, UNITS], [H, 2 * KK], [1, UNIT_ROWS]]),
                                             axis=AX.XY, op=ALU.min))
                for side, op in ((0, ALU.is_gt), (1, ALU.is_lt)):
                    step(nc.vector.tensor_tensor(sub(need, 0, PAIRS, side * PU, [[N_WIN, UNITS], [1, N_WIN]]),
                                                 sub(unit_range, 0, PAIRS, side * UNITS, [[1, UNITS], [0, N_WIN]]),
                                                 sub(bounds, 0, PAIRS, side * N_WIN, [[0, UNITS], [1, N_WIN]]), op))
                step(nc.vector.tensor_tensor(need[:, PU:], need[:, 0:PU], need[:, PU:], ALU.max))
                step(nc.vector.tensor_copy(need[:, 0:PU], need[:, PU:]))
                dve.wait_ge(S["x_need_loaded"], 16)
                step(nc.vector.tensor_tensor_scan(ordinal, needed, needed, 0.0, ALU.add, ALU.bypass))
                step(nc.vector.tensor_tensor(numbered, ordinal, needed, ALU.mult))
                step(nc.vector.tensor_reduce(by_unit[:, :], sub(X, 0, 1, 0, [[N_WIN, N_UNITS], [1, N_WIN]]),
                                             axis=AX.X, op=ALU.max))
                step(nc.vector.tensor_reduce(by_pair[:, :], sub(X, 0, 1, 0, [[PU, PAIRS], [1, PU]]),
                                             axis=AX.X, op=ALU.max))
                for k, first in enumerate((0, BASE_WIN + 2)):
                    step(nc.vector.tensor_reduce(far_count[:, k:k + 1], sub(X, 0, 1, first, [[N_WIN, N_UNITS], [1, BASE_WIN - 1]]),
                                                 axis=AX.XY, op=ALU.max))
                step(nc.vector.tensor_tensor(far_count[:, 2:3], far_count[:, 0:1], far_count[:, 1:2], ALU.max))
                nc.vector.tensor_copy(any_far[:, :], far_count[:, 2:3]).then_inc(S["x_tables"], 1)
                nc.vector.tensor_copy(turn_of[:, :], numbered).then_inc(S["x_tables"], 1)
                nc.vector.tensor_copy(any_unit[:, :], by_unit[:, :]).then_inc(S["x_tables"], 1)
                nc.vector.tensor_copy(any_pair[:, :], by_pair[:, :]).then_inc(S["x_tables"], 1)

                def work(turn, pair, u, win):
                    for q in range(UNIT_ROWS):
                        dve.wait_ge(Q["x_plus_ready"][q], turn)
                        nc.vector.scalar_tensor_tensor(xtent[:, :], xps_m[:, 0:ROW], 0.0, xplus[:, :],
                                                       ALU.max, ALU.min).then_inc(Q["x_tent_ready"][q], 1)
                        dve.wait_ge(Q["x_dist_ready"][q], turn)
                        nc.vector.tensor_scalar(xdist[:, :], xdist[:, :], 1.0, 1.0, ALU.min, ALU.subtract).then_inc(Q["x_capped"][q], 1)
                        dve.wait_ge(Q["x_capped"][q], turn)
                        dve.wait_ge(Q["x_sampled"][q], turn)
                        nc.vector.tensor_tensor(sub(xG, 0, 128, q * ROW, [[UNIT_ROWS * ROW, 2], [1, ROW]]),
                                                sub(xdist, 0, 128, 0, [[ROW, 2], [1, ROW]]),
                                                sub(xps_v, 0, 128, 0, [[512, 2], [1, ROW]]), ALU.mult).then_inc(Q["x_weighted"][q], 1)
                    dve.wait_ge(S["x_reduced"], turn)
                    dve.wait_ge(S["x_before"], 64 * turn)
                    nc.vector.scalar_tensor_tensor(added_to[:, :], xps_r[:, 0:UPX // 2], -1.0, before[:, :],
                                                   ALU.mult, ALU.add).then_inc(S["x_added"], 1)
                windows(dve, work)

            @block.scalar
            def _(act):
                for tile, name in ((xsel32, "sel"), (xwin_bias, "win_bias"), (xconv_w, "conv_w")):
                    n = tile[:].shape[1]
                    act.dma_start(tile[:, :], dram(name, 0, [[n, 128], [1, n]])).then_inc(S["x_consts"], 16)
                act.wait_ge(S["x_consts"], 48)
                nc.scalar.copy(xsel[:, :], xsel32[:, :]).then_inc(S["x_cast"], 1)

                def work(turn, pair, u, win):
                    for q in range(UNIT_ROWS):
                        act.wait_ge(Q["x_spreads"][q], turn)
                        nc.scalar.activation(xplus[:, :], xps_p[:, 0:ROW], ACT.Relu).then_inc(Q["x_plus_ready"][q], 1)
                        nc.scalar.activation(sub(xdist, 0, 128, 0, [[ROW, 2], [1, ROW]]),
                                             sub(xps_y, 0, 128, 0, [[512, 2], [1, ROW]]), ACT.Abs,
                                             bias=sub(xwin_bias, 0, 128, win, [[1, 1]])).then_inc(Q["x_dist_ready"][q], 1)
                windows(act, work)

            @block.tensor
            def _(pe):
                pe.wait_ge(S["x_cast"], 1)
                pe.wait_ge(S["x_cleared"], 5)
                taps = lambda q: sub(xrows, 0, 128, q * W, [[UPX, KK], [1, W]])

                def work(turn, pair, u, win):
                    pe.wait_ge(S["x_loaded"], 64 * turn)
                    for q in range(UNIT_ROWS):
                        if q:
                            pe.wait_ge(Q["x_weighted"][q - 1], turn)
                        nc.tensor.matmul(xps_p[:, 0:ROW], xsel[:, 0:128], taps(q), start=True, stop=True)
                        nc.tensor.matmul(xps_m[:, 0:ROW], xsel[:, 128:256], taps(q), start=True, stop=True)
                        for i in range(2):
                            m = nc.tensor.matmul(xps_y[:, i * 512:i * 512 + ROW], xsel[:, (2 + i) * 128:(3 + i) * 128],
                                                 taps(q), start=True, stop=True)
                        m.then_inc(Q["x_spreads"][q], 1)
                        pe.wait_ge(Q["x_tent_ready"][q], turn)
                        for i in range(2):
                            for ky in range(3):
                                m = nc.tensor.matmul(xps_v[:, i * 512 + ky * 3 * W:i * 512 + (ky + 1) * 3 * W],
                                                     xstage[i][:, (q + ky) * C:(q + ky + WIN) * C],
                                                     xtent[:, ky * 3 * W:(ky + 1) * 3 * W], start=True, stop=True)
                        m.then_inc(Q["x_sampled"][q], 1)
                    pe.wait_ge(Q["x_weighted"][UNIT_ROWS - 1], turn)
                    for k in range(KK):
                        for j in range(4):
                            i, h = j // 2, j % 2
                            m = nc.tensor.matmul(xps_r[32 * j:32 * j + 32, 0:UPX // 2], xconv_w[:, k * 32:(k + 1) * 32],
                                                 sub(xG, 0, 128, (i * UNIT_ROWS + 2 * h) * ROW + k * W, [[ROW, 2], [1, W]]),
                                                 start=(k == 0), stop=(k == KK - 1))
                    m.then_inc(S["x_reduced"], 1)
                windows(pe, work)


        with ExitStack() as st:
            sb, ps, sem = tools(st)
            CH = 448
            NCH = GROUPS * HW // CH
            PER = HW // CH
            stats = sb("stats", NCH * 6)
            mv = sb("mv", 2)
            t = sb("t", 12)
            y = [sb(f"y{i}", HW) for i in range(2)]
            ps_s = [ps("ps_mean"), ps("ps_var")]
            loaded = [sem(f"conv_loaded{g}") for g in range(GROUPS)]
            dve_step, pe_step, act_step, activated, added = [sem(n) for n in (
                "bn_dve_step", "bn_pe_step", "bn_act_step", "activated", "added")]
            out_stored = [sem(f"out_stored{i}") for i in range(2)]
            block = st.enter_context(nc.Block())

            @block.sync
            def _(sp):
                for g in range(GROUPS):
                    sp.dma_start(X[:, g * HW:(g + 1) * HW],
                                 dram("conv", g * 128 * HW, [[HW, 128], [1, HW]])).then_inc(loaded[g], 16)
                for g in range(GROUPS):
                    sp.wait_ge(added, g + 1)
                    sp.dma_start(dram("out", g * 128 * HW, [[HW, 128], [1, HW]]), y[g % 2][:, :]).then_inc(out_stored[g % 2], 16)
                for i in range(2):
                    sp.wait_ge(out_stored[i], 32)

            @block.tensor
            def _(pe):
                pe.wait_ge(dve_step, 2)
                nc.tensor.matmul(ps_s[0][:, 0:1], same_channel[:, :], mv[:, 0:1], start=True, stop=True).then_inc(pe_step, 1)
                pe.wait_ge(dve_step, 5)
                nc.tensor.matmul(ps_s[1][:, 0:1], same_channel[:, :], t[:, 2:3], start=True, stop=True).then_inc(pe_step, 1)

            @block.scalar
            def _(act):
                act.wait_ge(dve_step, 6)
                nc.scalar.activation(t[:, 4:5], t[:, 3:4], ACT.Sqrt).then_inc(act_step, 1)
                act.wait_ge(dve_step, 12)
                for g in range(GROUPS):
                    wait(act, out_stored[g % 2], 16 * (g // 2))
                    nc.scalar.activation(y[g % 2][:, :], X[:, g * HW:(g + 1) * HW], ACT.Relu, scale=t[:, 8:9],
                                         bias=t[:, 10:11]).then_inc(activated, 1)

            @block.vector
            def _(dve):
                done = [0]

                def step(ins):
                    done[0] += 1
                    ins.then_inc(dve_step, 1)
                    dve.wait_ge(dve_step, done[0])

                for c in range(NCH):
                    if c % PER == 0:
                        dve.wait_ge(loaded[c // PER], 16)
                    last = nc.vector.bn_stats(stats[:, c * 6:(c + 1) * 6], X[:, c * CH:(c + 1) * CH])
                step(last)
                step(nc.vector.bn_aggr(mv[:, :], stats[:, :]))
                dve.wait_ge(pe_step, 1)
                step(nc.vector.tensor_scalar(t[:, 0:1], ps_s[0][:, 0:1], 1.0 / GB, None, ALU.mult))
                step(nc.vector.tensor_tensor(t[:, 1:2], mv[:, 0:1], t[:, 0:1], ALU.subtract))
                step(nc.vector.scalar_tensor_tensor(t[:, 2:3], t[:, 1:2], t[:, 1:2], mv[:, 1:2],
                                                    ALU.mult, ALU.add))
                dve.wait_ge(pe_step, 2)
                step(nc.vector.tensor_scalar(t[:, 3:4], ps_s[1][:, 0:1], 1.0 / GB, 1e-5, ALU.mult, ALU.add))
                dve.wait_ge(act_step, 1)
                step(nc.vector.reciprocal(t[:, 5:6], t[:, 4:5]))
                step(nc.vector.scalar_tensor_tensor(t[:, 6:7], t[:, 5:6], t[:, 3:4], t[:, 4:5],
                                                    ALU.mult, ALU.add))
                step(nc.vector.reciprocal(t[:, 7:8], t[:, 6:7]))
                step(nc.vector.tensor_scalar(t[:, 8:9], t[:, 7:8], 2.0, vecs[:, 1:2], ALU.mult, ALU.mult))
                step(nc.vector.tensor_tensor(t[:, 9:10], t[:, 0:1], t[:, 8:9], ALU.mult))
                step(nc.vector.tensor_tensor(t[:, 10:11], vecs[:, 2:3], t[:, 9:10], ALU.subtract))
                for g in range(GROUPS):
                    dve.wait_ge(activated, g + 1)
                    nc.vector.tensor_tensor(y[g % 2][:, :].rearrange("p (r w) -> p r w", w=W),
                                            y[g % 2][:, :].rearrange("p (r w) -> p r w", w=W),
                                            sub(XH, 0, 128, g * PADHW + PADW + 1, [[PADW, H], [1, W]]),
                                            ALU.add).then_inc(added, 1)


def shape_constants():
    import numpy as np
    f = np.float32
    p = np.arange(128)
    img, ch = p // C, p % C
    eye = np.eye(128, dtype=f)
    out = {"ident": eye, "same_image": (img[:, None] == img[None]).astype(f),
           "same_channel": (ch[:, None] == ch[None]).astype(f), "eps_eye": (1e-5 * eye).astype(f),
           "shrink": (0.9 + 0.1 * eye).astype(f)}
    grid = np.arange(W)[None, None, :] + (np.arange(KK) % 3 - 1)[:, None, None] + np.zeros((KK, H, W))
    out["grid"] = np.broadcast_to(grid.astype(f), (B, KK, H, W)).copy().reshape(128, DENSE)
    sel = np.zeros((128, 4, 128), f)
    col = np.arange(W)
    for i in range(2):
        for k in range(2):
            sel[KINDS * i + k, 0, 64 * i + col] = 1.0
            sel[KINDS * i + 2 + k, 0, 64 * i + col] = 1.0 - col
            sel[KINDS * i + k, 1, 64 * i + col] = -1.0
            sel[KINDS * i + 2 + k, 1, 64 * i + col] = 1.0 + col
            sel[KINDS * i + 4 + k, 2 + i, :] = 1.0
    out["sel"] = sel.reshape(128, 512)
    out["win_bias"] = -(WIN * np.arange(N_WIN)[None, :] - 60 + (p // C)[:, None]).astype(f)
    big = 3e38
    j = np.arange(N_WIN)
    start = WIN * j - 60
    hi = np.where(j > BASE_WIN, start - 1, big).astype(f)
    lo = np.where(j < BASE_WIN, start + WIN, -big).astype(f)
    out["bounds"] = np.broadcast_to(np.stack([hi, lo])[None], (PAIRS, 2, N_WIN)).copy().reshape(PAIRS, 2 * N_WIN)
    return out


def kernel(x, L0_conv_beta, L1_conv_w_off, L1_conv_b_off, L1_conv_w, L1_conv_b, L1_conv_gamma, L1_conv_beta):
    import numpy as np
    import concourse.bacc as bacc
    from concourse.bass_utils import run_bass_kernel_spmd
    f = np.float32
    arrays = shape_constants()
    arrays["x"] = np.ascontiguousarray(x)
    w_off, w = np.asarray(L1_conv_w_off), np.asarray(L1_conv_w)
    tile = lambda v: np.tile(np.asarray(v), GB)
    vecs = np.zeros((128, 4), f)
    for n, v in enumerate((L0_conv_beta, L1_conv_gamma, L1_conv_beta)):
        vecs[:, n] = tile(v)
    arrays["vecs"] = vecs
    woff = np.zeros((3, 2, C, 3, 3, 32), f)
    boff = np.zeros((3, 32), f)
    for i in range(2):
        for kind in range(3):
            woff[:, i, :, :, kind, KK * i:KK * (i + 1)] = w_off[kind * KK:(kind + 1) * KK].transpose(2, 1, 3, 0)
            boff[kind, KK * i:KK * (i + 1)] = np.asarray(L1_conv_b_off)[kind * KK:(kind + 1) * KK]
    arrays["woff"] = woff.reshape(3 * 2 * C, 3 * 96)
    arrays["boff"] = boff.reshape(96, 1)
    conv_w = np.zeros((WIN, C, KK, 32), f)
    conv_w[:, :, :, :O] = w.reshape(O, C, KK).transpose(1, 2, 0)[None]
    arrays["conv_w"] = conv_w.reshape(128, KK * 32)
    conv_b = np.zeros((4, 32), f)
    conv_b[:, :O] = np.asarray(L1_conv_b)[None]
    arrays["conv_b"] = conv_b.reshape(128, 1)

    nc = bacc.Bacc("TRN2", target_bir_lowering=False, num_devices=1)
    fp32 = mybir.dt.float32
    dr = {n: nc.dram_tensor(f"in_{n}", a.shape, fp32, kind="ExternalInput").ap() for n, a in arrays.items()}
    for name, size, dt in (("xt", B * W * XT_ROW, fp32), ("xh", B * C * PADHW, fp32), ("om", 3 * PLANE, fp32),
                           ("parts", KINDS * PLANE, fp32), ("row_max", PLANE // W, fp32), ("row_min", PLANE // W, fp32),
                           ("conv", B * O * HW, fp32), ("needed", 2 * N_UNITS * N_WIN, fp32)):
        dr[name] = nc.dram_tensor(f"scratch_{name}", (size,), dt, kind=KIND.get(name, "Internal")).ap()
    dr["out"] = nc.dram_tensor("out", (B, O, H, W), fp32, kind="ExternalOutput").ap()
    program(nc, dr)
    r = run_bass_kernel_spmd(nc, [{f"in_{n}": a for n, a in arrays.items()}], core_ids=[0])
    return r.results[0]["out"]
```

```python
import concourse.bass as bass
from concourse import mybir
from contextlib import ExitStack

B, C, H, W = 32, 16, 56, 56
O = 16
KK = 9
HW = H * W
M_ALL = B * HW
GROUPS = 4
GB = B // GROUPS
PADW = W + 2
PADHW = (H + 2) * PADW
PAIRS = B // 2
UNIT_ROWS = 4
UNITS = H // UNIT_ROWS
N_UNITS = PAIRS * UNITS
UPX = UNIT_ROWS * W
WIN = 8
N_WIN = 15
BASE_WIN = 7
STAGE_ROWS = UNIT_ROWS + 2 + WIN - 1
TOP = 64
NEAR = 2 * WIN
XT_ROWS = TOP + H + TOP
XT_ROW = XT_ROWS * C
PLANE = B * KK * HW
CONV_IMG = 2 * UNITS * 32 * UPX // 2
OM_IMG = 32 * HW
DENSE = PLANE // 128
DCH = 392
D_RING = 3
D_IT = DENSE // DCH // D_RING
NT = 10
KINDS = 6
TAPS_PX = KK * W



def program(nc, dr):
    fp32, f32r, i32 = mybir.dt.float32, mybir.dt.float32r, mybir.dt.int32
    ALU, ACT, AX = mybir.AluOpType, mybir.ActivationFunctionType, mybir.AxisListType

    def dram(name, offset, dims):
        return bass.AP(tensor=dr[name].tensor, offset=offset, ap=dims)

    def sub(tile, part, parts, offset, dims):
        pitch = tile[:].ap[0][0]
        return bass.AP(tensor=tile[:].tensor, offset=part * pitch + offset, ap=[[pitch, parts]] + dims)

    def peel(eng, count, body):
        body(0, False)
        with eng.Fori(1, count - 1) as it:
            body(it, False)
        body(count - 1, True)

    def wait(eng, sem, value):
        if not (isinstance(value, int) and value <= 0):
            eng.wait_ge(sem, value)

    outer = ExitStack()
    with outer:
        def tools(stack):
            def sb(name, cols, dt=fp32, parts=128):
                return stack.enter_context(nc.sbuf_tensor(name, [parts, cols], dt))

            def ps(name, banks=1):
                return stack.enter_context(nc.psum_tensor(name, [128, 512 * banks], fp32))

            def sem(name):
                return stack.enter_context(nc.semaphore(name))
            return sb, ps, sem

        sb, ps, sem = tools(outer)
        X = sb("X", GROUPS * HW)
        XH = sb("XH", GROUPS * PADHW)
        ident = sb("ident", 128)
        same_image = sb("same_image", 128)
        same_channel = sb("same_channel", 128)
        vecs = sb("vecs", 4)
        wm = sb("wm", 128)
        zeros = sb("zeros", XT_ROWS * C)

        with ExitStack() as st:
            sb, ps, sem = tools(st)
            CH = 448
            IT = GROUPS * HW // CH // 2
            eps_eye = sb("eps_eye", 128)
            shrink = sb("shrink", 128)
            xs4 = sb("xs4", GROUPS)
            small = sb("small", 8)
            flat = [sb(f"flat{i}", CH) for i in range(2)]
            pix = [sb(f"pix{i}", 512, parts=112) for i in range(2)]
            S1, S2, SN, Pm, P15, PP, PS = [sb(n, 128) for n in ("S1", "S2", "SN", "Pm", "P15", "PP", "PS")]
            sig = sb("sig", C)
            ps_pix = [ps(f"ps_pix{i}") for i in range(2)]
            ps_gram = ps("ps_gram")
            ps_a, ps_b, ps_c = ps("ps_a"), ps("ps_b"), ps("ps_c")
            consts_loaded = sem("consts_loaded")
            x_loaded = [sem(f"x_loaded{g}") for g in range(GROUPS)]
            dve_step, pe_step, act_step = sem("dve_step"), sem("pe_step"), sem("act_step")
            centred, staged, transposed, evacuated, grammed = [
                sem(n) for n in ("centred", "staged", "transposed", "evacuated", "grammed")]
            new_p, products, pp_ready, act_ready = [sem(n) for n in ("new_p", "products", "pp_ready", "act_ready")]
            zeroed = sem("zeroed")
            LOADS = ((ident, "ident"), (same_image, "same_image"), (same_channel, "same_channel"), (vecs, "vecs"),
                     (eps_eye, "eps_eye"), (shrink, "shrink"))
            block = st.enter_context(nc.Block())

            @block.sync
            def _(sp):
                for g in range(GROUPS):
                    sp.dma_start(X[:, g * HW:(g + 1) * HW],
                                 dram("x", g * 128 * HW, [[HW, 128], [1, HW]])).then_inc(x_loaded[g], 16)

            @block.gpsimd
            def _(pool):
                pool.memset(XH[:, :], 0.0).then_inc(zeroed, 1)
                pool.memset(zeros[:, :], 0.0).then_inc(zeroed, 1)
                pool.wait_ge(zeroed, 2)

            @block.scalar
            def _(act):
                for tile, name in LOADS:
                    n = tile[:].shape[1]
                    act.dma_start(tile[:, :], dram(name, 0, [[n, 128], [1, n]])).then_inc(consts_loaded, 16)
                act.wait_ge(centred, GROUPS)

                def stage(it, last):
                    for b in range(2):
                        c = 2 * it + b
                        wait(act, transposed, c - 1)
                        nc.scalar.copy(flat[b][:, :], sub(X, 0, 128, c * CH, [[1, CH]])).then_inc(staged, 1)
                peel(act, IT, stage)
                act.wait_ge(dve_step, 11)
                nc.scalar.activation(small[:, 4:5], small[:, 3:4], ACT.Sqrt).then_inc(act_step, 1)

                def newton(i, last):
                    act.wait_ge(new_p, i + 1)
                    nc.scalar.mul(P15[:, :], Pm[:, :], 1.5).then_inc(act_ready, 1)
                    act.wait_ge(products, 3 * i + 2)
                    nc.scalar.copy(PS[:, :], ps_b[:, 0:128]).then_inc(act_ready, 1)
                peel(act, NT, newton)

            @block.vector
            def _(dve):
                done = [0]

                def step(ins):
                    done[0] += 1
                    ins.then_inc(dve_step, 1)
                    dve.wait_ge(dve_step, done[0])

                for g in range(GROUPS):
                    dve.wait_ge(x_loaded[g], 16)
                    last = nc.vector.reduce_sum(xs4[:, g:g + 1], X[:, g * HW:(g + 1) * HW], axis=AX.X)
                step(last)
                step(nc.vector.reduce_sum(small[:, 0:1], xs4[:, :], axis=AX.X))
                dve.wait_ge(pe_step, 1)
                step(nc.vector.tensor_scalar(small[:, 1:2], ps_a[:, 0:1], 1.0 / M_ALL, None, ALU.mult))
                for g in range(GROUPS):
                    v = X[:, g * HW:(g + 1) * HW]
                    nc.vector.tensor_scalar(v, v, small[:, 1:2], None, ALU.subtract).then_inc(centred, 1)

                def evac(it, last):
                    for b in range(2):
                        c = 2 * it + b
                        dve.wait_ge(transposed, c + 1)
                        wait(dve, grammed, c - 1)
                        nc.vector.tensor_copy(pix[b][:, :], ps_pix[b][0:112, :]).then_inc(evacuated, 1)
                peel(dve, IT, evac)
                dve.wait_ge(grammed, 2 * IT)
                step(nc.vector.tensor_tensor(S1[:, :], ps_gram[:, 0:128], same_image[:, :], ALU.mult))
                dve.wait_ge(pe_step, 2)
                step(nc.vector.reduce_sum(sig[:, :], sub(ps_b, 0, 128, 0, [[1, C], [C, GB]]), axis=AX.X))
                step(nc.vector.tensor_tensor(S2[:, :].rearrange("p (b c) -> p b c", c=C),
                                             sub(sig, 0, 128, 0, [[0, GB], [1, C]]),
                                             same_image[:, :].rearrange("p (b c) -> p b c", c=C), ALU.mult))
                step(nc.vector.scalar_tensor_tensor(S1[:, :], S2[:, :], 1.0 / M_ALL, eps_eye[:, :],
                                                    ALU.mult, ALU.add))
                step(nc.vector.tensor_tensor(S2[:, :], S1[:, :], shrink[:, :], ALU.mult))
                step(nc.vector.tensor_tensor(S1[:, :], S2[:, :], ident[:, :], ALU.mult))
                step(nc.vector.reduce_sum(small[:, 2:3], S1[:, :], axis=AX.X))
                dve.wait_ge(pe_step, 3)
                step(nc.vector.reciprocal(small[:, 3:4], ps_c[:, 0:1]))
                step(nc.vector.tensor_scalar(SN[:, :], S2[:, :], small[:, 3:4], None, ALU.mult))
                dve.wait_ge(act_step, 1)
                step(nc.vector.reciprocal(small[:, 5:6], small[:, 4:5]))
                step(nc.vector.scalar_tensor_tensor(small[:, 6:7], small[:, 5:6], small[:, 3:4], small[:, 4:5],
                                                    ALU.mult, ALU.add))
                step(nc.vector.tensor_scalar(small[:, 7:8], small[:, 6:7], 0.5, None, ALU.mult))
                nc.vector.tensor_copy(Pm[:, :], ident[:, :]).then_inc(new_p, 1)

                def newton(i, last):
                    dve.wait_ge(products, 3 * i + 1)
                    nc.vector.tensor_copy(PP[:, :], ps_a[:, 0:128]).then_inc(pp_ready, 1)
                    dve.wait_ge(products, 3 * i + 3)
                    dve.wait_ge(act_ready, 2 * i + 1)
                    nc.vector.scalar_tensor_tensor(Pm[:, :], ps_c[:, 0:128], -0.5, P15[:, :],
                                                   ALU.mult, ALU.add).then_inc(new_p, 1)
                peel(dve, NT, newton)
                dve.wait_ge(new_p, NT + 1)
                step(nc.vector.tensor_scalar(wm[:, :], Pm[:, :], small[:, 7:8], None, ALU.mult))

            @block.tensor
            def _(pe):
                pe.wait_ge(consts_loaded, 16 * len(LOADS))
                pe.wait_ge(dve_step, 2)
                nc.tensor.matmul(ps_a[:, 0:1], same_channel[:, :], small[:, 0:1],
                                 start=True, stop=True).then_inc(pe_step, 1)

                def gram(it, last, first):
                    for b in range(2):
                        c = 2 * it + b
                        pe.wait_ge(staged, c + 1)
                        wait(pe, evacuated, c - 1)
                        for i in range(4):
                            t = nc.tensor.transpose(ps_pix[b][0:112, i * 128:(i + 1) * 128],
                                                    flat[b][:, i * 112:(i + 1) * 112], ident[:, :])
                        t.then_inc(transposed, 1)
                        pe.wait_ge(evacuated, c + 1)
                        for i in range(4):
                            m = nc.tensor.matmul(ps_gram[:, 0:128], pix[b][:, i * 128:(i + 1) * 128],
                                                 pix[b][:, i * 128:(i + 1) * 128],
                                                 start=(first and b == 0 and i == 0), stop=(last and b == 1 and i == 3))
                        m.then_inc(grammed, 1)
                peel(pe, IT, lambda it, last: gram(it, last, isinstance(it, int) and it == 0))
                pe.wait_ge(dve_step, 4)
                nc.tensor.matmul(ps_b[:, 0:128], same_channel[:, :], S1[:, :], start=True, stop=True).then_inc(pe_step, 1)
                pe.wait_ge(dve_step, 10)
                nc.tensor.matmul(ps_c[:, 0:1], same_image[:, :], small[:, 2:3], start=True, stop=True).then_inc(pe_step, 1)
                pe.wait_ge(dve_step, 12)

                def newton(i, last):
                    pe.wait_ge(new_p, i + 1)
                    nc.tensor.matmul(ps_a[:, 0:128], Pm[:, :], Pm[:, :], start=True, stop=True).then_inc(products, 1)
                    nc.tensor.matmul(ps_b[:, 0:128], Pm[:, :], SN[:, :], start=True, stop=True).then_inc(products, 1)
                    pe.wait_ge(pp_ready, i + 1)
                    pe.wait_ge(act_ready, 2 * i + 2)
                    nc.tensor.matmul(ps_c[:, 0:128], PP[:, :], PS[:, :], start=True, stop=True).then_inc(products, 1)
                peel(pe, NT, newton)

        with ExitStack() as st:
            sb, ps, sem = tools(st)
            ROWS = 8
            CH = ROWS * W
            IT = H // ROWS
            xst = [sb(f"xst{i}", CH + W) for i in range(2)]
            xts = [sb(f"xts{i}", GB * ROWS * C, parts=W) for i in range(2)]
            xts_hi = [sb(f"xts_hi{i}", GB // 2 * ROWS * C, f32r, parts=W) for i in range(2)]
            xts_lo = [sb(f"xts_lo{i}", GB // 2 * ROWS * C, f32r, parts=W) for i in range(2)]
            ps_w = [ps(f"ps_w{i}") for i in range(2)]
            ps_x = [ps(f"ps_x{i}", 2) for i in range(2)]
            padded, rounded, lowered = sem("padded"), sem("rounded"), sem("lowered")
            whitened, with_beta, kept, turned, sorted_, stored_pads, stored_xh = [
                sem(n) for n in ("whitened", "with_beta", "kept", "turned", "sorted", "stored_pads", "stored_xh")]
            stored_xt = [sem(f"stored_xt{i}") for i in range(2)]
            block = st.enter_context(nc.Block())

            def even(tile):
                return sub(tile, 0, W, 0, [[2 * ROWS * C, GB // 2], [1, ROWS * C]])

            def halves(tile):
                return sub(tile, 0, W, 0, [[ROWS * C, GB // 2], [1, ROWS * C]])

            @block.tensor
            def _(pe):
                pe.wait_ge(padded, 2)

                def lead(c, g, yb):
                    wait(pe, with_beta, c - 1)
                    nc.tensor.matmul(ps_w[g % 2][:, 0:CH], wm[:, :], sub(X, 0, 128, g * HW + yb * CH, [[1, CH]]),
                                     start=True, stop=True).then_inc(whitened, 1)

                def body(yb, last):
                    for g in range(GROUPS):
                        c = yb * GROUPS + g
                        lead(c, g, yb)
                        pe.wait_ge(with_beta, c + 1)
                        wait(pe, sorted_, c - 1)
                        for r in range(ROWS):
                            t = nc.tensor.transpose(ps_x[g % 2][0:2 * W, r * 128:(r + 1) * 128],
                                                    xst[g % 2][:, r * W:(r + 2) * W], ident[:, :])
                        t.then_inc(turned, 1)
                peel(pe, IT, body)

            @block.scalar
            def _(act):
                def body(yb, last):
                    for g in range(GROUPS):
                        c = yb * GROUPS + g
                        act.wait_ge(whitened, c + 1)
                        wait(act, turned, c - 1)
                        wait(act, kept, c - 1)
                        nc.scalar.activation(xst[g % 2][:, 0:CH], ps_w[g % 2][:, 0:CH], ACT.Identity,
                                             bias=vecs[:, 0:1]).then_inc(with_beta, 1)
                        act.wait_ge(sorted_, c + 1)
                        wait(act, stored_xt[g % 2], 48 * (yb * 2 + g // 2))
                        nc.scalar.copy(halves(xts_hi[g % 2]), even(xts[g % 2])).then_inc(rounded, 1)
                peel(act, IT, body)

            @block.gpsimd
            def _(pool):
                for i in range(2):
                    pool.memset(xst[i][:, CH:CH + W], 0.0).then_inc(padded, 1)

                def body(yb, last):
                    for g in range(GROUPS):
                        pool.wait_ge(with_beta, yb * GROUPS + g + 1)
                        pool.tensor_copy(sub(XH, 0, 128, g * PADHW + (yb * ROWS + 1) * PADW + 1, [[PADW, ROWS], [1, W]]),
                                         xst[g % 2][:, 0:CH].rearrange("p (r w) -> p r w", w=W)).then_inc(kept, 1)
                        pool.wait_ge(rounded, yb * GROUPS + g + 1)
                        wait(pool, stored_xt[g % 2], 48 * (yb * 2 + g // 2))
                        pool.tensor_tensor(halves(xts_lo[g % 2]), even(xts[g % 2]), halves(xts_hi[g % 2]).bitcast(fp32),
                                           ALU.subtract).then_inc(lowered, 1)
                peel(pool, IT, body)

            @block.vector
            def _(dve):
                def body(yb, last):
                    for g in range(GROUPS):
                        c = yb * GROUPS + g
                        dve.wait_ge(turned, c + 1)
                        wait(dve, stored_xt[g % 2], 48 * (yb * 2 + g // 2))
                        for h in range(2):
                            e = nc.vector.tensor_copy(
                                sub(xts[g % 2], 0, W, h * 4 * C, [[ROWS * C, GB], [C, 4], [1, C]]),
                                sub(ps_x[g % 2], 0, W, h * 512, [[C, GB], [128, 4], [1, C]]))
                        e.then_inc(sorted_, 1)
                peel(dve, IT, body)

            @block.sync
            def _(sp):
                for first in (TOP - NEAR, TOP + H):
                    sp.dma_start(dram("xt", first * C, [[XT_ROW, W], [W * XT_ROW, B], [1, NEAR * C]]),
                                 sub(zeros, 0, W, 0, [[0, B], [1, NEAR * C]])).then_inc(stored_pads, 16)
                for first in (TOP - WIN, TOP + H):
                    for name in ("xt_hi", "xt_lo"):
                        sp.dma_start(dram(name, first * C, [[XT_ROW, W], [W * XT_ROW, PAIRS], [1, WIN * C]]),
                                     sub(zeros, 0, W, 0, [[0, PAIRS], [1, WIN * C]])).then_inc(stored_pads, 16)

                for row in (0, H + 1):
                    sp.dma_start(dram("xh", row * PADW, [[PADHW, 128], [128 * PADHW, GROUPS], [1, PADW]]),
                                 sub(XH, 0, 128, row * PADW, [[PADHW, GROUPS], [1, PADW]])).then_inc(stored_xh, 16)

                def body(yb, last):
                    for g in range(GROUPS):
                        sp.wait_ge(sorted_, yb * GROUPS + g + 1)
                        sp.dma_start(dram("xt", g * GB * W * XT_ROW + (TOP + yb * ROWS) * C,
                                          [[XT_ROW, W], [W * XT_ROW, GB], [1, ROWS * C]]),
                                     sub(xts[g % 2], 0, W, 0, [[ROWS * C, GB], [1, ROWS * C]])).then_inc(stored_xt[g % 2], 16)
                        for name, tile, ready in (("xt_hi", xts_hi[g % 2], rounded), ("xt_lo", xts_lo[g % 2], lowered)):
                            sp.wait_ge(ready, yb * GROUPS + g + 1)
                            sp.dma_start(dram(name, g * GB // 2 * W * XT_ROW + (TOP + yb * ROWS) * C,
                                              [[XT_ROW, W], [W * XT_ROW, GB // 2], [1, ROWS * C]]),
                                         sub(tile, 0, W, 0, [[ROWS * C, GB // 2], [1, ROWS * C]]).bitcast(fp32)
                                         ).then_inc(stored_xt[g % 2], 16)
                        sp.wait_ge(kept, yb * GROUPS + g + 1)
                        sp.dma_start(dram("xh", g * 128 * PADHW + (yb * ROWS + 1) * PADW, [[PADHW, 128], [1, ROWS * PADW]]),
                                     sub(XH, 0, 128, g * PADHW + (yb * ROWS + 1) * PADW, [[1, ROWS * PADW]])
                                     ).then_inc(stored_xh, 16)
                peel(sp, IT, body)
                sp.wait_ge(stored_xh, 16 * (IT * GROUPS + 2))
                sp.wait_ge(stored_pads, 96)
                for i in range(2):
                    sp.wait_ge(stored_xt[i], 48 * IT * 2)

        with ExitStack() as st:
            sb, ps, sem = tools(st)
            ROWS = 7
            CH = ROWS * W
            HALF = H // 2
            NCH = HALF // ROWS
            SHIFTS = 3 * 2 * C
            woff = sb("woff", 3 * 2 * 32)
            boff = sb("boff", 1)
            x3 = [sb(f"x3{i}", H * PADW) for i in range(2)]
            om = [sb(f"om{i}", HALF * W) for i in range(2)]
            ps_o = [ps(f"ps_o{i}") for i in range(2)]
            w_loaded, convolved, biased, x3_padded = [sem(n) for n in ("w_loaded", "convolved", "biased", "x3_padded")]
            x3_loaded = [sem(f"x3_loaded{i}") for i in range(2)]
            om_stored = [sem(f"om_stored{i}") for i in range(2)]
            block = st.enter_context(nc.Block())

            @block.sync
            def _(sp):
                sp.dma_start(woff[:, :], dram("woff", 0, [[3 * 2 * 32, 128], [1, 3 * 2 * 32]])).then_inc(w_loaded, 16)
                sp.dma_start(boff[:, :], dram("boff", 0, [[1, 128], [1, 1]])).then_inc(w_loaded, 16)

                def body(it, last):
                    for b in range(2):
                        pair = 2 * it + b
                        wait(sp, convolved, (pair - 1) * NCH)
                        for dy in range(3):
                            sp.dma_start(sub(x3[b], dy * 2 * C, 2 * C, 0, [[1, H * PADW]]),
                                         dram("xh", pair * 2 * C * PADHW + dy * PADW,
                                              [[PADHW, 2 * C], [1, H * PADW]])).then_inc(x3_loaded[b], 16)
                peel(sp, PAIRS // 2, body)

            @block.vector
            def _(dve):
                for b in range(2):
                    dve.memset(x3[b][SHIFTS:128, :], 0.0).then_inc(x3_padded, 1)

            @block.tensor
            def _(pe):
                pe.wait_ge(w_loaded, 32)
                pe.wait_ge(x3_padded, 2)

                def body(it, last):
                    for b in range(2):
                        pair = 2 * it + b
                        pe.wait_ge(x3_loaded[b], 48 * (it + 1))
                        for ch in range(NCH):
                            n = pair * NCH + ch
                            wait(pe, biased, n - 1)
                            for kx in range(3):
                                for j in range(4):
                                    i, h = j // 2, j % 2
                                    m = nc.tensor.matmul(ps_o[ch % 2][32 * j:32 * j + 32, 0:CH],
                                                         woff[:, (2 * kx + i) * 32:(2 * kx + i + 1) * 32],
                                                         sub(x3[b], 0, 128, (h * HALF + ch * ROWS) * PADW + kx,
                                                             [[PADW, ROWS], [1, W]]),
                                                         start=(kx == 0), stop=(kx == 2))
                            m.then_inc(convolved, 1)
                peel(pe, PAIRS // 2, body)

            @block.scalar
            def _(act):
                act.wait_ge(w_loaded, 32)

                def body(it, last):
                    for b in range(2):
                        pair = 2 * it + b
                        wait(act, om_stored[b], 64 * it)
                        for ch in range(NCH):
                            n = pair * NCH + ch
                            act.wait_ge(convolved, n + 1)
                            nc.scalar.activation(om[b][:, ch * CH:(ch + 1) * CH], ps_o[ch % 2][:, 0:CH],
                                                 ACT.Identity, bias=boff[:, 0:1]).then_inc(biased, 1)
                        act.wait_ge(biased, (pair + 1) * NCH)
                        for j in range(4):
                            i, h = j // 2, j % 2
                            act.dma_start(dram("om", (pair * 2 + i) * OM_IMG + h * HALF * W, [[HW, 32], [1, HALF * W]]),
                                          sub(om[b], 32 * j, 32, 0, [[1, HALF * W]])).then_inc(om_stored[b], 16)
                peel(act, PAIRS // 2, body)
                for b in range(2):
                    act.wait_ge(om_stored[b], 64 * PAIRS // 2)

        with ExitStack() as st:
            sb, ps, sem = tools(st)
            RPC = DCH // W
            val = [sb(f"val{i}", 3 * DCH) for i in range(D_RING)]
            px = [sb(f"px{i}", DCH) for i in range(D_RING)]
            logit = [sb(f"logit{i}", DCH) for i in range(D_RING)]
            column, tap_shift = sb("column", W), sb("tap_shift", D_RING * D_IT)
            grid_loaded = sem("grid_loaded")
            parts = [sb(f"parts{i}", KINDS * DCH, f32r) for i in range(D_RING)]
            row_max, row_min = sb("row_max", DENSE // W), sb("row_min", DENSE // W)
            loaded = [sem(f"loaded{i}") for i in range(D_RING)]
            stored = [sem(f"stored{i}") for i in range(D_RING)]
            masked, summed, ranged, scaled, high, low, ranges_stored = [sem(n) for n in (
                "masked", "summed", "ranged", "scaled", "high", "low", "ranges_stored")]
            block = st.enter_context(nc.Block())

            def part(b, k):
                return sub(parts[b], 0, 128, k * DCH, [[2 * DCH, 3], [1, DCH]])

            def three(tile):
                return sub(tile, 0, 128, 0, [[DCH, 3], [1, DCH]])

            def overlapped(eng, lead, tail):
                lead(0, 0)

                def body(it, last):
                    for b in range(D_RING):
                        wrap = b == D_RING - 1
                        if not (last and wrap):
                            lead(it + (1 if wrap else 0), 0 if wrap else b + 1)
                        tail(it, b)
                peel(eng, D_IT, body)

            @block.sync
            def _(sp):
                def lead(it, b):
                    n = D_RING * it + b
                    wait(sp, low, n - D_RING + 1)
                    for tile, off, kind in ((logit[b], 0, 2), (px[b], 0, 1), (val[b], 2 * DCH, 0)):
                        sp.dma_start(sub(tile, 0, 128, off, [[1, DCH]]),
                                     dram("om", kind * KK * HW + n * DCH, [[OM_IMG, B], [DENSE, 128 // B], [1, DCH]])
                                     ).then_inc(loaded[b], 16)

                sp.dma_start(column[:, :], dram("column", 0, [[W, 128], [1, W]])).then_inc(grid_loaded, 16)
                sp.dma_start(tap_shift[:, :], dram("tap_shift", 0, [[D_RING * D_IT, 128], [1, D_RING * D_IT]])
                             ).then_inc(grid_loaded, 16)

                def body(it, last):
                    for b in range(D_RING):
                        lead(it, b)
                peel(sp, D_IT, body)
                sp.wait_ge(ranged, D_RING * D_IT)
                for tile, name in ((row_max, "row_max"), (row_min, "row_min")):
                    sp.dma_start(dram(name, 0, [[DENSE // W, 128], [1, DENSE // W]]), tile[:, :]).then_inc(ranges_stored, 16)
                for b in range(D_RING):
                    sp.wait_ge(stored[b], 16 * D_IT)
                sp.wait_ge(ranges_stored, 32)

            @block.scalar
            def _(act):
                def lead(it, b):
                    n = D_RING * it + b
                    act.wait_ge(loaded[b], 48 * (it + 1))
                    nc.scalar.activation(sub(val[b], 0, 128, DCH, [[1, DCH]]), logit[b][:, :], ACT.Sigmoid).then_inc(masked, 1)

                def store(it, b):
                    n = D_RING * it + b
                    act.wait_ge(low, n + 1)
                    act.dma_start(dram("parts", n * DCH, [[DENSE, 128], [PLANE, KINDS], [1, DCH]]),
                                  sub(parts[b], 0, 128, 0, [[DCH, KINDS], [1, DCH]]).bitcast(fp32)).then_inc(stored[b], 16)

                def tail(it, b):
                    n = D_RING * it + b
                    act.wait_ge(scaled, n + 1)
                    wait(act, stored[b], 16 * it)
                    nc.scalar.copy(part(b, 0), three(val[b])).then_inc(high, 1)
                    if b or not (isinstance(it, int) and it == 0):
                        store(it if b else it - 1, (b - 1) % D_RING)
                overlapped(act, lead, tail)
                store(D_IT - 1, D_RING - 1)

            @block.gpsimd
            def _(pool):
                def body(it, last):
                    for b in range(D_RING):
                        n = D_RING * it + b
                        pool.wait_ge(high, n + 1)
                        pool.tensor_tensor(part(b, 1), three(val[b]), part(b, 0).bitcast(fp32), ALU.subtract).then_inc(low, 1)
                peel(pool, D_IT, body)

            @block.vector
            def _(dve):
                dve.wait_ge(grid_loaded, 32)

                def body(it, last):
                    for b in range(D_RING):
                        n = D_RING * it + b
                        dve.wait_ge(loaded[b], 48 * (it + 1))
                        nc.vector.scalar_tensor_tensor(sub(px[b], 0, 128, 0, [[W, RPC], [1, W]]),
                                                       sub(px[b], 0, 128, 0, [[W, RPC], [1, W]]),
                                                       sub(tap_shift, 0, 128, n, [[1, 1]]),
                                                       sub(column, 0, 128, 0, [[0, RPC], [1, W]]),
                                                       ALU.add, ALU.add).then_inc(summed, 1)
                        oy = sub(val[b], 0, 128, 2 * DCH, [[W, RPC], [1, W]])
                        nc.vector.tensor_reduce(sub(row_max, 0, 128, n * RPC, [[1, RPC]]), oy, axis=AX.X, op=ALU.max)
                        nc.vector.tensor_reduce(sub(row_min, 0, 128, n * RPC, [[1, RPC]]), oy, axis=AX.X,
                                                op=ALU.min).then_inc(ranged, 1)
                        dve.wait_ge(summed, n + 1)
                        dve.wait_ge(masked, n + 1)
                        nc.vector.tensor_tensor(sub(val[b], 0, 128, 0, [[1, DCH]]), sub(val[b], 0, 128, DCH, [[1, DCH]]),
                                                px[b][:, :], ALU.mult).then_inc(scaled, 1)
                peel(dve, D_IT, body)

        def conv_halves(tile, pair, u):
            for i in range(2):
                yield (dram("conv", (pair * 2 + i) * CONV_IMG + u * 2 * 32 * UPX // 2, [[UPX // 2, 64], [1, UPX // 2]]),
                       sub(tile, 64 * i, 64, 0, [[1, UPX // 2]]))

        with ExitStack() as st:
            sb, ps, sem = tools(st)
            ROW = TAPS_PX
            sel32 = sb("sel32", 4 * 128)
            sel = sb("sel", 4 * 128, f32r)
            sel_plus, sel_minus, sel_y = sel[:, 0:128], sel[:, 128:256], [sel[:, 256:384], sel[:, 384:512]]
            win_bias = sb("win_bias", N_WIN)
            conv_w = sb("conv_w", KK * 32)
            conv_b = sb("conv_b", 1)
            stage = [sb(f"stage{b}", STAGE_ROWS * C) for b in range(2)]
            stage_hi = [sb(f"stage_hi{b}", STAGE_ROWS * C, f32r) for b in range(2)]
            stage_lo = [sb(f"stage_lo{b}", STAGE_ROWS * C, f32r) for b in range(2)]
            rows = [sb(f"rows{b}", KK * UPX, f32r) for b in range(2)]
            plus = [sb(f"plus{b}", ROW) for b in range(2)]
            tent_x = [sb(f"tent_x{q}", ROW) for q in range(UNIT_ROWS)]
            tent_a = [sb(f"tent_a{q}", ROW, f32r) for q in range(UNIT_ROWS)]
            tent_rest = [sb(f"tent_rest{b}", ROW, parts=64) for b in range(2)]
            dist_y = [sb(f"dist_y{b}", 2 * ROW) for b in range(2)]
            G = [sb(f"G{b}", 2 * UNIT_ROWS * ROW) for b in range(2)]
            res = [sb(f"res{b}", UPX // 2) for b in range(2)]
            ps_p, ps_m = ps("ps_p"), ps("ps_m")
            ps_y, ps_v = ps("ps_y", 2), ps("ps_v", 2)
            ps_r = [ps(f"ps_r{b}") for b in range(2)]
            consts_loaded, cleared, cast = sem("dcn_consts_loaded"), sem("cleared"), sem("cast")
            stage_loaded = [sem(f"stage_loaded{b}") for b in range(2)]
            rows_loaded = [sem(f"rows_loaded{b}") for b in range(2)]
            x_spread, y_spread, plus_ready, tent_ready, dist_ready, dist_capped, sampled, weighted, reduced, res_ready = [
                sem(n) for n in ("x_spread", "y_spread", "plus_ready", "tent_ready", "dist_ready", "dist_capped",
                                 "sampled", "weighted", "reduced", "res_ready")]
            res_stored = [sem(f"res_stored{b}") for b in range(2)]
            tent_rounded, rest_ready, rest_moved = sem("tent_rounded"), sem("rest_ready"), sem("rest_moved")
            LOADS_PER_UNIT = 5
            LOADS = ((sel32, "sel"), (win_bias, "win_bias"), (conv_w, "conv_w"), (conv_b, "conv_b"))
            IT = N_UNITS // 2
            block = st.enter_context(nc.Block())

            def place(eng, it, b):
                pair, u = it // (UNITS // 2), (it % (UNITS // 2)) * 2 + b
                return (pair, u) if isinstance(it, int) else (eng.snap(pair), eng.snap(u))

            def load_unit(eng, b, pair, u):
                row = (TOP - 1 + u * UNIT_ROWS + WIN * BASE_WIN - 60) * C
                eng.dma_start(sub(stage[b], 64, W, 0, [[1, STAGE_ROWS * C]]),
                              dram("xt", (pair * 2 + 1) * W * XT_ROW + row,
                                   [[XT_ROW, W], [1, STAGE_ROWS * C]])).then_inc(stage_loaded[b], 16)
                for tile, name in ((stage_hi[b], "xt_hi"), (stage_lo[b], "xt_lo")):
                    for half in range(2):
                        eng.dma_start(sub(tile, 64 * half, W, 0, [[1, STAGE_ROWS * C]]).bitcast(fp32),
                                      dram(name, pair * W * XT_ROW + row,
                                           [[XT_ROW, W], [1, STAGE_ROWS * C]])).then_inc(stage_loaded[b], 16)

            def load_rows(eng, b, pair, u):
                for i in range(2):
                    eng.dma_start(sub(rows[b], KINDS * i, KINDS, 0, [[UPX, KK], [1, UPX]]).bitcast(fp32),
                                  dram("parts", (pair * 2 + i) * KK * HW + u * UPX,
                                       [[PLANE, KINDS], [HW, KK], [1, UPX]])).then_inc(rows_loaded[b], 16)

            def taps(b, q):
                return sub(rows[b], 0, 128, q * W, [[UPX, KK], [1, W]])

            @block.sync
            def _(sp):
                sp.wait_ge(cleared, 8)

                def body(it, last):
                    for b in range(2):
                        n = 2 * it + b
                        pair, u = place(sp, it, b)
                        wait(sp, y_spread, UNIT_ROWS * (n - 1))
                        load_rows(sp, b, pair, u)
                        wait(sp, sampled, 2 * UNIT_ROWS * (n - 1))
                        load_unit(sp, b, pair, u)
                peel(sp, IT, body)

            def stream(eng, ops, later=()):
                def run(it, b, q, last):
                    for ahead, op in ops:
                        row = b * UNIT_ROWS + q + ahead
                        more, row = row // (2 * UNIT_ROWS), row % (2 * UNIT_ROWS)
                        if not (last and more) and not (it is None and not more):
                            op(0 if it is None else it + more if more else it, row // UNIT_ROWS, row % UNIT_ROWS)

                first = max(ahead for ahead, op in ops)
                for q in range(UNIT_ROWS - first, UNIT_ROWS):
                    run(None, 1, q, False)

                def body(it, last):
                    for b in range(2):
                        for q in range(UNIT_ROWS):
                            run(it, b, q, last)
                            for units, steps, op in later:
                                if q in steps and not (isinstance(it, int) and 2 * it + b < units):
                                    op(it + (b - units) // 2, (b - units) % 2, q)
                peel(eng, IT, body)
                for b in range(2):
                    for q in range(UNIT_ROWS):
                        for units, steps, op in later:
                            if q in steps and b < units:
                                op(IT + (b - units) // 2, (b - units) % 2, q)

            @block.gpsimd
            def _(pool):
                for b in range(2):
                    for tile in (stage[b][:, :], stage_hi[b][:, :].bitcast(fp32), stage_lo[b][:, :].bitcast(fp32),
                                 rows[b][:, :].bitcast(fp32)):
                        pool.memset(tile, 0.0).then_inc(cleared, 1)

                def rest(it, b, q):
                    r = (2 * it + b) * UNIT_ROWS + q
                    pool.wait_ge(tent_rounded, r + 1)
                    wait(pool, rest_moved, r - 1)
                    pool.tensor_tensor(tent_rest[q % 2][:, :], tent_x[q][0:64, :], tent_a[q][0:64, :].bitcast(fp32),
                                       ALU.subtract).then_inc(rest_ready, 1)
                stream(pool, [(2, rest)])

            @block.tensor
            def _(pe):
                pe.wait_ge(cast, 1)
                pe.wait_ge(consts_loaded, 16 * len(LOADS))

                def spread_x(it, b, q):
                    r = (2 * it + b) * UNIT_ROWS + q
                    if q == 0:
                        pe.wait_ge(rows_loaded[b], 32 * (it + 1))
                    wait(pe, plus_ready, r)
                    nc.tensor.matmul(ps_p[:, 0:ROW], sel_plus, taps(b, q), start=True, stop=True)
                    wait(pe, tent_ready, r)
                    nc.tensor.matmul(ps_m[:, 0:ROW], sel_minus, taps(b, q), start=True, stop=True).then_inc(x_spread, 1)

                def spread_y(it, b, q):
                    r = (2 * it + b) * UNIT_ROWS + q
                    wait(pe, dist_ready, r)
                    for i in range(2):
                        m = nc.tensor.matmul(ps_y[:, i * 512:i * 512 + ROW], sel_y[i], taps(b, q), start=True, stop=True)
                    m.then_inc(y_spread, 1)

                def columns(q, i, passes):
                    for ky in range(3):
                        for n, (image, tent) in enumerate(passes):
                            m = nc.tensor.matmul(ps_v[:, i * 512 + ky * 3 * W:i * 512 + (ky + 1) * 3 * W],
                                                 image[:, (q + ky) * C:(q + ky + WIN) * C],
                                                 tent[:, ky * 3 * W:(ky + 1) * 3 * W],
                                                 start=(n == 0), stop=(n == len(passes) - 1))
                    m.then_inc(sampled, 1)

                def columns_b(it, b, q):
                    r = (2 * it + b) * UNIT_ROWS + q
                    if q == 0:
                        pe.wait_ge(stage_loaded[b], 16 * LOADS_PER_UNIT * (it + 1))
                    pe.wait_ge(tent_ready, r + 1)
                    wait(pe, weighted, 2 * r - 1)
                    columns(q, 1, [(stage[b], tent_x[q])])

                def columns_a(it, b, q):
                    r = (2 * it + b) * UNIT_ROWS + q
                    pe.wait_ge(rest_moved, r + 1)
                    wait(pe, weighted, 2 * r)
                    columns(q, 0, [(stage_hi[b], tent_a[q]), (stage_lo[b], tent_a[q])])

                def taps_and_channels(it, b, q):
                    n = 2 * it + b
                    if q == 0:
                        pe.wait_ge(weighted, 2 * UNIT_ROWS * (n + 1))
                        wait(pe, res_ready, n - 1)
                    for k in range(KK * q // UNIT_ROWS, KK * (q + 1) // UNIT_ROWS):
                        for j in range(4):
                            i, h = j // 2, j % 2
                            m = nc.tensor.matmul(ps_r[b][32 * j:32 * j + 32, 0:UPX // 2], conv_w[:, k * 32:(k + 1) * 32],
                                                 sub(G[b], 0, 128, (i * UNIT_ROWS + 2 * h) * ROW + k * W, [[ROW, 2], [1, W]]),
                                                 start=(k == 0), stop=(k == KK - 1))
                    if q == UNIT_ROWS - 1:
                        m.then_inc(reduced, 1)
                stream(pe, [(1, spread_y), (0, columns_b), (3, spread_x), (0, columns_a)],
                       [(1, range(UNIT_ROWS), taps_and_channels)])

            @block.scalar
            def _(act):
                for tile, name in LOADS:
                    n = tile[:].shape[1]
                    act.dma_start(tile[:, :], dram(name, 0, [[n, 128], [1, n]])).then_inc(consts_loaded, 16)
                act.wait_ge(consts_loaded, 16 * len(LOADS))
                nc.scalar.copy(sel[:, :], sel32[:, :]).then_inc(cast, 1)

                def relu(it, b, q):
                    r = (2 * it + b) * UNIT_ROWS + q
                    act.wait_ge(x_spread, r + 1)
                    wait(act, tent_ready, r - 1)
                    nc.scalar.activation(plus[q % 2][:, :], ps_p[:, 0:ROW], ACT.Relu).then_inc(plus_ready, 1)

                def distance(it, b, q):
                    r = (2 * it + b) * UNIT_ROWS + q
                    act.wait_ge(y_spread, r + 1)
                    wait(act, weighted, 2 * (r - 1))
                    nc.scalar.activation(sub(dist_y[q % 2], 0, 128, 0, [[ROW, 2], [1, ROW]]),
                                         sub(ps_y, 0, 128, 0, [[512, 2], [1, ROW]]), ACT.Abs,
                                         bias=win_bias[:, BASE_WIN:BASE_WIN + 1]).then_inc(dist_ready, 1)

                def rounding(it, b, q):
                    r = (2 * it + b) * UNIT_ROWS + q
                    act.wait_ge(tent_ready, r + 1)
                    wait(act, sampled, 2 * (r - 3))
                    nc.scalar.copy(tent_a[q][0:64, :], tent_x[q][0:64, :]).then_inc(tent_rounded, 1)

                def store(it, b, q):
                    pair, u = place(act, it, b)
                    act.wait_ge(res_ready, 2 * it + b + 1)
                    for there, here in conv_halves(res[b], pair, u):
                        act.dma_start(there, here).then_inc(res_stored[b], 16)

                def result(it, b, q):
                    n = 2 * it + b
                    act.wait_ge(reduced, n + 1)
                    wait(act, res_stored[b], 32 * it)
                    nc.scalar.activation(res[b][:, :], ps_r[b][:, 0:UPX // 2], ACT.Identity, scale=-1.0,
                                         bias=conv_b[:, 0:1]).then_inc(res_ready, 1)
                stream(act, [(1, distance), (2, rounding), (3, relu)],
                       [(2, (0,), result), (2, (2,), store)])
                for b in range(2):
                    act.wait_ge(res_stored[b], 32 * IT)

            @block.vector
            def _(dve):
                def tent(it, b, q):
                    r = (2 * it + b) * UNIT_ROWS + q
                    dve.wait_ge(x_spread, r + 1)
                    dve.wait_ge(plus_ready, r + 1)
                    wait(dve, sampled, 2 * (r - 3))
                    nc.vector.scalar_tensor_tensor(tent_x[q][:, :], ps_m[:, 0:ROW], 0.0, plus[q % 2][:, :],
                                                   ALU.max, ALU.min).then_inc(tent_ready, 1)

                def move(it, b, q):
                    r = (2 * it + b) * UNIT_ROWS + q
                    dve.wait_ge(rest_ready, r + 1)
                    wait(dve, sampled, 2 * (r - 3))
                    nc.vector.tensor_copy(tent_a[q][64:128, :], tent_rest[q % 2][:, :]).then_inc(rest_moved, 1)

                def cap(it, b, q):
                    r = (2 * it + b) * UNIT_ROWS + q
                    dve.wait_ge(dist_ready, r + 1)
                    nc.vector.tensor_scalar(dist_y[q % 2][:, :], dist_y[q % 2][:, :], 1.0, 1.0,
                                            ALU.min, ALU.subtract).then_inc(dist_capped, 1)

                def weight(it, b, q):
                    r = (2 * it + b) * UNIT_ROWS + q
                    if q == 0:
                        wait(dve, reduced, 2 * it + b - 1)
                    dve.wait_ge(dist_capped, r + 1)
                    for n, i in enumerate((1, 0)):
                        dve.wait_ge(sampled, 2 * r + 1 + n)
                        nc.vector.tensor_tensor(
                            sub(G[b], 0, 128, (i * UNIT_ROWS + q) * ROW, [[1, ROW]]),
                            sub(dist_y[q % 2], 0, 128, i * ROW, [[1, ROW]]),
                            sub(ps_v, 0, 128, i * 512, [[1, ROW]]), ALU.mult).then_inc(weighted, 1)
                stream(dve, [(2, tent), (0, cap), (1, move), (0, weight)])

        with ExitStack() as st:
            sb, ps, sem = tools(st)
            ROW = TAPS_PX
            TABLE = N_UNITS * N_WIN
            PU = UNITS * N_WIN
            ranges = sb("ranges", 2 * 2 * KK * H, parts=PAIRS)
            unit_range = sb("unit_range", 2 * UNITS, parts=PAIRS)
            bounds = sb("bounds", 2 * N_WIN, parts=PAIRS)
            need = sb("need", 2 * PU, parts=PAIRS)
            needed, ordinal, numbered = (X[0:1, k * TABLE:(k + 1) * TABLE] for k in range(3))
            by_unit = sb("by_unit", N_UNITS, parts=1)
            by_pair = sb("by_pair", PAIRS, parts=1)
            turn_of = sb("turn_of", TABLE, i32, parts=1)
            any_unit = sb("any_unit", N_UNITS, i32, parts=1)
            any_pair = sb("any_pair", PAIRS, i32, parts=1)
            far_count = sb("far_count", 3, parts=1)
            any_far = sb("any_far", 1, i32, parts=1)
            xsel32 = sb("xsel32", 4 * 128)
            xsel = sb("xsel", 4 * 128, f32r)
            xwin_bias = sb("xwin_bias", N_WIN)
            xconv_w = sb("xconv_w", KK * 32)
            xstage = [sb(f"xstage{i}", STAGE_ROWS * C) for i in range(2)]
            xrows = sb("xrows", KK * UPX, f32r)
            xplus, xtent = sb("xplus", ROW), sb("xtent", ROW)
            xdist = sb("xdist", 2 * ROW)
            xG = sb("xG", 2 * UNIT_ROWS * ROW)
            before, added_to = sb("before", UPX // 2), sb("added_to", UPX // 2)
            xps_p, xps_m, xps_r = ps("xps_p"), ps("xps_m"), ps("xps_r")
            xps_y, xps_v = ps("xps_y", 2), ps("xps_v", 2)
            names = ("x_consts", "x_cleared", "x_cast", "x_ranges", "x_step", "x_need_stored", "x_need_loaded", "x_tables",
                     "x_pads", "x_loaded", "x_before", "x_reduced", "x_added", "x_stored", "x_turn")
            S = {n: sem(n) for n in names}
            Q = {n: [sem(f"{n}_row{q}") for q in range(UNIT_ROWS)] for n in (
                "x_spreads", "x_plus_ready", "x_tent_ready", "x_dist_ready", "x_capped", "x_sampled", "x_weighted")}
            block = st.enter_context(nc.Block())

            def windows(eng, work):
                eng.wait_ge(S["x_tables"], 4)
                with eng.Fori(0, PAIRS) as pair:
                    some = eng.value_load(any_pair[0:1, bass.ds(pair, 1)], min_val=0, max_val=1)
                    with eng.If(some > 0):
                        with eng.Fori(0, UNITS) as u:
                            some_u = eng.value_load(any_unit[0:1, bass.ds(pair * UNITS + u, 1)], min_val=0, max_val=1)
                            with eng.If(some_u > 0):
                                with eng.Fori(0, N_WIN) as win:
                                    turn = eng.value_load(turn_of[0:1, bass.ds((pair * UNITS + u) * N_WIN + win, 1)],
                                                          min_val=0, max_val=TABLE)
                                    with eng.If(turn > 0):
                                        work(turn, pair, u, win)
                                    eng.nop()
                            eng.nop()
                    eng.nop()

            @block.sync
            def _(sp):
                for k, name in enumerate(("row_max", "row_min")):
                    n = 2 * KK * H
                    sp.dma_start(sub(ranges, 0, PAIRS, k * n, [[1, n]]), dram(name, 0, [[n, PAIRS], [1, n]])).then_inc(S["x_ranges"], 16)
                sp.dma_start(bounds[:, :], dram("bounds", 0, [[2 * N_WIN, PAIRS], [1, 2 * N_WIN]])).then_inc(S["x_ranges"], 16)
                sp.wait_ge(S["x_step"], 6)
                sp.dma_start(dram("needed", 0, [[PU, PAIRS], [1, PU]]), need[:, 0:PU]).then_inc(S["x_need_stored"], 16)
                sp.wait_ge(S["x_need_stored"], 16)
                sp.dma_start(needed, dram("needed", 0, [[TABLE, 1], [1, TABLE]])).then_inc(S["x_need_loaded"], 16)
                sp.wait_ge(S["x_cleared"], 5)
                sp.wait_ge(S["x_tables"], 4)
                far = sp.value_load(any_far[0:1, 0:1], min_val=0, max_val=1)
                with sp.If(far > 0):
                    for a, z in ((0, TOP - NEAR), (TOP + H + NEAR, XT_ROWS)):
                        sp.dma_start(dram("xt", a * C, [[XT_ROW, W], [W * XT_ROW, B], [1, (z - a) * C]]),
                                     sub(zeros, 0, W, 0, [[0, B], [1, (z - a) * C]])).then_inc(S["x_pads"], 16)
                    sp.wait_ge(S["x_pads"], 32)
                sp.nop()

                def work(turn, pair, u, win):
                    for i in range(2):
                        sp.dma_start(sub(xstage[i], 64 * i, W, 0, [[1, STAGE_ROWS * C]]),
                                     dram("xt", (pair * 2 + i) * W * XT_ROW + (TOP - 1 - 60 + u * UNIT_ROWS + win * WIN) * C,
                                          [[XT_ROW, W], [1, STAGE_ROWS * C]])).then_inc(S["x_loaded"], 16)
                        sp.dma_start(sub(xrows, KINDS * i, KINDS, 0, [[UPX, KK], [1, UPX]]).bitcast(fp32),
                                     dram("parts", (pair * 2 + i) * KK * HW + u * UPX,
                                          [[PLANE, KINDS], [HW, KK], [1, UPX]])).then_inc(S["x_loaded"], 16)
                    for there, here in conv_halves(before, pair, u):
                        sp.dma_start(here, there).then_inc(S["x_before"], 16)
                    sp.wait_ge(S["x_added"], turn)
                    sp.sem_inc(S["x_turn"], 1)
                    for there, here in conv_halves(added_to, pair, u):
                        sp.dma_start(there, here).then_inc(S["x_stored"], 16)
                    sp.wait_ge(S["x_stored"], 32 * turn)
                    sp.sem_inc(S["x_turn"], 1)
                windows(sp, work)

            @block.gpsimd
            def _(pool):
                for tile in (xstage[0][:, :], xstage[1][:, :], xrows[:, :].bitcast(fp32), before[:, :], added_to[:, :]):
                    pool.memset(tile, 0.0).then_inc(S["x_cleared"], 1)

            @block.vector
            def _(dve):
                done = [0]

                def step(ins):
                    done[0] += 1
                    ins.then_inc(S["x_step"], 1)
                    dve.wait_ge(S["x_step"], done[0])

                dve.wait_ge(S["x_ranges"], 48)
                n = 2 * KK * H
                step(nc.vector.tensor_reduce(unit_range[:, 0:UNITS],
                                             sub(ranges, 0, PAIRS, 0, [[UNIT_ROWS, UNITS], [H, 2 * KK], [1, UNIT_ROWS]]),
                                             axis=AX.XY, op=ALU.max))
                step(nc.vector.tensor_reduce(unit_range[:, UNITS:],
                                             sub(ranges, 0, PAIRS, n, [[UNIT_ROWS, UNITS], [H, 2 * KK], [1, UNIT_ROWS]]),
                                             axis=AX.XY, op=ALU.min))
                for side, op in ((0, ALU.is_gt), (1, ALU.is_lt)):
                    step(nc.vector.tensor_tensor(sub(need, 0, PAIRS, side * PU, [[N_WIN, UNITS], [1, N_WIN]]),
                                                 sub(unit_range, 0, PAIRS, side * UNITS, [[1, UNITS], [0, N_WIN]]),
                                                 sub(bounds, 0, PAIRS, side * N_WIN, [[0, UNITS], [1, N_WIN]]), op))
                step(nc.vector.tensor_tensor(need[:, PU:], need[:, 0:PU], need[:, PU:], ALU.max))
                step(nc.vector.tensor_copy(need[:, 0:PU], need[:, PU:]))
                dve.wait_ge(S["x_need_loaded"], 16)
                step(nc.vector.tensor_tensor_scan(ordinal, needed, needed, 0.0, ALU.add, ALU.bypass))
                step(nc.vector.tensor_tensor(numbered, ordinal, needed, ALU.mult))
                step(nc.vector.tensor_reduce(by_unit[:, :], sub(X, 0, 1, 0, [[N_WIN, N_UNITS], [1, N_WIN]]),
                                             axis=AX.X, op=ALU.max))
                step(nc.vector.tensor_reduce(by_pair[:, :], sub(X, 0, 1, 0, [[PU, PAIRS], [1, PU]]),
                                             axis=AX.X, op=ALU.max))
                for k, first in enumerate((0, BASE_WIN + 2)):
                    step(nc.vector.tensor_reduce(far_count[:, k:k + 1], sub(X, 0, 1, first, [[N_WIN, N_UNITS], [1, BASE_WIN - 1]]),
                                                 axis=AX.XY, op=ALU.max))
                step(nc.vector.tensor_tensor(far_count[:, 2:3], far_count[:, 0:1], far_count[:, 1:2], ALU.max))
                nc.vector.tensor_copy(any_far[:, :], far_count[:, 2:3]).then_inc(S["x_tables"], 1)
                nc.vector.tensor_copy(turn_of[:, :], numbered).then_inc(S["x_tables"], 1)
                nc.vector.tensor_copy(any_unit[:, :], by_unit[:, :]).then_inc(S["x_tables"], 1)
                nc.vector.tensor_copy(any_pair[:, :], by_pair[:, :]).then_inc(S["x_tables"], 1)

                def work(turn, pair, u, win):
                    for q in range(UNIT_ROWS):
                        dve.wait_ge(Q["x_plus_ready"][q], turn)
                        nc.vector.scalar_tensor_tensor(xtent[:, :], xps_m[:, 0:ROW], 0.0, xplus[:, :],
                                                       ALU.max, ALU.min).then_inc(Q["x_tent_ready"][q], 1)
                        dve.wait_ge(Q["x_dist_ready"][q], turn)
                        nc.vector.tensor_scalar(xdist[:, :], xdist[:, :], 1.0, 1.0, ALU.min, ALU.subtract).then_inc(Q["x_capped"][q], 1)
                        dve.wait_ge(Q["x_capped"][q], turn)
                        dve.wait_ge(Q["x_sampled"][q], turn)
                        nc.vector.tensor_tensor(sub(xG, 0, 128, q * ROW, [[UNIT_ROWS * ROW, 2], [1, ROW]]),
                                                sub(xdist, 0, 128, 0, [[ROW, 2], [1, ROW]]),
                                                sub(xps_v, 0, 128, 0, [[512, 2], [1, ROW]]), ALU.mult).then_inc(Q["x_weighted"][q], 1)
                    dve.wait_ge(S["x_reduced"], turn)
                    dve.wait_ge(S["x_before"], 32 * turn)
                    nc.vector.scalar_tensor_tensor(added_to[:, :], xps_r[:, 0:UPX // 2], -1.0, before[:, :],
                                                   ALU.mult, ALU.add).then_inc(S["x_added"], 1)
                windows(dve, work)

            @block.scalar
            def _(act):
                for tile, name in ((xsel32, "sel"), (xwin_bias, "win_bias"), (xconv_w, "conv_w")):
                    n = tile[:].shape[1]
                    act.dma_start(tile[:, :], dram(name, 0, [[n, 128], [1, n]])).then_inc(S["x_consts"], 16)
                act.wait_ge(S["x_consts"], 48)
                nc.scalar.copy(xsel[:, :], xsel32[:, :]).then_inc(S["x_cast"], 1)

                def work(turn, pair, u, win):
                    for q in range(UNIT_ROWS):
                        act.wait_ge(Q["x_spreads"][q], turn)
                        nc.scalar.activation(xplus[:, :], xps_p[:, 0:ROW], ACT.Relu).then_inc(Q["x_plus_ready"][q], 1)
                        nc.scalar.activation(sub(xdist, 0, 128, 0, [[ROW, 2], [1, ROW]]),
                                             sub(xps_y, 0, 128, 0, [[512, 2], [1, ROW]]), ACT.Abs,
                                             bias=sub(xwin_bias, 0, 128, win, [[1, 1]])).then_inc(Q["x_dist_ready"][q], 1)
                windows(act, work)

            @block.tensor
            def _(pe):
                pe.wait_ge(S["x_cast"], 1)
                pe.wait_ge(S["x_cleared"], 5)
                taps = lambda q: sub(xrows, 0, 128, q * W, [[UPX, KK], [1, W]])

                def work(turn, pair, u, win):
                    pe.wait_ge(S["x_loaded"], 64 * turn)
                    for q in range(UNIT_ROWS):
                        if q:
                            pe.wait_ge(Q["x_weighted"][q - 1], turn)
                        nc.tensor.matmul(xps_p[:, 0:ROW], xsel[:, 0:128], taps(q), start=True, stop=True)
                        nc.tensor.matmul(xps_m[:, 0:ROW], xsel[:, 128:256], taps(q), start=True, stop=True)
                        for i in range(2):
                            m = nc.tensor.matmul(xps_y[:, i * 512:i * 512 + ROW], xsel[:, (2 + i) * 128:(3 + i) * 128],
                                                 taps(q), start=True, stop=True)
                        m.then_inc(Q["x_spreads"][q], 1)
                        pe.wait_ge(Q["x_tent_ready"][q], turn)
                        for i in range(2):
                            for ky in range(3):
                                m = nc.tensor.matmul(xps_v[:, i * 512 + ky * 3 * W:i * 512 + (ky + 1) * 3 * W],
                                                     xstage[i][:, (q + ky) * C:(q + ky + WIN) * C],
                                                     xtent[:, ky * 3 * W:(ky + 1) * 3 * W], start=True, stop=True)
                        m.then_inc(Q["x_sampled"][q], 1)
                    pe.wait_ge(Q["x_weighted"][UNIT_ROWS - 1], turn)
                    for k in range(KK):
                        for j in range(4):
                            i, h = j // 2, j % 2
                            m = nc.tensor.matmul(xps_r[32 * j:32 * j + 32, 0:UPX // 2], xconv_w[:, k * 32:(k + 1) * 32],
                                                 sub(xG, 0, 128, (i * UNIT_ROWS + 2 * h) * ROW + k * W, [[ROW, 2], [1, W]]),
                                                 start=(k == 0), stop=(k == KK - 1))
                    m.then_inc(S["x_reduced"], 1)
                windows(pe, work)


        with ExitStack() as st:
            sb, ps, sem = tools(st)
            CH = 448
            NCH = GROUPS * HW // CH
            PER = HW // CH
            stats = sb("stats", NCH * 6)
            mv = sb("mv", 2)
            t = sb("t", 12)
            y = [sb(f"y{i}", HW) for i in range(2)]
            ps_s = [ps("ps_mean"), ps("ps_var")]
            loaded = [sem(f"conv_loaded{g}") for g in range(GROUPS)]
            dve_step, pe_step, act_step, activated, added = [sem(n) for n in (
                "bn_dve_step", "bn_pe_step", "bn_act_step", "activated", "added")]
            out_stored = [sem(f"out_stored{i}") for i in range(2)]
            block = st.enter_context(nc.Block())

            @block.sync
            def _(sp):
                for img in range(B):
                    g = img // GB
                    sp.dma_start(sub(X, img % GB * O, O, g * HW, [[UPX // 2, 2 * UNITS], [1, UPX // 2]]),
                                 dram("conv", img * CONV_IMG, [[UPX // 2, O], [32 * UPX // 2, 2 * UNITS], [1, UPX // 2]])
                                 ).then_inc(loaded[g], 16)
                for g in range(GROUPS):
                    sp.wait_ge(added, g + 1)
                    sp.dma_start(dram("out", g * 128 * HW, [[HW, 128], [1, HW]]), y[g % 2][:, :]).then_inc(out_stored[g % 2], 16)
                for i in range(2):
                    sp.wait_ge(out_stored[i], 32)

            @block.tensor
            def _(pe):
                pe.wait_ge(dve_step, 2)
                nc.tensor.matmul(ps_s[0][:, 0:1], same_channel[:, :], mv[:, 0:1], start=True, stop=True).then_inc(pe_step, 1)
                pe.wait_ge(dve_step, 5)
                nc.tensor.matmul(ps_s[1][:, 0:1], same_channel[:, :], t[:, 2:3], start=True, stop=True).then_inc(pe_step, 1)

            @block.scalar
            def _(act):
                act.wait_ge(dve_step, 6)
                nc.scalar.activation(t[:, 4:5], t[:, 3:4], ACT.Sqrt).then_inc(act_step, 1)
                act.wait_ge(dve_step, 12)
                for g in range(GROUPS):
                    wait(act, out_stored[g % 2], 16 * (g // 2))
                    nc.scalar.activation(y[g % 2][:, :], X[:, g * HW:(g + 1) * HW], ACT.Relu, scale=t[:, 8:9],
                                         bias=t[:, 10:11]).then_inc(activated, 1)

            @block.vector
            def _(dve):
                done = [0]

                def step(ins):
                    done[0] += 1
                    ins.then_inc(dve_step, 1)
                    dve.wait_ge(dve_step, done[0])

                for c in range(NCH):
                    if c % PER == 0:
                        dve.wait_ge(loaded[c // PER], 16 * GB)
                    last = nc.vector.bn_stats(stats[:, c * 6:(c + 1) * 6], X[:, c * CH:(c + 1) * CH])
                step(last)
                step(nc.vector.bn_aggr(mv[:, :], stats[:, :]))
                dve.wait_ge(pe_step, 1)
                step(nc.vector.tensor_scalar(t[:, 0:1], ps_s[0][:, 0:1], 1.0 / GB, None, ALU.mult))
                step(nc.vector.tensor_tensor(t[:, 1:2], mv[:, 0:1], t[:, 0:1], ALU.subtract))
                step(nc.vector.scalar_tensor_tensor(t[:, 2:3], t[:, 1:2], t[:, 1:2], mv[:, 1:2],
                                                    ALU.mult, ALU.add))
                dve.wait_ge(pe_step, 2)
                step(nc.vector.tensor_scalar(t[:, 3:4], ps_s[1][:, 0:1], 1.0 / GB, 1e-5, ALU.mult, ALU.add))
                dve.wait_ge(act_step, 1)
                step(nc.vector.reciprocal(t[:, 5:6], t[:, 4:5]))
                step(nc.vector.scalar_tensor_tensor(t[:, 6:7], t[:, 5:6], t[:, 3:4], t[:, 4:5],
                                                    ALU.mult, ALU.add))
                step(nc.vector.reciprocal(t[:, 7:8], t[:, 6:7]))
                step(nc.vector.tensor_scalar(t[:, 8:9], t[:, 7:8], 2.0, vecs[:, 1:2], ALU.mult, ALU.mult))
                step(nc.vector.tensor_tensor(t[:, 9:10], t[:, 0:1], t[:, 8:9], ALU.mult))
                step(nc.vector.tensor_tensor(t[:, 10:11], vecs[:, 2:3], t[:, 9:10], ALU.subtract))
                for g in range(GROUPS):
                    dve.wait_ge(activated, g + 1)
                    nc.vector.tensor_tensor(y[g % 2][:, :].rearrange("p (r w) -> p r w", w=W),
                                            y[g % 2][:, :].rearrange("p (r w) -> p r w", w=W),
                                            sub(XH, 0, 128, g * PADHW + PADW + 1, [[PADW, H], [1, W]]),
                                            ALU.add).then_inc(added, 1)


def shape_constants():
    import numpy as np
    f = np.float32
    p = np.arange(128)
    img, ch = p // C, p % C
    eye = np.eye(128, dtype=f)
    out = {"ident": eye, "same_image": (img[:, None] == img[None]).astype(f),
           "same_channel": (ch[:, None] == ch[None]).astype(f), "eps_eye": (1e-5 * eye).astype(f),
           "shrink": (0.9 + 0.1 * eye).astype(f)}
    out["column"] = np.broadcast_to(np.arange(W, dtype=f), (128, W)).copy()
    first = (np.arange(128) % (128 // B) * DENSE)[:, None] + np.arange(DENSE // DCH)[None] * DCH
    out["tap_shift"] = (first // HW % 3 - 1).astype(f)
    sel = np.zeros((128, 4, 128), f)
    col = np.arange(W)
    for i in range(2):
        for k in range(2):
            sel[KINDS * i + k, 0, 64 * i + col] = 1.0
            sel[KINDS * i + 2 + k, 0, 64 * i + col] = 1.0 - col
            sel[KINDS * i + k, 1, 64 * i + col] = -1.0
            sel[KINDS * i + 2 + k, 1, 64 * i + col] = 1.0 + col
            sel[KINDS * i + 4 + k, 2 + i, :] = 1.0
    out["sel"] = sel.reshape(128, 512)
    out["win_bias"] = -(WIN * np.arange(N_WIN)[None, :] - 60 + (p // C)[:, None]).astype(f)
    big = 3e38
    j = np.arange(N_WIN)
    start = WIN * j - 60
    hi = np.where(j > BASE_WIN, start - 1, big).astype(f)
    lo = np.where(j < BASE_WIN, start + WIN, -big).astype(f)
    out["bounds"] = np.broadcast_to(np.stack([hi, lo])[None], (PAIRS, 2, N_WIN)).copy().reshape(PAIRS, 2 * N_WIN)
    return out


def kernel(x, L0_conv_beta, L1_conv_w_off, L1_conv_b_off, L1_conv_w, L1_conv_b, L1_conv_gamma, L1_conv_beta):
    import numpy as np
    import concourse.bacc as bacc
    from concourse.bass_utils import run_bass_kernel_spmd
    f = np.float32
    arrays = shape_constants()
    arrays["x"] = np.ascontiguousarray(x)
    w_off, w = np.asarray(L1_conv_w_off), np.asarray(L1_conv_w)
    tile = lambda v: np.tile(np.asarray(v), GB)
    vecs = np.zeros((128, 4), f)
    for n, v in enumerate((L0_conv_beta, L1_conv_gamma, L1_conv_beta)):
        vecs[:, n] = tile(v)
    arrays["vecs"] = vecs
    woff = np.zeros((4, 2, C, 3, 2, 32), f)
    boff = np.zeros((4, 32), f)
    for i in range(2):
        woff[:3, i, :, :, i, :3 * KK] = w_off.transpose(2, 1, 3, 0)
    boff[:, :3 * KK] = np.asarray(L1_conv_b_off)[None]
    arrays["woff"] = woff.reshape(128, 3 * 2 * 32)
    arrays["boff"] = boff.reshape(128, 1)
    conv_w = np.zeros((WIN, C, KK, 32), f)
    conv_w[:, :, :, :O] = w.reshape(O, C, KK).transpose(1, 2, 0)[None]
    arrays["conv_w"] = conv_w.reshape(128, KK * 32)
    conv_b = np.zeros((4, 32), f)
    conv_b[:, :O] = np.asarray(L1_conv_b)[None]
    arrays["conv_b"] = conv_b.reshape(128, 1)

    nc = bacc.Bacc("TRN2", target_bir_lowering=False, num_devices=1)
    fp32 = mybir.dt.float32
    dr = {n: nc.dram_tensor(f"in_{n}", a.shape, fp32, kind="ExternalInput").ap() for n, a in arrays.items()}
    for name, size, dt in (("xt", B * W * XT_ROW, fp32), ("xt_hi", PAIRS * W * XT_ROW, fp32),
                           ("xt_lo", PAIRS * W * XT_ROW, fp32), ("xh", B * C * PADHW, fp32), ("om", B * OM_IMG, fp32),
                           ("parts", KINDS * PLANE, fp32), ("row_max", PLANE // W, fp32), ("row_min", PLANE // W, fp32),
                           ("conv", B * CONV_IMG, fp32), ("needed", 2 * N_UNITS * N_WIN, fp32)):
        dr[name] = nc.dram_tensor(f"scratch_{name}", (size,), dt, kind="Internal").ap()
    dr["out"] = nc.dram_tensor("out", (B, O, H, W), fp32, kind="ExternalOutput").ap()
    program(nc, dr)
    r = run_bass_kernel_spmd(nc, [{f"in_{n}": a for n, a in arrays.items()}], core_ids=[0])
    return r.results[0]["out"]
```

```python
import concourse.bass as bass
from concourse import mybir
from contextlib import ExitStack

B, C, H, W = 32, 16, 56, 56
O = 16
KK = 9
HW = H * W
M_ALL = B * HW
GROUPS = 4
GB = B // GROUPS
PADW = W + 2
PADHW = (H + 2) * PADW
PAIRS = B // 2
UNIT_ROWS = 4
UNITS = H // UNIT_ROWS
N_UNITS = PAIRS * UNITS
UPX = UNIT_ROWS * W
WIN = 8
N_WIN = 15
BASE_WIN = 7
STAGE_ROWS = UNIT_ROWS + 2 + WIN - 1
TOP = 64
NEAR = 2 * WIN
XT_ROWS = TOP + H + TOP
XT_ROW = XT_ROWS * C
PLANE = B * KK * HW
OM_IMG = 32 * HW
DENSE = PLANE // 128
DCH = 392
D_RING = 3
D_IT = DENSE // DCH // D_RING
NT = 10
KINDS = 6
TAPS_PX = KK * W
UNIT_SAMPLES = 2 * UNIT_ROWS * TAPS_PX
CONV_ROW = HW // 2


def program(nc, dr):
    fp32, f32r, i32 = mybir.dt.float32, mybir.dt.float32r, mybir.dt.int32
    ALU, ACT, AX = mybir.AluOpType, mybir.ActivationFunctionType, mybir.AxisListType

    def dram(name, offset, dims):
        return bass.AP(tensor=dr[name].tensor, offset=offset, ap=dims)

    def sub(tile, part, parts, offset, dims):
        pitch = tile[:].ap[0][0]
        return bass.AP(tensor=tile[:].tensor, offset=part * pitch + offset, ap=[[pitch, parts]] + dims)

    def peel(eng, count, body):
        body(0, False)
        with eng.Fori(1, count - 1) as it:
            body(it, False)
        body(count - 1, True)

    def wait(eng, sem, value):
        if not (isinstance(value, int) and value <= 0):
            eng.wait_ge(sem, value)

    outer = ExitStack()
    with outer:
        def tools(stack):
            def sb(name, cols, dt=fp32, parts=128):
                return stack.enter_context(nc.sbuf_tensor(name, [parts, cols], dt))

            def ps(name, banks=1):
                return stack.enter_context(nc.psum_tensor(name, [128, 512 * banks], fp32))

            def sem(name):
                return stack.enter_context(nc.semaphore(name))
            return sb, ps, sem

        sb, ps, sem = tools(outer)
        X = sb("X", max(GROUPS * HW, 4 * UNIT_SAMPLES))
        XH = sb("XH", GROUPS * PADHW)
        ident = sb("ident", 128)
        same_image = sb("same_image", 128)
        same_channel = sb("same_channel", 128)
        vecs = sb("vecs", 3)
        wm = sb("wm", 128)
        zeros = sb("zeros", XT_ROWS * C)

        with ExitStack() as st:
            sb, ps, sem = tools(st)
            CH = 448
            IT = GROUPS * HW // CH // 2
            eps_eye = sb("eps_eye", 128)
            shrink = sb("shrink", 128)
            xs4 = sb("xs4", GROUPS)
            small = sb("small", 8)
            flat = [sb(f"flat{i}", CH) for i in range(2)]
            pix = [sb(f"pix{i}", 512, parts=112) for i in range(2)]
            S1, S2, SN, Pm, P15, PP, PS = [sb(n, 128) for n in ("S1", "S2", "SN", "Pm", "P15", "PP", "PS")]
            sig = sb("sig", C)
            ps_pix = [ps(f"ps_pix{i}") for i in range(2)]
            ps_gram = ps("ps_gram")
            ps_a, ps_b, ps_c = ps("ps_a"), ps("ps_b"), ps("ps_c")
            consts_loaded = sem("consts_loaded")
            x_loaded = [sem(f"x_loaded{g}") for g in range(GROUPS)]
            dve_step, pe_step, act_step = sem("dve_step"), sem("pe_step"), sem("act_step")
            centred, staged, transposed, evacuated, grammed = [
                sem(n) for n in ("centred", "staged", "transposed", "evacuated", "grammed")]
            new_p, products, pp_ready, act_ready = [sem(n) for n in ("new_p", "products", "pp_ready", "act_ready")]
            zeroed = sem("zeroed")
            LOADS = ((ident, "ident"), (same_image, "same_image"), (same_channel, "same_channel"), (vecs, "vecs"),
                     (eps_eye, "eps_eye"), (shrink, "shrink"))
            block = st.enter_context(nc.Block())

            @block.sync
            def _(sp):
                for g in range(GROUPS):
                    sp.dma_start(X[:, g * HW:(g + 1) * HW],
                                 dram("x", g * 128 * HW, [[HW, 128], [1, HW]])).then_inc(x_loaded[g], 16)

            @block.gpsimd
            def _(pool):
                pool.memset(XH[:, :], 0.0).then_inc(zeroed, 1)
                pool.memset(zeros[:, :], 0.0).then_inc(zeroed, 1)
                pool.wait_ge(zeroed, 2)

            @block.scalar
            def _(act):
                for tile, name in LOADS:
                    n = tile[:].shape[1]
                    act.dma_start(tile[:, :], dram(name, 0, [[n, 128], [1, n]])).then_inc(consts_loaded, 16)
                act.wait_ge(centred, GROUPS)

                def stage(it, last):
                    for b in range(2):
                        c = 2 * it + b
                        wait(act, transposed, c - 1)
                        nc.scalar.copy(flat[b][:, :], sub(X, 0, 128, c * CH, [[1, CH]])).then_inc(staged, 1)
                peel(act, IT, stage)
                act.wait_ge(dve_step, 11)
                nc.scalar.activation(small[:, 4:5], small[:, 3:4], ACT.Sqrt).then_inc(act_step, 1)

                def newton(i, last):
                    act.wait_ge(new_p, i + 1)
                    nc.scalar.mul(P15[:, :], Pm[:, :], 1.5).then_inc(act_ready, 1)
                    act.wait_ge(products, 3 * i + 2)
                    nc.scalar.copy(PS[:, :], ps_b[:, 0:128]).then_inc(act_ready, 1)
                peel(act, NT, newton)

            @block.vector
            def _(dve):
                done = [0]

                def step(ins):
                    done[0] += 1
                    ins.then_inc(dve_step, 1)
                    dve.wait_ge(dve_step, done[0])

                for g in range(GROUPS):
                    dve.wait_ge(x_loaded[g], 16)
                    last = nc.vector.reduce_sum(xs4[:, g:g + 1], X[:, g * HW:(g + 1) * HW], axis=AX.X)
                step(last)
                step(nc.vector.reduce_sum(small[:, 0:1], xs4[:, :], axis=AX.X))
                dve.wait_ge(pe_step, 1)
                step(nc.vector.tensor_scalar(small[:, 1:2], ps_a[:, 0:1], 1.0 / M_ALL, None, ALU.mult))
                for g in range(GROUPS):
                    v = X[:, g * HW:(g + 1) * HW]
                    nc.vector.tensor_scalar(v, v, small[:, 1:2], None, ALU.subtract).then_inc(centred, 1)

                def evac(it, last):
                    for b in range(2):
                        c = 2 * it + b
                        dve.wait_ge(transposed, c + 1)
                        wait(dve, grammed, c - 1)
                        nc.vector.tensor_copy(pix[b][:, :], ps_pix[b][0:112, :]).then_inc(evacuated, 1)
                peel(dve, IT, evac)
                dve.wait_ge(grammed, 2 * IT)
                step(nc.vector.tensor_tensor(S1[:, :], ps_gram[:, 0:128], same_image[:, :], ALU.mult))
                dve.wait_ge(pe_step, 2)
                step(nc.vector.reduce_sum(sig[:, :], sub(ps_b, 0, 128, 0, [[1, C], [C, GB]]), axis=AX.X))
                step(nc.vector.tensor_tensor(S2[:, :].rearrange("p (b c) -> p b c", c=C),
                                             sub(sig, 0, 128, 0, [[0, GB], [1, C]]),
                                             same_image[:, :].rearrange("p (b c) -> p b c", c=C), ALU.mult))
                step(nc.vector.scalar_tensor_tensor(S1[:, :], S2[:, :], 1.0 / M_ALL, eps_eye[:, :],
                                                    ALU.mult, ALU.add))
                step(nc.vector.tensor_tensor(S2[:, :], S1[:, :], shrink[:, :], ALU.mult))
                step(nc.vector.tensor_tensor(S1[:, :], S2[:, :], ident[:, :], ALU.mult))
                step(nc.vector.reduce_sum(small[:, 2:3], S1[:, :], axis=AX.X))
                dve.wait_ge(pe_step, 3)
                step(nc.vector.reciprocal(small[:, 3:4], ps_c[:, 0:1]))
                step(nc.vector.tensor_scalar(SN[:, :], S2[:, :], small[:, 3:4], None, ALU.mult))
                dve.wait_ge(act_step, 1)
                step(nc.vector.reciprocal(small[:, 5:6], small[:, 4:5]))
                step(nc.vector.scalar_tensor_tensor(small[:, 6:7], small[:, 5:6], small[:, 3:4], small[:, 4:5],
                                                    ALU.mult, ALU.add))
                step(nc.vector.tensor_scalar(small[:, 7:8], small[:, 6:7], 0.5, None, ALU.mult))
                nc.vector.tensor_copy(Pm[:, :], ident[:, :]).then_inc(new_p, 1)

                def newton(i, last):
                    dve.wait_ge(products, 3 * i + 1)
                    nc.vector.tensor_copy(PP[:, :], ps_a[:, 0:128]).then_inc(pp_ready, 1)
                    dve.wait_ge(products, 3 * i + 3)
                    dve.wait_ge(act_ready, 2 * i + 1)
                    nc.vector.scalar_tensor_tensor(Pm[:, :], ps_c[:, 0:128], -0.5, P15[:, :],
                                                   ALU.mult, ALU.add).then_inc(new_p, 1)
                peel(dve, NT, newton)
                dve.wait_ge(new_p, NT + 1)
                step(nc.vector.tensor_scalar(wm[:, :], Pm[:, :], small[:, 7:8], None, ALU.mult))

            @block.tensor
            def _(pe):
                pe.wait_ge(consts_loaded, 16 * len(LOADS))
                pe.wait_ge(dve_step, 2)
                nc.tensor.matmul(ps_a[:, 0:1], same_channel[:, :], small[:, 0:1],
                                 start=True, stop=True).then_inc(pe_step, 1)

                def turn(it, b):
                    c = 2 * it + b
                    pe.wait_ge(staged, c + 1)
                    wait(pe, evacuated, c - 1)
                    for i in range(4):
                        t = nc.tensor.transpose(ps_pix[b][0:112, i * 128:(i + 1) * 128],
                                                flat[b][:, i * 112:(i + 1) * 112], ident[:, :])
                    t.then_inc(transposed, 1)

                def gram(it, last):
                    for b in range(2):
                        if not (last and b == 1):
                            turn(it + b, 1 - b)
                        pe.wait_ge(evacuated, 2 * it + b + 1)
                        for i in range(4):
                            m = nc.tensor.matmul(ps_gram[:, 0:128], pix[b][:, i * 128:(i + 1) * 128],
                                                 pix[b][:, i * 128:(i + 1) * 128],
                                                 start=(isinstance(it, int) and it == 0 and b == 0 and i == 0),
                                                 stop=(last and b == 1 and i == 3))
                        m.then_inc(grammed, 1)
                turn(0, 0)
                peel(pe, IT, gram)
                pe.wait_ge(dve_step, 4)
                nc.tensor.matmul(ps_b[:, 0:128], same_channel[:, :], S1[:, :], start=True, stop=True).then_inc(pe_step, 1)
                pe.wait_ge(dve_step, 10)
                nc.tensor.matmul(ps_c[:, 0:1], same_image[:, :], small[:, 2:3], start=True, stop=True).then_inc(pe_step, 1)
                pe.wait_ge(dve_step, 12)

                def newton(i, last):
                    pe.wait_ge(new_p, i + 1)
                    nc.tensor.matmul(ps_a[:, 0:128], Pm[:, :], Pm[:, :], start=True, stop=True).then_inc(products, 1)
                    nc.tensor.matmul(ps_b[:, 0:128], Pm[:, :], SN[:, :], start=True, stop=True).then_inc(products, 1)
                    pe.wait_ge(pp_ready, i + 1)
                    pe.wait_ge(act_ready, 2 * i + 2)
                    nc.tensor.matmul(ps_c[:, 0:128], PP[:, :], PS[:, :], start=True, stop=True).then_inc(products, 1)
                peel(pe, NT, newton)

        with ExitStack() as st:
            sb, ps, sem = tools(st)
            ROWS = 8
            CH = ROWS * W
            IT = H // ROWS
            xst = [sb(f"xst{i}", CH + W) for i in range(2)]
            xts = [sb(f"xts{i}", GB * ROWS * C, parts=W) for i in range(2)]
            xts_hi = [sb(f"xts_hi{i}", GB // 2 * ROWS * C, f32r, parts=W) for i in range(2)]
            xts_lo = [sb(f"xts_lo{i}", GB // 2 * ROWS * C, f32r, parts=W) for i in range(2)]
            ps_w = [ps(f"ps_w{i}") for i in range(2)]
            ps_x = [ps(f"ps_x{i}", 2) for i in range(2)]
            padded, rounded, lowered = sem("padded"), sem("rounded"), sem("lowered")
            whitened, with_beta, kept, turned, sorted_, stored_pads, stored_xh = [
                sem(n) for n in ("whitened", "with_beta", "kept", "turned", "sorted", "stored_pads", "stored_xh")]
            stored_xt = [sem(f"stored_xt{i}") for i in range(2)]
            block = st.enter_context(nc.Block())

            def even(tile):
                return sub(tile, 0, W, 0, [[2 * ROWS * C, GB // 2], [1, ROWS * C]])

            def halves(tile):
                return sub(tile, 0, W, 0, [[ROWS * C, GB // 2], [1, ROWS * C]])

            @block.tensor
            def _(pe):
                pe.wait_ge(padded, 2)

                def lead(c, g, yb):
                    wait(pe, with_beta, c - 1)
                    nc.tensor.matmul(ps_w[g % 2][:, 0:CH], wm[:, :], sub(X, 0, 128, g * HW + yb * CH, [[1, CH]]),
                                     start=True, stop=True).then_inc(whitened, 1)

                def body(yb, last):
                    for g in range(GROUPS):
                        c = yb * GROUPS + g
                        if not (last and g == GROUPS - 1):
                            lead(c + 1, (g + 1) % GROUPS, yb + (g + 1) // GROUPS)
                        pe.wait_ge(with_beta, c + 1)
                        wait(pe, sorted_, c - 1)
                        for r in range(ROWS):
                            t = nc.tensor.transpose(ps_x[g % 2][0:2 * W, r * 128:(r + 1) * 128],
                                                    xst[g % 2][:, r * W:(r + 2) * W], ident[:, :])
                        t.then_inc(turned, 1)
                lead(0, 0, 0)
                peel(pe, IT, body)

            @block.scalar
            def _(act):
                def beta(yb, g):
                    c = yb * GROUPS + g
                    act.wait_ge(whitened, c + 1)
                    wait(act, turned, c - 1)
                    wait(act, kept, c - 1)
                    nc.scalar.activation(xst[g % 2][:, 0:CH], ps_w[g % 2][:, 0:CH], ACT.Identity,
                                         bias=vecs[:, 0:1]).then_inc(with_beta, 1)

                def body(yb, last):
                    for g in range(GROUPS):
                        c = yb * GROUPS + g
                        if not (last and g == GROUPS - 1):
                            beta(yb + (g + 1) // GROUPS, (g + 1) % GROUPS)
                        act.wait_ge(sorted_, c + 1)
                        wait(act, stored_xt[g % 2], 48 * (yb * 2 + g // 2))
                        nc.scalar.copy(halves(xts_hi[g % 2]), even(xts[g % 2])).then_inc(rounded, 1)
                beta(0, 0)
                peel(act, IT, body)

            @block.gpsimd
            def _(pool):
                for i in range(2):
                    pool.memset(xst[i][:, CH:CH + W], 0.0).then_inc(padded, 1)

                def body(yb, last):
                    for g in range(GROUPS):
                        pool.wait_ge(rounded, yb * GROUPS + g + 1)
                        wait(pool, stored_xt[g % 2], 48 * (yb * 2 + g // 2))
                        pool.tensor_tensor(halves(xts_lo[g % 2]), even(xts[g % 2]), halves(xts_hi[g % 2]).bitcast(fp32),
                                           ALU.subtract).then_inc(lowered, 1)
                peel(pool, IT, body)

            @block.vector
            def _(dve):
                def body(yb, last):
                    for g in range(GROUPS):
                        c = yb * GROUPS + g
                        dve.wait_ge(with_beta, c + 1)
                        nc.vector.tensor_copy(
                            sub(XH, 0, 128, g * PADHW + (yb * ROWS + 1) * PADW + 1, [[PADW, ROWS], [1, W]]),
                            xst[g % 2][:, 0:CH].rearrange("p (r w) -> p r w", w=W)).then_inc(kept, 1)
                        dve.wait_ge(turned, c + 1)
                        wait(dve, stored_xt[g % 2], 48 * (yb * 2 + g // 2))
                        for h in range(2):
                            e = nc.vector.tensor_copy(
                                sub(xts[g % 2], 0, W, h * 4 * C, [[ROWS * C, GB], [C, 4], [1, C]]),
                                sub(ps_x[g % 2], 0, W, h * 512, [[C, GB], [128, 4], [1, C]]))
                        e.then_inc(sorted_, 1)
                peel(dve, IT, body)

            @block.sync
            def _(sp):
                for first in (TOP - NEAR, TOP + H):
                    sp.dma_start(dram("xt", first * C, [[XT_ROW, W], [W * XT_ROW, B], [1, NEAR * C]]),
                                 sub(zeros, 0, W, 0, [[0, B], [1, NEAR * C]])).then_inc(stored_pads, 16)
                for first in (TOP - WIN, TOP + H):
                    for name in ("xt_hi", "xt_lo"):
                        sp.dma_start(dram(name, first * C, [[XT_ROW, W], [W * XT_ROW, PAIRS], [1, WIN * C]]),
                                     sub(zeros, 0, W, 0, [[0, PAIRS], [1, WIN * C]])).then_inc(stored_pads, 16)

                for row in (0, H + 1):
                    sp.dma_start(dram("xh", row * PADW, [[PADHW, 128], [128 * PADHW, GROUPS], [1, PADW]]),
                                 sub(XH, 0, 128, row * PADW, [[PADHW, GROUPS], [1, PADW]])).then_inc(stored_xh, 16)

                def body(yb, last):
                    for g in range(GROUPS):
                        sp.wait_ge(sorted_, yb * GROUPS + g + 1)
                        sp.dma_start(dram("xt", g * GB * W * XT_ROW + (TOP + yb * ROWS) * C,
                                          [[XT_ROW, W], [W * XT_ROW, GB], [1, ROWS * C]]),
                                     sub(xts[g % 2], 0, W, 0, [[ROWS * C, GB], [1, ROWS * C]])).then_inc(stored_xt[g % 2], 16)
                        for name, tile, ready in (("xt_hi", xts_hi[g % 2], rounded), ("xt_lo", xts_lo[g % 2], lowered)):
                            sp.wait_ge(ready, yb * GROUPS + g + 1)
                            sp.dma_start(dram(name, g * GB // 2 * W * XT_ROW + (TOP + yb * ROWS) * C,
                                              [[XT_ROW, W], [W * XT_ROW, GB // 2], [1, ROWS * C]]),
                                         sub(tile, 0, W, 0, [[ROWS * C, GB // 2], [1, ROWS * C]]).bitcast(fp32)
                                         ).then_inc(stored_xt[g % 2], 16)
                        sp.wait_ge(kept, yb * GROUPS + g + 1)
                        sp.dma_start(dram("xh", g * 128 * PADHW + (yb * ROWS + 1) * PADW, [[PADHW, 128], [1, ROWS * PADW]]),
                                     sub(XH, 0, 128, g * PADHW + (yb * ROWS + 1) * PADW, [[1, ROWS * PADW]])
                                     ).then_inc(stored_xh, 16)
                peel(sp, IT, body)
                sp.wait_ge(stored_xh, 16 * (IT * GROUPS + 2))
                sp.wait_ge(stored_pads, 96)
                for i in range(2):
                    sp.wait_ge(stored_xt[i], 48 * IT * 2)

        with ExitStack() as st:
            sb, ps, sem = tools(st)
            ROWS = 7
            CH = ROWS * W
            HALF = H // 2
            NCH = HALF // ROWS
            SHIFTS = 3 * 2 * C
            woff = sb("woff", 3 * 2 * 32)
            boff = sb("boff", 1)
            x3 = [sb(f"x3{i}", H * PADW) for i in range(2)]
            om = [sb(f"om{i}", HALF * W) for i in range(2)]
            ps_o = [ps(f"ps_o{i}") for i in range(2)]
            w_loaded, convolved, biased, x3_padded = [sem(n) for n in ("w_loaded", "convolved", "biased", "x3_padded")]
            x3_loaded = [sem(f"x3_loaded{i}") for i in range(2)]
            om_stored = [sem(f"om_stored{i}") for i in range(2)]
            block = st.enter_context(nc.Block())

            @block.sync
            def _(sp):
                sp.dma_start(woff[:, :], dram("woff", 0, [[3 * 2 * 32, 128], [1, 3 * 2 * 32]])).then_inc(w_loaded, 16)
                sp.dma_start(boff[:, :], dram("boff", 0, [[1, 128], [1, 1]])).then_inc(w_loaded, 16)

                def body(it, last):
                    for b in range(2):
                        pair = 2 * it + b
                        wait(sp, convolved, (pair - 1) * NCH)
                        for dy in range(3):
                            sp.dma_start(sub(x3[b], dy * 2 * C, 2 * C, 0, [[1, H * PADW]]),
                                         dram("xh", pair * 2 * C * PADHW + dy * PADW,
                                              [[PADHW, 2 * C], [1, H * PADW]])).then_inc(x3_loaded[b], 16)
                peel(sp, PAIRS // 2, body)

            @block.vector
            def _(dve):
                for b in range(2):
                    dve.memset(x3[b][SHIFTS:128, :], 0.0).then_inc(x3_padded, 1)

            @block.tensor
            def _(pe):
                pe.wait_ge(w_loaded, 32)
                pe.wait_ge(x3_padded, 2)

                def body(it, last):
                    for b in range(2):
                        pair = 2 * it + b
                        pe.wait_ge(x3_loaded[b], 48 * (it + 1))
                        for ch in range(NCH):
                            n = pair * NCH + ch
                            wait(pe, biased, n - 1)
                            for kx in range(3):
                                for j in range(4):
                                    i, h = j // 2, j % 2
                                    m = nc.tensor.matmul(ps_o[ch % 2][32 * j:32 * j + 32, 0:CH],
                                                         woff[:, (2 * kx + i) * 32:(2 * kx + i + 1) * 32],
                                                         sub(x3[b], 0, 128, (h * HALF + ch * ROWS) * PADW + kx,
                                                             [[PADW, ROWS], [1, W]]),
                                                         start=(kx == 0), stop=(kx == 2))
                            m.then_inc(convolved, 1)
                peel(pe, PAIRS // 2, body)

            @block.scalar
            def _(act):
                act.wait_ge(w_loaded, 32)

                def body(it, last):
                    for b in range(2):
                        pair = 2 * it + b
                        wait(act, om_stored[b], 64 * it)
                        for ch in range(NCH):
                            n = pair * NCH + ch
                            act.wait_ge(convolved, n + 1)
                            nc.scalar.activation(om[b][:, ch * CH:(ch + 1) * CH], ps_o[ch % 2][:, 0:CH],
                                                 ACT.Identity, bias=boff[:, 0:1]).then_inc(biased, 1)
                        act.wait_ge(biased, (pair + 1) * NCH)
                        for j in range(4):
                            i, h = j // 2, j % 2
                            act.dma_start(dram("om", (pair * 2 + i) * OM_IMG + h * HALF * W, [[HW, 32], [1, HALF * W]]),
                                          sub(om[b], 32 * j, 32, 0, [[1, HALF * W]])).then_inc(om_stored[b], 16)
                peel(act, PAIRS // 2, body)
                for b in range(2):
                    act.wait_ge(om_stored[b], 64 * PAIRS // 2)

        with ExitStack() as st:
            sb, ps, sem = tools(st)
            RPC = DCH // W
            val = [sb(f"val{i}", 3 * DCH) for i in range(D_RING)]
            px = [sb(f"px{i}", DCH) for i in range(D_RING)]
            logit = [sb(f"logit{i}", DCH) for i in range(D_RING)]
            column, tap_shift = sb("column", W), sb("tap_shift", D_RING * D_IT)
            grid_loaded = sem("grid_loaded")
            parts = [sb(f"parts{i}", KINDS * DCH, f32r) for i in range(D_RING)]
            row_max, row_min = sb("row_max", DENSE // W), sb("row_min", DENSE // W)
            loaded = [sem(f"loaded{i}") for i in range(D_RING)]
            stored = [sem(f"stored{i}") for i in range(D_RING)]
            masked, summed, ranged, scaled, high, low, ranges_stored = [sem(n) for n in (
                "masked", "summed", "ranged", "scaled", "high", "low", "ranges_stored")]
            block = st.enter_context(nc.Block())

            def part(b, k):
                return sub(parts[b], 0, 128, k * DCH, [[2 * DCH, 3], [1, DCH]])

            def three(tile):
                return sub(tile, 0, 128, 0, [[DCH, 3], [1, DCH]])

            def overlapped(eng, lead, tail):
                lead(0, 0)

                def body(it, last):
                    for b in range(D_RING):
                        wrap = b == D_RING - 1
                        if not (last and wrap):
                            lead(it + (1 if wrap else 0), 0 if wrap else b + 1)
                        tail(it, b)
                peel(eng, D_IT, body)

            @block.sync
            def _(sp):
                def lead(it, b):
                    n = D_RING * it + b
                    wait(sp, low, n - D_RING + 1)
                    for tile, off, kind in ((logit[b], 0, 2), (px[b], 0, 1), (val[b], 2 * DCH, 0)):
                        sp.dma_start(sub(tile, 0, 128, off, [[1, DCH]]),
                                     dram("om", kind * KK * HW + n * DCH, [[OM_IMG, B], [DENSE, 128 // B], [1, DCH]])
                                     ).then_inc(loaded[b], 16)

                sp.dma_start(column[:, :], dram("column", 0, [[W, 128], [1, W]])).then_inc(grid_loaded, 16)
                sp.dma_start(tap_shift[:, :], dram("tap_shift", 0, [[D_RING * D_IT, 128], [1, D_RING * D_IT]])
                             ).then_inc(grid_loaded, 16)

                def body(it, last):
                    for b in range(D_RING):
                        lead(it, b)
                peel(sp, D_IT, body)
                sp.wait_ge(ranged, D_RING * D_IT)
                for tile, name in ((row_max, "row_max"), (row_min, "row_min")):
                    sp.dma_start(dram(name, 0, [[DENSE // W, 128], [1, DENSE // W]]), tile[:, :]).then_inc(ranges_stored, 16)
                for b in range(D_RING):
                    sp.wait_ge(stored[b], 16 * D_IT)
                sp.wait_ge(ranges_stored, 32)

            @block.scalar
            def _(act):
                def lead(it, b):
                    n = D_RING * it + b
                    act.wait_ge(loaded[b], 48 * (it + 1))
                    nc.scalar.activation(sub(val[b], 0, 128, DCH, [[1, DCH]]), logit[b][:, :], ACT.Sigmoid).then_inc(masked, 1)

                def store(it, b):
                    n = D_RING * it + b
                    act.wait_ge(low, n + 1)
                    act.dma_start(dram("parts", n * DCH, [[DENSE, 128], [PLANE, KINDS], [1, DCH]]),
                                  sub(parts[b], 0, 128, 0, [[DCH, KINDS], [1, DCH]]).bitcast(fp32)).then_inc(stored[b], 16)

                def tail(it, b):
                    n = D_RING * it + b
                    act.wait_ge(scaled, n + 1)
                    wait(act, stored[b], 16 * it)
                    nc.scalar.copy(part(b, 0), three(val[b])).then_inc(high, 1)
                    if b or not (isinstance(it, int) and it == 0):
                        store(it if b else it - 1, (b - 1) % D_RING)
                overlapped(act, lead, tail)
                store(D_IT - 1, D_RING - 1)

            @block.gpsimd
            def _(pool):
                def body(it, last):
                    for b in range(D_RING):
                        n = D_RING * it + b
                        pool.wait_ge(high, n + 1)
                        pool.tensor_tensor(part(b, 1), three(val[b]), part(b, 0).bitcast(fp32), ALU.subtract).then_inc(low, 1)
                peel(pool, D_IT, body)

            @block.vector
            def _(dve):
                dve.wait_ge(grid_loaded, 32)

                def body(it, last):
                    for b in range(D_RING):
                        n = D_RING * it + b
                        dve.wait_ge(loaded[b], 48 * (it + 1))
                        nc.vector.scalar_tensor_tensor(sub(px[b], 0, 128, 0, [[W, RPC], [1, W]]),
                                                       sub(px[b], 0, 128, 0, [[W, RPC], [1, W]]),
                                                       sub(tap_shift, 0, 128, n, [[1, 1]]),
                                                       sub(column, 0, 128, 0, [[0, RPC], [1, W]]),
                                                       ALU.add, ALU.add).then_inc(summed, 1)
                        oy = sub(val[b], 0, 128, 2 * DCH, [[W, RPC], [1, W]])
                        nc.vector.tensor_reduce(sub(row_max, 0, 128, n * RPC, [[1, RPC]]), oy, axis=AX.X, op=ALU.max)
                        nc.vector.tensor_reduce(sub(row_min, 0, 128, n * RPC, [[1, RPC]]), oy, axis=AX.X,
                                                op=ALU.min).then_inc(ranged, 1)
                        dve.wait_ge(summed, n + 1)
                        dve.wait_ge(masked, n + 1)
                        nc.vector.tensor_tensor(sub(val[b], 0, 128, 0, [[1, DCH]]), sub(val[b], 0, 128, DCH, [[1, DCH]]),
                                                px[b][:, :], ALU.mult).then_inc(scaled, 1)
                peel(dve, D_IT, body)

        with ExitStack() as st:
            sb, ps, sem = tools(st)
            ROW = TAPS_PX
            sel32 = sb("sel32", 4 * 128)
            sel = sb("sel", 4 * 128, f32r)
            sel_plus, sel_minus, sel_y = sel[:, 0:128], sel[:, 128:256], [sel[:, 256:384], sel[:, 384:512]]
            win_bias = sb("win_bias", N_WIN)
            conv_w = sb("conv_w", KK * 32)
            conv_b = sb("conv_b", 1)
            stage = [sb(f"stage{b}", STAGE_ROWS * C) for b in range(2)]
            stage_hi = [sb(f"stage_hi{b}", STAGE_ROWS * C, f32r) for b in range(2)]
            stage_lo = [sb(f"stage_lo{b}", STAGE_ROWS * C, f32r) for b in range(2)]
            rows = [sb(f"rows{b}", KK * UPX, f32r) for b in range(2)]
            plus = [sb(f"plus{b}", ROW) for b in range(2)]
            tent_x = [sb(f"tent_x{q}", ROW) for q in range(UNIT_ROWS)]
            tent_a = [sb(f"tent_a{q}", ROW, f32r) for q in range(UNIT_ROWS)]
            tent_rest = [sb(f"tent_rest{b}", ROW, parts=64) for b in range(2)]
            dist_y = [sb(f"dist_y{b}", 2 * ROW) for b in range(2)]
            res = sb("res", UPX)
            ps_p, ps_m = ps("ps_p"), ps("ps_m")
            ps_y, ps_v = ps("ps_y", 2), ps("ps_v", 2)
            ps_r = ps("ps_r")
            consts_loaded, cleared, cast = sem("dcn_consts_loaded"), sem("cleared"), sem("cast")
            stage_loaded = [sem(f"stage_loaded{b}") for b in range(2)]
            rows_loaded = [sem(f"rows_loaded{b}") for b in range(2)]
            x_spread, y_spread, plus_ready, tent_ready, dist_ready, dist_capped, sampled, weighted, reduced, res_ready = [
                sem(n) for n in ("x_spread", "y_spread", "plus_ready", "tent_ready", "dist_ready", "dist_capped",
                                 "sampled", "weighted", "reduced", "res_ready")]
            res_stored = sem("res_stored")
            tent_rounded, rest_ready, rest_moved = sem("tent_rounded"), sem("rest_ready"), sem("rest_moved")
            LOADS_PER_UNIT = 5
            LOADS = ((sel32, "sel"), (win_bias, "win_bias"), (conv_w, "conv_w"), (conv_b, "conv_b"))
            IN_BODY = 4
            IT = N_UNITS // IN_BODY
            block = st.enter_context(nc.Block())

            def place(eng, it, b):
                n = IN_BODY * it + b
                return (n // UNITS, n % UNITS) if isinstance(it, int) else (eng.snap(n // UNITS), eng.snap(n % UNITS))

            def load_unit(eng, b, pair, u):
                row = (TOP - 1 + u * UNIT_ROWS + WIN * BASE_WIN - 60) * C
                eng.dma_start(sub(stage[b % 2], 64, W, 0, [[1, STAGE_ROWS * C]]),
                              dram("xt", (pair * 2 + 1) * W * XT_ROW + row,
                                   [[XT_ROW, W], [1, STAGE_ROWS * C]])).then_inc(stage_loaded[b % 2], 16)
                for tile, name in ((stage_hi[b % 2], "xt_hi"), (stage_lo[b % 2], "xt_lo")):
                    for half in range(2):
                        eng.dma_start(sub(tile, 64 * half, W, 0, [[1, STAGE_ROWS * C]]).bitcast(fp32),
                                      dram(name, pair * W * XT_ROW + row,
                                           [[XT_ROW, W], [1, STAGE_ROWS * C]])).then_inc(stage_loaded[b % 2], 16)

            def load_rows(eng, b, pair, u):
                for i in range(2):
                    eng.dma_start(sub(rows[b % 2], KINDS * i, KINDS, 0, [[UPX, KK], [1, UPX]]).bitcast(fp32),
                                  dram("parts", (pair * 2 + i) * KK * HW + u * UPX,
                                       [[PLANE, KINDS], [HW, KK], [1, UPX]])).then_inc(rows_loaded[b % 2], 16)

            def samples(b, i, q, dims, first=0):
                return sub(X, 0, 128, b * UNIT_SAMPLES + (i * UNIT_ROWS + q) * ROW + first, dims)

            def taps(b, q):
                return sub(rows[b % 2], 0, 128, q * W, [[UPX, KK], [1, W]])

            @block.sync
            def _(sp):
                sp.wait_ge(cleared, 8)

                def store(it, half):
                    pair, u = place(sp, it, 2 * half)
                    sp.wait_ge(res_ready, 2 * it + half + 1)
                    for i in range(2):
                        sp.dma_start(dram("conv", (pair * 2 + i) * 64 * CONV_ROW + u * (UPX // 2), [[CONV_ROW, 64], [1, UPX]]),
                                     res[64 * i:64 * i + 64, :]).then_inc(res_stored, 16)

                def body(it, last):
                    for b in range(IN_BODY):
                        n = IN_BODY * it + b
                        pair, u = place(sp, it, b)
                        wait(sp, y_spread, UNIT_ROWS * (n - 1))
                        load_rows(sp, b, pair, u)
                        wait(sp, sampled, 2 * UNIT_ROWS * (n - 1))
                        load_unit(sp, b, pair, u)
                        if b % 2 == 1 and not (isinstance(it, int) and it == 0):
                            store(it - 1, b // 2)
                peel(sp, IT, body)
                for half in range(2):
                    store(IT - 1, half)
                sp.wait_ge(res_stored, 32 * 2 * IT)

            def stream(eng, ops, later=None):
                def run(it, b, q, last):
                    for ahead, op in ops:
                        row = b * UNIT_ROWS + q + ahead
                        more, row = row // (IN_BODY * UNIT_ROWS), row % (IN_BODY * UNIT_ROWS)
                        if not (last and more) and not (it is None and not more):
                            op(0 if it is None else it + more if more else it, row // UNIT_ROWS, row % UNIT_ROWS)

                first = max(ahead for ahead, op in ops)
                for q in range(UNIT_ROWS - first, UNIT_ROWS):
                    run(None, IN_BODY - 1, q, False)

                def body(it, last):
                    for b in range(IN_BODY):
                        for q in range(UNIT_ROWS):
                            run(it, b, q, last)
                            t = b % 2 * UNIT_ROWS + q
                            if later and b >= 2:
                                later(it, 0, t)
                            elif later and not (isinstance(it, int) and it == 0):
                                later(it - 1, 1, t)
                peel(eng, IT, body)
                if later:
                    for t in range(2 * UNIT_ROWS):
                        later(IT - 1, 1, t)

            @block.gpsimd
            def _(pool):
                for b in range(2):
                    for tile in (stage[b % 2][:, :], stage_hi[b % 2][:, :].bitcast(fp32), stage_lo[b % 2][:, :].bitcast(fp32),
                                 rows[b % 2][:, :].bitcast(fp32)):
                        pool.memset(tile, 0.0).then_inc(cleared, 1)

                def rest(it, b, q):
                    r = (IN_BODY * it + b) * UNIT_ROWS + q
                    pool.wait_ge(tent_rounded, r + 1)
                    wait(pool, rest_moved, r - 1)
                    pool.tensor_tensor(tent_rest[q % 2][:, :], tent_x[q][0:64, :], tent_a[q][0:64, :].bitcast(fp32),
                                       ALU.subtract).then_inc(rest_ready, 1)
                stream(pool, [(2, rest)])

            @block.tensor
            def _(pe):
                pe.wait_ge(cast, 1)
                pe.wait_ge(consts_loaded, 16 * len(LOADS))

                def spread_x(it, b, q):
                    r = (IN_BODY * it + b) * UNIT_ROWS + q
                    if q == 0:
                        pe.wait_ge(rows_loaded[b % 2], 32 * (2 * it + b // 2 + 1))
                    wait(pe, plus_ready, r)
                    nc.tensor.matmul(ps_p[:, 0:ROW], sel_plus, taps(b, q), start=True, stop=True)
                    wait(pe, tent_ready, r)
                    nc.tensor.matmul(ps_m[:, 0:ROW], sel_minus, taps(b, q), start=True, stop=True).then_inc(x_spread, 1)

                def spread_y(it, b, q):
                    r = (IN_BODY * it + b) * UNIT_ROWS + q
                    wait(pe, dist_ready, r)
                    for i in range(2):
                        m = nc.tensor.matmul(ps_y[:, i * 512:i * 512 + ROW], sel_y[i], taps(b, q), start=True, stop=True)
                    m.then_inc(y_spread, 1)

                def columns(q, i, passes):
                    for ky in range(3):
                        for n, (image, tent) in enumerate(passes):
                            m = nc.tensor.matmul(ps_v[:, i * 512 + ky * 3 * W:i * 512 + (ky + 1) * 3 * W],
                                                 image[:, (q + ky) * C:(q + ky + WIN) * C],
                                                 tent[:, ky * 3 * W:(ky + 1) * 3 * W],
                                                 start=(n == 0), stop=(n == len(passes) - 1))
                    m.then_inc(sampled, 1)

                def columns_b(it, b, q):
                    r = (IN_BODY * it + b) * UNIT_ROWS + q
                    if q == 0:
                        pe.wait_ge(stage_loaded[b % 2], 16 * LOADS_PER_UNIT * (2 * it + b // 2 + 1))
                    pe.wait_ge(tent_ready, r + 1)
                    wait(pe, weighted, 2 * r - 1)
                    columns(q, 1, [(stage[b % 2], tent_x[q])])

                def columns_a(it, b, q):
                    r = (IN_BODY * it + b) * UNIT_ROWS + q
                    pe.wait_ge(rest_moved, r + 1)
                    wait(pe, weighted, 2 * r)
                    columns(q, 0, [(stage_hi[b % 2], tent_a[q]), (stage_lo[b % 2], tent_a[q])])

                def taps_and_channels(it, half, t):
                    if t == 0:
                        pe.wait_ge(weighted, 4 * UNIT_ROWS * (2 * it + half + 1))
                        wait(pe, res_ready, 2 * it + half)
                    last = 2 * UNIT_ROWS - 1
                    for k in range(KK * t // last, KK * (t + 1) // last) if t < last else ():
                        for j in range(4):
                            i, unit = j // 2, j % 2
                            m = nc.tensor.matmul(ps_r[32 * j:32 * j + 32, 0:UPX], conv_w[:, k * 32:(k + 1) * 32],
                                                 samples(2 * half + unit, i, 0, [[ROW, UNIT_ROWS], [1, W]], k * W),
                                                 start=(k == 0), stop=(k == KK - 1))
                        if k == KK - 1:
                            m.then_inc(reduced, 1)
                stream(pe, [(1, spread_y), (0, columns_b), (3, spread_x), (0, columns_a)], taps_and_channels)

            @block.scalar
            def _(act):
                for tile, name in LOADS:
                    n = tile[:].shape[1]
                    act.dma_start(tile[:, :], dram(name, 0, [[n, 128], [1, n]])).then_inc(consts_loaded, 16)
                act.wait_ge(consts_loaded, 16 * len(LOADS))
                nc.scalar.copy(sel[:, :], sel32[:, :]).then_inc(cast, 1)

                def relu(it, b, q):
                    r = (IN_BODY * it + b) * UNIT_ROWS + q
                    act.wait_ge(x_spread, r + 1)
                    wait(act, tent_ready, r - 1)
                    nc.scalar.activation(plus[q % 2][:, :], ps_p[:, 0:ROW], ACT.Relu).then_inc(plus_ready, 1)

                def distance(it, b, q):
                    r = (IN_BODY * it + b) * UNIT_ROWS + q
                    act.wait_ge(y_spread, r + 1)
                    wait(act, weighted, 2 * (r - 1))
                    nc.scalar.activation(sub(dist_y[q % 2], 0, 128, 0, [[ROW, 2], [1, ROW]]),
                                         sub(ps_y, 0, 128, 0, [[512, 2], [1, ROW]]), ACT.Abs,
                                         bias=win_bias[:, BASE_WIN:BASE_WIN + 1]).then_inc(dist_ready, 1)

                def rounding(it, b, q):
                    r = (IN_BODY * it + b) * UNIT_ROWS + q
                    act.wait_ge(tent_ready, r + 1)
                    wait(act, sampled, 2 * (r - 3))
                    nc.scalar.copy(tent_a[q][0:64, :], tent_x[q][0:64, :]).then_inc(tent_rounded, 1)

                def result(it, half, t):
                    if t == 2 * UNIT_ROWS - 1:
                        act.wait_ge(reduced, 2 * it + half + 1)
                        wait(act, res_stored, 32 * (2 * it + half))
                        nc.scalar.activation(res[:, :], ps_r[:, 0:UPX], ACT.Identity, scale=-1.0,
                                             bias=conv_b[:, 0:1]).then_inc(res_ready, 1)
                stream(act, [(1, distance), (2, rounding), (3, relu)], result)

            @block.vector
            def _(dve):
                def tent(it, b, q):
                    r = (IN_BODY * it + b) * UNIT_ROWS + q
                    dve.wait_ge(x_spread, r + 1)
                    dve.wait_ge(plus_ready, r + 1)
                    wait(dve, sampled, 2 * (r - 3))
                    nc.vector.scalar_tensor_tensor(tent_x[q][:, :], ps_m[:, 0:ROW], 0.0, plus[q % 2][:, :],
                                                   ALU.max, ALU.min).then_inc(tent_ready, 1)

                def move(it, b, q):
                    r = (IN_BODY * it + b) * UNIT_ROWS + q
                    dve.wait_ge(rest_ready, r + 1)
                    wait(dve, sampled, 2 * (r - 3))
                    nc.vector.tensor_copy(tent_a[q][64:128, :], tent_rest[q % 2][:, :]).then_inc(rest_moved, 1)

                def cap(it, b, q):
                    r = (IN_BODY * it + b) * UNIT_ROWS + q
                    dve.wait_ge(dist_ready, r + 1)
                    nc.vector.tensor_scalar(dist_y[q % 2][:, :], dist_y[q % 2][:, :], 1.0, 1.0,
                                            ALU.min, ALU.subtract).then_inc(dist_capped, 1)

                def weight(it, b, q):
                    r = (IN_BODY * it + b) * UNIT_ROWS + q
                    if q == 0 and b % 2 == 0:
                        wait(dve, reduced, 2 * it + b // 2 - 1)
                    dve.wait_ge(dist_capped, r + 1)
                    for n, i in enumerate((1, 0)):
                        dve.wait_ge(sampled, 2 * r + 1 + n)
                        nc.vector.tensor_tensor(
                            samples(b, i, q, [[1, ROW]]),
                            sub(dist_y[q % 2], 0, 128, i * ROW, [[1, ROW]]),
                            sub(ps_v, 0, 128, i * 512, [[1, ROW]]), ALU.mult).then_inc(weighted, 1)
                stream(dve, [(2, tent), (0, cap), (1, move), (0, weight)])

        with ExitStack() as st:
            sb, ps, sem = tools(st)
            ROW = TAPS_PX
            TABLE = N_UNITS * N_WIN
            PU = UNITS * N_WIN
            FLAGS = UNITS + 2
            ranges = sb("ranges", 2 * 2 * KK * H, parts=PAIRS)
            unit_range = sb("unit_range", 2 * UNITS, parts=PAIRS)
            bounds = sb("bounds", 2 * N_WIN, parts=PAIRS)
            need = sb("need", 2 * PU, parts=PAIRS)
            flags = sb("flags", FLAGS + 2, parts=PAIRS)
            needed, ordinal = (X[0:1, k * TABLE:(k + 1) * TABLE] for k in range(2))
            all_flags = sb("all_flags", PAIRS * FLAGS, parts=1)
            turn_of = sb("turn_of", TABLE, i32, parts=1)
            any_unit = sb("any_unit", N_UNITS, i32, parts=1)
            any_pair = sb("any_pair", PAIRS, i32, parts=1)
            far_any = sb("far_any", 1, parts=1)
            any_far = sb("any_far", 1, i32, parts=1)
            xsel32 = sb("xsel32", 4 * 128)
            xsel = sb("xsel", 4 * 128, f32r)
            xwin_bias = sb("xwin_bias", N_WIN)
            xconv_w = sb("xconv_w", KK * 32)
            xstage = [sb(f"xstage{i}", STAGE_ROWS * C) for i in range(2)]
            xrows = sb("xrows", KK * UPX, f32r)
            xplus, xtent = sb("xplus", ROW), sb("xtent", ROW)
            xdist = sb("xdist", 2 * ROW)
            xG = sb("xG", 2 * UNIT_ROWS * ROW)
            before, added_to = sb("before", UPX // 2), sb("added_to", UPX // 2)
            xps_p, xps_m, xps_r = ps("xps_p"), ps("xps_m"), ps("xps_r")
            xps_y, xps_v = ps("xps_y", 2), ps("xps_v", 2)
            names = ("x_consts", "x_cleared", "x_cast", "x_ranges", "x_step", "x_need_stored", "x_need_loaded", "x_tables",
                     "x_pads", "x_loaded", "x_before", "x_reduced", "x_added", "x_stored", "x_turn")
            S = {n: sem(n) for n in names}
            Q = {n: [sem(f"{n}_row{q}") for q in range(UNIT_ROWS)] for n in (
                "x_spreads", "x_plus_ready", "x_tent_ready", "x_dist_ready", "x_capped", "x_sampled", "x_weighted")}
            block = st.enter_context(nc.Block())

            def windows(eng, work):
                eng.wait_ge(S["x_tables"], 4)
                with eng.Fori(0, PAIRS) as pair:
                    some = eng.value_load(any_pair[0:1, bass.ds(pair, 1)], min_val=0, max_val=1)
                    with eng.If(some > 0):
                        with eng.Fori(0, UNITS) as u:
                            some_u = eng.value_load(any_unit[0:1, bass.ds(pair * UNITS + u, 1)], min_val=0, max_val=1)
                            with eng.If(some_u > 0):
                                with eng.Fori(0, N_WIN) as win:
                                    turn = eng.value_load(turn_of[0:1, bass.ds((pair * UNITS + u) * N_WIN + win, 1)],
                                                          min_val=0, max_val=TABLE)
                                    with eng.If(turn > 0):
                                        work(turn, pair, u, win)
                                    eng.nop()
                            eng.nop()
                    eng.nop()

            def conv_quarters(tile, pair, u):
                for j in range(4):
                    i, h = j // 2, j % 2
                    yield (dram("conv", (pair * 2 + i) * 64 * CONV_ROW + (u % 2) * 32 * CONV_ROW + (u // 2) * UPX + h * (UPX // 2),
                                [[CONV_ROW, O], [1, UPX // 2]]),
                           sub(tile, 32 * j, O, 0, [[1, UPX // 2]]))

            @block.sync
            def _(sp):
                for k, name in enumerate(("row_max", "row_min")):
                    n = 2 * KK * H
                    sp.dma_start(sub(ranges, 0, PAIRS, k * n, [[1, n]]), dram(name, 0, [[n, PAIRS], [1, n]])).then_inc(S["x_ranges"], 16)
                sp.dma_start(bounds[:, :], dram("bounds", 0, [[2 * N_WIN, PAIRS], [1, 2 * N_WIN]])).then_inc(S["x_ranges"], 16)
                sp.wait_ge(S["x_step"], 10)
                sp.dma_start(dram("needed", 0, [[PU, PAIRS], [1, PU]]), need[:, PU:]).then_inc(S["x_need_stored"], 16)
                sp.dma_start(dram("needed", TABLE, [[FLAGS, PAIRS], [1, FLAGS]]), flags[:, 0:FLAGS]).then_inc(S["x_need_stored"], 16)
                sp.wait_ge(S["x_need_stored"], 32)
                sp.dma_start(all_flags[:, :], dram("needed", TABLE, [[PAIRS * FLAGS, 1], [1, PAIRS * FLAGS]])
                             ).then_inc(S["x_need_loaded"], 16)
                sp.dma_start(needed, dram("needed", 0, [[TABLE, 1], [1, TABLE]])).then_inc(S["x_need_loaded"], 16)
                sp.wait_ge(S["x_cleared"], 5)
                sp.wait_ge(S["x_tables"], 4)
                far = sp.value_load(any_far[0:1, 0:1], min_val=0, max_val=1)
                with sp.If(far > 0):
                    for a, z in ((0, TOP - NEAR), (TOP + H + NEAR, XT_ROWS)):
                        sp.dma_start(dram("xt", a * C, [[XT_ROW, W], [W * XT_ROW, B], [1, (z - a) * C]]),
                                     sub(zeros, 0, W, 0, [[0, B], [1, (z - a) * C]])).then_inc(S["x_pads"], 16)
                    sp.wait_ge(S["x_pads"], 32)
                sp.nop()

                def work(turn, pair, u, win):
                    for i in range(2):
                        sp.dma_start(sub(xstage[i], 64 * i, W, 0, [[1, STAGE_ROWS * C]]),
                                     dram("xt", (pair * 2 + i) * W * XT_ROW + (TOP - 1 - 60 + u * UNIT_ROWS + win * WIN) * C,
                                          [[XT_ROW, W], [1, STAGE_ROWS * C]])).then_inc(S["x_loaded"], 16)
                        sp.dma_start(sub(xrows, KINDS * i, KINDS, 0, [[UPX, KK], [1, UPX]]).bitcast(fp32),
                                     dram("parts", (pair * 2 + i) * KK * HW + u * UPX,
                                          [[PLANE, KINDS], [HW, KK], [1, UPX]])).then_inc(S["x_loaded"], 16)
                    for there, here in conv_quarters(before, pair, u):
                        sp.dma_start(here, there).then_inc(S["x_before"], 16)
                    sp.wait_ge(S["x_added"], turn)
                    sp.sem_inc(S["x_turn"], 1)
                    for there, here in conv_quarters(added_to, pair, u):
                        sp.dma_start(there, here).then_inc(S["x_stored"], 16)
                    sp.wait_ge(S["x_stored"], 64 * turn)
                    sp.sem_inc(S["x_turn"], 1)
                windows(sp, work)

            @block.gpsimd
            def _(pool):
                for tile in (xstage[0][:, :], xstage[1][:, :], xrows[:, :].bitcast(fp32), before[:, :], added_to[:, :]):
                    pool.memset(tile, 0.0).then_inc(S["x_cleared"], 1)

            @block.vector
            def _(dve):
                done = [0]

                def step(ins):
                    done[0] += 1
                    ins.then_inc(S["x_step"], 1)
                    dve.wait_ge(S["x_step"], done[0])

                dve.wait_ge(S["x_ranges"], 48)
                n = 2 * KK * H
                step(nc.vector.tensor_reduce(unit_range[:, 0:UNITS],
                                             sub(ranges, 0, PAIRS, 0, [[UNIT_ROWS, UNITS], [H, 2 * KK], [1, UNIT_ROWS]]),
                                             axis=AX.XY, op=ALU.max))
                step(nc.vector.tensor_reduce(unit_range[:, UNITS:],
                                             sub(ranges, 0, PAIRS, n, [[UNIT_ROWS, UNITS], [H, 2 * KK], [1, UNIT_ROWS]]),
                                             axis=AX.XY, op=ALU.min))
                for side, op in ((0, ALU.is_gt), (1, ALU.is_lt)):
                    step(nc.vector.tensor_tensor(sub(need, 0, PAIRS, side * PU, [[N_WIN, UNITS], [1, N_WIN]]),
                                                 sub(unit_range, 0, PAIRS, side * UNITS, [[1, UNITS], [0, N_WIN]]),
                                                 sub(bounds, 0, PAIRS, side * N_WIN, [[0, UNITS], [1, N_WIN]]), op))
                step(nc.vector.tensor_tensor(need[:, PU:], need[:, 0:PU], need[:, PU:], ALU.max))
                step(nc.vector.tensor_reduce(flags[:, 0:UNITS], sub(need, 0, PAIRS, PU, [[N_WIN, UNITS], [1, N_WIN]]),
                                             axis=AX.X, op=ALU.max))
                step(nc.vector.tensor_reduce(flags[:, UNITS:UNITS + 1], flags[:, 0:UNITS], axis=AX.X, op=ALU.max))
                for k, first in enumerate((0, BASE_WIN + 2)):
                    step(nc.vector.tensor_reduce(flags[:, FLAGS + k:FLAGS + k + 1],
                                                 sub(need, 0, PAIRS, PU + first, [[N_WIN, UNITS], [1, BASE_WIN - 1]]),
                                                 axis=AX.XY, op=ALU.max))
                step(nc.vector.tensor_tensor(flags[:, UNITS + 1:FLAGS], flags[:, FLAGS:FLAGS + 1],
                                             flags[:, FLAGS + 1:FLAGS + 2], ALU.max))
                dve.wait_ge(S["x_need_loaded"], 32)
                nc.vector.tensor_copy(any_unit[:, :].rearrange("p (a u) -> p a u", u=UNITS),
                                      sub(all_flags, 0, 1, 0, [[FLAGS, PAIRS], [1, UNITS]])).then_inc(S["x_tables"], 1)
                nc.vector.tensor_copy(any_pair[:, :], sub(all_flags, 0, 1, UNITS, [[FLAGS, PAIRS]])).then_inc(S["x_tables"], 1)
                step(nc.vector.tensor_reduce(far_any[:, :], sub(all_flags, 0, 1, UNITS + 1, [[FLAGS, PAIRS]]),
                                             axis=AX.X, op=ALU.max))
                nc.vector.tensor_copy(any_far[:, :], far_any[:, :]).then_inc(S["x_tables"], 1)
                step(nc.vector.tensor_tensor_scan(ordinal, needed, needed, 0.0, ALU.add, ALU.bypass))
                nc.vector.tensor_tensor(turn_of[:, :], ordinal, needed, ALU.mult).then_inc(S["x_tables"], 1)

                def work(turn, pair, u, win):
                    for q in range(UNIT_ROWS):
                        dve.wait_ge(Q["x_plus_ready"][q], turn)
                        nc.vector.scalar_tensor_tensor(xtent[:, :], xps_m[:, 0:ROW], 0.0, xplus[:, :],
                                                       ALU.max, ALU.min).then_inc(Q["x_tent_ready"][q], 1)
                        dve.wait_ge(Q["x_dist_ready"][q], turn)
                        nc.vector.tensor_scalar(xdist[:, :], xdist[:, :], 1.0, 1.0, ALU.min, ALU.subtract).then_inc(Q["x_capped"][q], 1)
                        dve.wait_ge(Q["x_capped"][q], turn)
                        dve.wait_ge(Q["x_sampled"][q], turn)
                        nc.vector.tensor_tensor(sub(xG, 0, 128, q * ROW, [[UNIT_ROWS * ROW, 2], [1, ROW]]),
                                                sub(xdist, 0, 128, 0, [[ROW, 2], [1, ROW]]),
                                                sub(xps_v, 0, 128, 0, [[512, 2], [1, ROW]]), ALU.mult).then_inc(Q["x_weighted"][q], 1)
                    dve.wait_ge(S["x_reduced"], turn)
                    dve.wait_ge(S["x_before"], 64 * turn)
                    nc.vector.scalar_tensor_tensor(added_to[:, :], xps_r[:, 0:UPX // 2], -1.0, before[:, :],
                                                   ALU.mult, ALU.add).then_inc(S["x_added"], 1)
                windows(dve, work)

            @block.scalar
            def _(act):
                for tile, name in ((xsel32, "sel"), (xwin_bias, "win_bias"), (xconv_w, "conv_w")):
                    n = tile[:].shape[1]
                    act.dma_start(tile[:, :], dram(name, 0, [[n, 128], [1, n]])).then_inc(S["x_consts"], 16)
                act.wait_ge(S["x_consts"], 48)
                nc.scalar.copy(xsel[:, :], xsel32[:, :]).then_inc(S["x_cast"], 1)

                def work(turn, pair, u, win):
                    for q in range(UNIT_ROWS):
                        act.wait_ge(Q["x_spreads"][q], turn)
                        nc.scalar.activation(xplus[:, :], xps_p[:, 0:ROW], ACT.Relu).then_inc(Q["x_plus_ready"][q], 1)
                        nc.scalar.activation(sub(xdist, 0, 128, 0, [[ROW, 2], [1, ROW]]),
                                             sub(xps_y, 0, 128, 0, [[512, 2], [1, ROW]]), ACT.Abs,
                                             bias=sub(xwin_bias, 0, 128, win, [[1, 1]])).then_inc(Q["x_dist_ready"][q], 1)
                windows(act, work)

            @block.tensor
            def _(pe):
                pe.wait_ge(S["x_cast"], 1)
                pe.wait_ge(S["x_cleared"], 5)
                taps = lambda q: sub(xrows, 0, 128, q * W, [[UPX, KK], [1, W]])

                def work(turn, pair, u, win):
                    pe.wait_ge(S["x_loaded"], 64 * turn)
                    for q in range(UNIT_ROWS):
                        if q:
                            pe.wait_ge(Q["x_weighted"][q - 1], turn)
                        nc.tensor.matmul(xps_p[:, 0:ROW], xsel[:, 0:128], taps(q), start=True, stop=True)
                        nc.tensor.matmul(xps_m[:, 0:ROW], xsel[:, 128:256], taps(q), start=True, stop=True)
                        for i in range(2):
                            m = nc.tensor.matmul(xps_y[:, i * 512:i * 512 + ROW], xsel[:, (2 + i) * 128:(3 + i) * 128],
                                                 taps(q), start=True, stop=True)
                        m.then_inc(Q["x_spreads"][q], 1)
                        pe.wait_ge(Q["x_tent_ready"][q], turn)
                        for i in range(2):
                            for ky in range(3):
                                m = nc.tensor.matmul(xps_v[:, i * 512 + ky * 3 * W:i * 512 + (ky + 1) * 3 * W],
                                                     xstage[i][:, (q + ky) * C:(q + ky + WIN) * C],
                                                     xtent[:, ky * 3 * W:(ky + 1) * 3 * W], start=True, stop=True)
                        m.then_inc(Q["x_sampled"][q], 1)
                    pe.wait_ge(Q["x_weighted"][UNIT_ROWS - 1], turn)
                    for k in range(KK):
                        for j in range(4):
                            i, h = j // 2, j % 2
                            m = nc.tensor.matmul(xps_r[32 * j:32 * j + 32, 0:UPX // 2], xconv_w[:, k * 32:(k + 1) * 32],
                                                 sub(xG, 0, 128, (i * UNIT_ROWS + 2 * h) * ROW + k * W, [[ROW, 2], [1, W]]),
                                                 start=(k == 0), stop=(k == KK - 1))
                    m.then_inc(S["x_reduced"], 1)
                windows(pe, work)


        with ExitStack() as st:
            sb, ps, sem = tools(st)
            CH = 448
            NCH = GROUPS * HW // CH
            PER = HW // CH
            stats = sb("stats", NCH * 6)
            mv = sb("mv", 2)
            t = sb("t", 12)
            y = [sb(f"y{i}", HW) for i in range(2)]
            ps_s = [ps("ps_mean"), ps("ps_var")]
            loaded = [sem(f"conv_loaded{g}") for g in range(GROUPS)]
            dve_step, pe_step, act_step, activated, added = [sem(n) for n in (
                "bn_dve_step", "bn_pe_step", "bn_act_step", "activated", "added")]
            out_stored = [sem(f"out_stored{i}") for i in range(2)]
            block = st.enter_context(nc.Block())

            @block.sync
            def _(sp):
                for g in range(GROUPS):
                    for h in range(2):
                        sp.dma_start(sub(X, 0, 128, g * HW + h * CONV_ROW, [[1, CONV_ROW]]),
                                     dram("conv", (g * GB * 64 + h * 32) * CONV_ROW,
                                          [[64 * CONV_ROW, GB], [CONV_ROW, O], [1, CONV_ROW]])).then_inc(loaded[g], 16)
                for g in range(GROUPS):
                    sp.wait_ge(added, g + 1)
                    sp.dma_start(dram("out", g * 128 * HW, [[HW, 128], [1, HW]]), y[g % 2][:, :]).then_inc(out_stored[g % 2], 16)
                for i in range(2):
                    sp.wait_ge(out_stored[i], 32)

            @block.tensor
            def _(pe):
                pe.wait_ge(dve_step, 2)
                nc.tensor.matmul(ps_s[0][:, 0:1], same_channel[:, :], mv[:, 0:1], start=True, stop=True).then_inc(pe_step, 1)
                pe.wait_ge(dve_step, 5)
                nc.tensor.matmul(ps_s[1][:, 0:1], same_channel[:, :], t[:, 2:3], start=True, stop=True).then_inc(pe_step, 1)

            @block.scalar
            def _(act):
                act.wait_ge(dve_step, 6)
                nc.scalar.activation(t[:, 4:5], t[:, 3:4], ACT.Sqrt).then_inc(act_step, 1)
                act.wait_ge(dve_step, 12)
                for g in range(GROUPS):
                    wait(act, out_stored[g % 2], 16 * (g // 2))
                    nc.scalar.activation(sub(y[g % 2], 0, 128, 0, [[UPX, 2], [2 * UPX, UNITS // 2], [1, UPX]]),
                                         sub(X, 0, 128, g * HW, [[CONV_ROW, 2], [UPX, UNITS // 2], [1, UPX]]),
                                         ACT.Relu, scale=t[:, 8:9],
                                         bias=t[:, 10:11]).then_inc(activated, 1)

            @block.vector
            def _(dve):
                done = [0]

                def step(ins):
                    done[0] += 1
                    ins.then_inc(dve_step, 1)
                    dve.wait_ge(dve_step, done[0])

                for c in range(NCH):
                    if c % PER == 0:
                        dve.wait_ge(loaded[c // PER], 32)
                    last = nc.vector.bn_stats(stats[:, c * 6:(c + 1) * 6], X[:, c * CH:(c + 1) * CH])
                step(last)
                step(nc.vector.bn_aggr(mv[:, :], stats[:, :]))
                dve.wait_ge(pe_step, 1)
                step(nc.vector.tensor_scalar(t[:, 0:1], ps_s[0][:, 0:1], 1.0 / GB, None, ALU.mult))
                step(nc.vector.tensor_tensor(t[:, 1:2], mv[:, 0:1], t[:, 0:1], ALU.subtract))
                step(nc.vector.scalar_tensor_tensor(t[:, 2:3], t[:, 1:2], t[:, 1:2], mv[:, 1:2],
                                                    ALU.mult, ALU.add))
                dve.wait_ge(pe_step, 2)
                step(nc.vector.tensor_scalar(t[:, 3:4], ps_s[1][:, 0:1], 1.0 / GB, 1e-5, ALU.mult, ALU.add))
                dve.wait_ge(act_step, 1)
                step(nc.vector.reciprocal(t[:, 5:6], t[:, 4:5]))
                step(nc.vector.scalar_tensor_tensor(t[:, 6:7], t[:, 5:6], t[:, 3:4], t[:, 4:5],
                                                    ALU.mult, ALU.add))
                step(nc.vector.reciprocal(t[:, 7:8], t[:, 6:7]))
                step(nc.vector.tensor_scalar(t[:, 8:9], t[:, 7:8], 2.0, vecs[:, 1:2], ALU.mult, ALU.mult))
                step(nc.vector.tensor_tensor(t[:, 9:10], t[:, 0:1], t[:, 8:9], ALU.mult))
                step(nc.vector.tensor_tensor(t[:, 10:11], vecs[:, 2:3], t[:, 9:10], ALU.subtract))
                for g in range(GROUPS):
                    dve.wait_ge(activated, g + 1)
                    nc.vector.tensor_tensor(y[g % 2][:, :].rearrange("p (r w) -> p r w", w=W),
                                            y[g % 2][:, :].rearrange("p (r w) -> p r w", w=W),
                                            sub(XH, 0, 128, g * PADHW + PADW + 1, [[PADW, H], [1, W]]),
                                            ALU.add).then_inc(added, 1)


def shape_constants():
    import numpy as np
    f = np.float32
    p = np.arange(128)
    img, ch = p // C, p % C
    eye = np.eye(128, dtype=f)
    out = {"ident": eye, "same_image": (img[:, None] == img[None]).astype(f),
           "same_channel": (ch[:, None] == ch[None]).astype(f), "eps_eye": (1e-5 * eye).astype(f),
           "shrink": (0.9 + 0.1 * eye).astype(f)}
    out["column"] = np.broadcast_to(np.arange(W, dtype=f), (128, W)).copy()
    first = (np.arange(128) % (128 // B) * DENSE)[:, None] + np.arange(DENSE // DCH)[None] * DCH
    out["tap_shift"] = (first // HW % 3 - 1).astype(f)
    sel = np.zeros((128, 4, 128), f)
    col = np.arange(W)
    for i in range(2):
        for k in range(2):
            sel[KINDS * i + k, 0, 64 * i + col] = 1.0
            sel[KINDS * i + 2 + k, 0, 64 * i + col] = 1.0 - col
            sel[KINDS * i + k, 1, 64 * i + col] = -1.0
            sel[KINDS * i + 2 + k, 1, 64 * i + col] = 1.0 + col
            sel[KINDS * i + 4 + k, 2 + i, :] = 1.0
    out["sel"] = sel.reshape(128, 512)
    out["win_bias"] = -(WIN * np.arange(N_WIN)[None, :] - 60 + (p // C)[:, None]).astype(f)
    big = 3e38
    j = np.arange(N_WIN)
    start = WIN * j - 60
    hi = np.where(j > BASE_WIN, start - 1, big).astype(f)
    lo = np.where(j < BASE_WIN, start + WIN, -big).astype(f)
    out["bounds"] = np.broadcast_to(np.stack([hi, lo])[None], (PAIRS, 2, N_WIN)).copy().reshape(PAIRS, 2 * N_WIN)
    return out


def kernel(x, L0_conv_beta, L1_conv_w_off, L1_conv_b_off, L1_conv_w, L1_conv_b, L1_conv_gamma, L1_conv_beta):
    import numpy as np
    import concourse.bacc as bacc
    from concourse.bass_utils import run_bass_kernel_spmd
    f = np.float32
    arrays = shape_constants()
    arrays["x"] = np.ascontiguousarray(x)
    w_off, w = np.asarray(L1_conv_w_off), np.asarray(L1_conv_w)
    tile = lambda v: np.tile(np.asarray(v), GB)
    vecs = np.zeros((128, 3), f)
    for n, v in enumerate((L0_conv_beta, L1_conv_gamma, L1_conv_beta)):
        vecs[:, n] = tile(v)
    arrays["vecs"] = vecs
    woff = np.zeros((4, 2, C, 3, 2, 32), f)
    boff = np.zeros((4, 32), f)
    for i in range(2):
        woff[:3, i, :, :, i, :3 * KK] = w_off.transpose(2, 1, 3, 0)
    boff[:, :3 * KK] = np.asarray(L1_conv_b_off)[None]
    arrays["woff"] = woff.reshape(128, 3 * 2 * 32)
    arrays["boff"] = boff.reshape(128, 1)
    conv_w = np.zeros((WIN, C, KK, 32), f)
    conv_w[:, :, :, :O] = w.reshape(O, C, KK).transpose(1, 2, 0)[None]
    arrays["conv_w"] = conv_w.reshape(128, KK * 32)
    conv_b = np.zeros((4, 32), f)
    conv_b[:, :O] = np.asarray(L1_conv_b)[None]
    arrays["conv_b"] = conv_b.reshape(128, 1)

    nc = bacc.Bacc("TRN2", target_bir_lowering=False, num_devices=1)
    fp32 = mybir.dt.float32
    dr = {n: nc.dram_tensor(f"in_{n}", a.shape, fp32, kind="ExternalInput").ap() for n, a in arrays.items()}
    for name, size, dt in (("xt", B * W * XT_ROW, fp32), ("xt_hi", PAIRS * W * XT_ROW, fp32),
                           ("xt_lo", PAIRS * W * XT_ROW, fp32), ("xh", B * C * PADHW, fp32), ("om", B * OM_IMG, fp32),
                           ("parts", KINDS * PLANE, fp32), ("row_max", PLANE // W, fp32), ("row_min", PLANE // W, fp32),
                           ("conv", B * 64 * CONV_ROW, fp32), ("needed", N_UNITS * N_WIN + PAIRS * (UNITS + 2), fp32)):
        dr[name] = nc.dram_tensor(f"scratch_{name}", (size,), dt, kind="Internal").ap()
    dr["out"] = nc.dram_tensor("out", (B, O, H, W), fp32, kind="ExternalOutput").ap()
    program(nc, dr)
    r = run_bass_kernel_spmd(nc, [{f"in_{n}": a for n, a in arrays.items()}], core_ids=[0])
    return r.results[0]["out"]
```
